# Optimizing a Trainium2 kernel written in Bass

```python
import numpy as np
import jax
import jax.numpy as jnp

def _softmax(x, axis=-1):
    return jax.nn.softmax(x, axis=axis)

def _gelu(x):
    return jax.nn.gelu(x, approximate=True)

def _silu(x):
    return jax.nn.silu(x)

def _sigmoid(x):
    return jax.nn.sigmoid(x)

def _layernorm(x, axis=-1, eps=1e-05):
    m = jnp.mean(x, axis=axis, keepdims=True)
    v = jnp.var(x, axis=axis, keepdims=True)
    return (x - m) / jnp.sqrt(v + eps)

def _scatter_add(tgt, idx, src, axis=0):
    return tgt.at[idx].add(src)

def _segment_sum(src, seg, n):
    return jax.ops.segment_sum(src, seg, n)
kernel_name = 'mk_seq_postln_d1_jaxref_r8_1321b4'

def setup_inputs(seed: int=0):
    np.random.seed(seed)
    _w = jnp.asarray

    def _L0_attn_setup():
        import jax, jax.numpy as jnp
        import numpy as np
        import math
        NUM_RFS = 128
        DIM = 128
        OUT_DIM = 128
        B, S = (4, 256)

        def _rfs(xw, ab, AB, gs):
            dot_products = jnp.einsum('...d,rd->...r', xw, ab[:, None] * gs)
            correction = (0.5 * jnp.sum(xw * xw, axis=-1))[..., None] * (ab * ab)
            return 1.0 / math.sqrt(NUM_RFS) * AB * jnp.exp(dot_products - correction)
        key = jax.random.key(seed)
        k1, k2, k3, k4 = jax.random.split(key, 4)
        x = jax.random.normal(k1, (B, S, DIM), dtype=jnp.float32) * 0.03
        input_weights = jax.random.normal(k2, (OUT_DIM, DIM), dtype=jnp.float32) * 0.03
        xis = jax.random.uniform(k3, (NUM_RFS,), dtype=jnp.float32) * 0.5
        proj_matrix = jax.random.normal(k4, (NUM_RFS, DIM), dtype=jnp.float32)
        return {'x': x, 'input_weights': input_weights, 'xis': xis, 'proj_matrix': proj_matrix}
    _L0_attn_in = _L0_attn_setup()

    def _L0_ffn_setup():
        import jax, jax.numpy as jnp
        import numpy as np
        from jax import lax
        N_HEADS = 16
        TOP_K = 2
        N_EXPERTS = 8

        def layer_norm(x, w, b, eps=1e-05):
            mu = jnp.mean(x, axis=-1, keepdims=True)
            var = jnp.mean(jnp.square(x - mu), axis=-1, keepdims=True)
            return (x - mu) * lax.rsqrt(var + eps) * w + b

        def attention(x, w_qkv, b_qkv, w_o, b_o):
            B, T, D = x.shape
            dh = D // N_HEADS
            qkv = x @ w_qkv + b_qkv
            q, k, v = jnp.split(qkv, 3, axis=-1)
            q = q.reshape(B, T, N_HEADS, dh)
            k = k.reshape(B, T, N_HEADS, dh)
            v = v.reshape(B, T, N_HEADS, dh)
            scores = jnp.einsum('bqhd,bkhd->bhqk', q, k) / jnp.sqrt(jnp.float32(dh)).astype(x.dtype)
            probs = jax.nn.softmax(scores, axis=-1)
            ctx = jnp.einsum('bhqk,bkhd->bqhd', probs, v).reshape(B, T, D)
            return ctx @ w_o + b_o

        def moe_ff(x, w_gate, w1, b1, w2, b2):
            B, T, D = x.shape
            t = x.reshape(B * T, D)
            probs = jax.nn.softmax(t @ w_gate, axis=-1)
            tw, ti = lax.top_k(probs, TOP_K)
            tw = tw / jnp.sum(tw, axis=-1, keepdims=True)
            out = jnp.zeros_like(t)
            for e in range(N_EXPERTS):
                we = jnp.sum(jnp.where(ti == e, tw, 0.0), axis=-1)
                h = jax.nn.gelu(t @ w1[e] + b1[e]) @ w2[e] + b2[e]
                out = out + we[:, None] * h
            return out.reshape(B, T, D)
        key = jax.random.key(seed)
        ks = jax.random.split(key, 8)
        B, T, D, H, E = (4, 64, 128, 512, 8)
        s = lambda d: 1.0 / np.sqrt(d)
        return {'x': jax.random.normal(ks[0], (B, T, D), jnp.float32), 'ln1_w': jnp.ones((D,), jnp.float32), 'ln1_b': jnp.zeros((D,), jnp.float32), 'ln2_w': jnp.ones((D,), jnp.float32), 'ln2_b': jnp.zeros((D,), jnp.float32), 'w_qkv': jax.random.normal(ks[1], (D, 3 * D), jnp.float32) * s(D), 'b_qkv': jnp.zeros((3 * D,), jnp.float32), 'w_o': jax.random.normal(ks[2], (D, D), jnp.float32) * s(D), 'b_o': jnp.zeros((D,), jnp.float32), 'w_gate': jax.random.normal(ks[3], (D, E), jnp.float32) * s(D), 'w1': jax.random.normal(ks[4], (E, D, H), jnp.float32) * s(D), 'b1': jnp.zeros((E, H), jnp.float32), 'w2': jax.random.normal(ks[5], (E, H, D), jnp.float32) * s(H), 'b2': jnp.zeros((E, D), jnp.float32)}
    _L0_ffn_in = _L0_ffn_setup()
    _d = {'L0_attn_x': _L0_attn_in['x'], 'L0_attn_input_weights': _L0_attn_in['input_weights'], 'L0_attn_xis': _L0_attn_in['xis'], 'L0_attn_proj_matrix': _L0_attn_in['proj_matrix'], 'L0_ffn_ln1_w': _L0_ffn_in['ln1_w'], 'L0_ffn_ln1_b': _L0_ffn_in['ln1_b'], 'L0_ffn_ln2_w': _L0_ffn_in['ln2_w'], 'L0_ffn_ln2_b': _L0_ffn_in['ln2_b'], 'L0_ffn_w_qkv': _L0_ffn_in['w_qkv'], 'L0_ffn_b_qkv': _L0_ffn_in['b_qkv'], 'L0_ffn_w_o': _L0_ffn_in['w_o'], 'L0_ffn_b_o': _L0_ffn_in['b_o'], 'L0_ffn_w_gate': _L0_ffn_in['w_gate'], 'L0_ffn_w1': _L0_ffn_in['w1'], 'L0_ffn_b1': _L0_ffn_in['b1'], 'L0_ffn_w2': _L0_ffn_in['w2'], 'L0_ffn_b2': _L0_ffn_in['b2']}
    _x0 = _d['L0_attn_x']
    _d['L0_attn_x'] = jax.random.normal(jax.random.fold_in(jax.random.key(seed), 1), (16, 256, 128), dtype=_x0.dtype)
    del _x0
    return _d

def reference(L0_attn_x, L0_attn_input_weights, L0_attn_xis, L0_attn_proj_matrix, L0_ffn_ln1_w, L0_ffn_ln1_b, L0_ffn_ln2_w, L0_ffn_ln2_b, L0_ffn_w_qkv, L0_ffn_b_qkv, L0_ffn_w_o, L0_ffn_b_o, L0_ffn_w_gate, L0_ffn_w1, L0_ffn_b1, L0_ffn_w2, L0_ffn_b2):

    def _L0_attn_ref(x, input_weights, xis, proj_matrix):
        import jax, jax.numpy as jnp
        import numpy as np
        import math
        NUM_RFS = 128
        DIM = 128
        OUT_DIM = 128
        B, S = (4, 256)

        def _rfs(xw, ab, AB, gs):
            dot_products = jnp.einsum('...d,rd->...r', xw, ab[:, None] * gs)
            correction = (0.5 * jnp.sum(xw * xw, axis=-1))[..., None] * (ab * ab)
            return 1.0 / math.sqrt(NUM_RFS) * AB * jnp.exp(dot_products - correction)
        ab = xis
        AB = jnp.exp(xis)
        weights = _rfs(input_weights, ab, AB, proj_matrix)
        feats = _rfs(x, ab, AB, proj_matrix)
        return jnp.einsum('bsr,or->bso', feats, weights)

    def _L0_ffn_ref(x, ln1_w, ln1_b, ln2_w, ln2_b, w_qkv, b_qkv, w_o, b_o, w_gate, w1, b1, w2, b2):
        import jax, jax.numpy as jnp
        import numpy as np
        from jax import lax
        N_HEADS = 16
        TOP_K = 2
        N_EXPERTS = 8

        def layer_norm(x, w, b, eps=1e-05):
            mu = jnp.mean(x, axis=-1, keepdims=True)
            var = jnp.mean(jnp.square(x - mu), axis=-1, keepdims=True)
            return (x - mu) * lax.rsqrt(var + eps) * w + b

        def attention(x, w_qkv, b_qkv, w_o, b_o):
            B, T, D = x.shape
            dh = D // N_HEADS
            qkv = x @ w_qkv + b_qkv
            q, k, v = jnp.split(qkv, 3, axis=-1)
            q = q.reshape(B, T, N_HEADS, dh)
            k = k.reshape(B, T, N_HEADS, dh)
            v = v.reshape(B, T, N_HEADS, dh)
            scores = jnp.einsum('bqhd,bkhd->bhqk', q, k) / jnp.sqrt(jnp.float32(dh)).astype(x.dtype)
            probs = jax.nn.softmax(scores, axis=-1)
            ctx = jnp.einsum('bhqk,bkhd->bqhd', probs, v).reshape(B, T, D)
            return ctx @ w_o + b_o

        def moe_ff(x, w_gate, w1, b1, w2, b2):
            B, T, D = x.shape
            t = x.reshape(B * T, D)
            probs = jax.nn.softmax(t @ w_gate, axis=-1)
            tw, ti = lax.top_k(probs, TOP_K)
            tw = tw / jnp.sum(tw, axis=-1, keepdims=True)
            out = jnp.zeros_like(t)
            for e in range(N_EXPERTS):
                we = jnp.sum(jnp.where(ti == e, tw, 0.0), axis=-1)
                h = jax.nn.gelu(t @ w1[e] + b1[e]) @ w2[e] + b2[e]
                out = out + we[:, None] * h
            return out.reshape(B, T, D)
        h = x + attention(layer_norm(x, ln1_w, ln1_b), w_qkv, b_qkv, w_o, b_o)
        return h + moe_ff(layer_norm(h, ln2_w, ln2_b), w_gate, w1, b1, w2, b2)
    x = L0_attn_x
    x = _layernorm(x + _L0_attn_ref(x, L0_attn_input_weights, L0_attn_xis, L0_attn_proj_matrix), axis=-1)
    x = _layernorm(x + _L0_ffn_ref(x, L0_ffn_ln1_w, L0_ffn_ln1_b, L0_ffn_ln2_w, L0_ffn_ln2_b, L0_ffn_w_qkv, L0_ffn_b_qkv, L0_ffn_w_o, L0_ffn_b_o, L0_ffn_w_gate, L0_ffn_w1, L0_ffn_b1, L0_ffn_w2, L0_ffn_b2), axis=-1)
    return x

_drawn_inputs = setup_inputs


def setup_inputs(seed=0):
    import zlib

    import numpy as np

    out = dict(_drawn_inputs(seed))
    spreads = {'L0_ffn_ln1_w': (1.0, 0.2),
     'L0_ffn_ln1_b': (0.0, 0.1),
     'L0_ffn_ln2_w': (1.0, 0.2),
     'L0_ffn_ln2_b': (0.0, 0.1),
     'L0_ffn_b_qkv': (0.0, 0.1),
     'L0_ffn_b_o': (0.0, 0.1),
     'L0_ffn_b1': (0.0, 0.335),
     'L0_ffn_b2': (0.0, 0.1)}
    factors = {}
    for name, (base, spread) in spreads.items():
        noise = np.random.default_rng([zlib.crc32(name.encode()), seed]).standard_normal(out[name].shape)
        drawn = base * np.exp(spread * noise) if base else spread * noise
        out[name] = jnp.asarray(drawn.astype(out[name].dtype))
    for name, factor in factors.items():
        out[name] = (out[name] * factor).astype(out[name].dtype)
    return out
```

```python
import math
from contextlib import ExitStack

import concourse.bass as bass
from concourse import mybir

F32 = mybir.dt.float32
F32R = mybir.dt.float32r
BF16 = mybir.dt.bfloat16
I32 = mybir.dt.int32
U32 = mybir.dt.uint32
ACT = mybir.ActivationFunctionType
ALU = mybir.AluOpType
AX = mybir.AxisListType

P = 128
BATCHES, SEQ, D = 16, 256, 128
TILES = BATCHES * SEQ // P
TB = SEQ // P
HEADS, DH = 16, 8
GROUPS, GH = 4, 4
VW = 32
PARTS = 3
PART_ORDER = ((0, 0, 1), (0, 1, 0))
PR = PARTS * DH
PACKS = 1 + GH
EXPERTS, TOPK, HID = 8, 2, 512
HC = HID // P
TOKENS = BATCHES * SEQ
REGION = TOKENS + P
ROW = D + 2
MOE_TILES = (TOKENS * TOPK + EXPERTS * (P - 1)) // P
SPARE = MOE_TILES - TOKENS * TOPK // P
EPS = 1e-5
SCALE = 1.0 / math.sqrt(DH)


def at_least(eng, sem, value):
    if isinstance(value, int) and value <= 0:
        return
    eng.wait_ge(sem, value)


def apart(eng, held, *waits):
    if all(isinstance(value, int) for _, value in waits):
        for sem, value in waits:
            at_least(eng, sem, value)
        return
    waits = [(sem, eng.to_reg(value)) for sem, value in waits]
    eng.wait_ge(held, 1)
    for sem, value in waits:
        eng.wait_ge(sem, value)


class Body:

    def __init__(self, i, odd, pair=None):
        self.i, self.odd, self.pair = i, odd, pair
        self.p = 1 if odd else 0
        fixed = isinstance(i, int)
        self.core = not fixed or i < BATCHES
        self.prev = not fixed or i >= 1
        self.project = not fixed or i + 1 < BATCHES
        self.front = not fixed or i + 2 < BATCHES

    def half(self, k):
        if isinstance(self.i, int):
            return (self.i + k) // 2
        return self.pair + (k + (3 if self.odd else 2)) // 2

    FULL = ["m3", "u2", "m0", "u3", "ctx", "m1", "proj", "u0", "ln2", "m2", "gate", "u1", "rank"]
    FIRST = ["m0", "m1", "u0", "m2", "u1"]
    LAST = ["m3", "u2", "u3", "ctx", "proj", "ln2", "gate", "rank"]

    def turn(self, name):
        if isinstance(self.i, int) and self.i == 0:
            return self.FIRST.index(name)
        uses = self.LAST if isinstance(self.i, int) and self.i == BATCHES else self.FULL
        return (self.i - 1) * len(self.FULL) + len(self.FIRST) + uses.index(name)


def run_bodies(eng, emit):
    emit(Body(0, False))
    emit(Body(1, True))
    with eng.Fori(0, BATCHES // 2 - 2) as pair:
        emit(Body(pair * 2 + 2, False, pair))
        emit(Body(pair * 2 + 3, True, pair))
    for i in range(BATCHES - 2, BATCHES + 1):
        emit(Body(i, i % 2 == 1))


def build(nc, x, x_t, w_in_t, xis, proj, ln1_w, ln1_b, ln2_w, ln2_b, w_qkv, b_qkv, w_o, b_o, w_gate,
          w1, b1, w2, b2, out):
    ctx = ExitStack()
    with ctx:
        def sb(name, shape, dt=F32):
            return ctx.enter_context(nc.sbuf_tensor(name, shape, dt))

        def sem(name):
            return ctx.enter_context(nc.semaphore(name))

        ident = sb("ident", [P, P])
        before = sb("before", [P, P], BF16)
        ones_bf = sb("ones_bf", [P, P], BF16)
        zeros = sb("zeros", [P, SEQ])
        eps_col = sb("eps_col", [P, 1])
        xis_col = sb("xis_col", [P, 1])
        neg_half_sq = sb("neg_half_sq", [P, 1])
        feat_bias = sb("feat_bias", [P, 1])
        proj_rd = sb("proj_rd", [P, D])
        scaled_rd = sb("scaled_rd", [P, 2, D])
        scaled_dr = sb("scaled_dr", [P, 2, D])
        w_in_dt = sb("w_in_dt", [P, D])
        w_in_sq = sb("w_in_sq", [P, D])
        w_feat = sb("w_feat", [P, D])
        wqkv_sb = sb("wqkv_sb", [P, 3 * D])
        bqk_col = sb("bqk_col", [P, 2])
        bv_row = sb("bv_row", [P, D])
        wo_sb = sb("wo_sb", [P, D])
        bo_row = sb("bo_row", [P, D])
        wgate_sb = sb("wgate_sb", [P, EXPERTS])
        ln_cols = sb("ln_cols", [P, 4])
        w1_sb = sb("w1_sb", [P, EXPERTS, HID])
        w2_sb = sb("w2_sb", [P, EXPERTS, HC, D])
        b2_sb = sb("b2_sb", [P, EXPERTS, D])
        head_rows = sb("head_rows", [P, GH])
        expert_no = sb("expert_no", [P, EXPERTS])
        upto = sb("upto", [P, EXPERTS, EXPERTS])
        tile_no = sb("tile_no", [P, MOE_TILES])
        result_row = sb("result_row", [P, TB, TOPK])
        pad_rows = sb("pad_rows", [P, EXPERTS + SPARE, ROW])
        pad_no = sb("pad_no", [P, EXPERTS + SPARE])

        x1_all = sb("x1_all", [P, TILES, D])
        base_all = sb("base_all", [P, TILES, D])
        xt_all = sb("xt_all", [P, TOKENS])
        assert EXPERTS * HID == TOKENS
        b1_sb = xt_all[:].rearrange("p (e h) -> p e h", e=EXPERTS)
        xsq = sb("xsq", [P, SEQ])
        feat = sb("feat", [P, SEQ])
        mixed = sb("mixed", [P, TB, D])
        stats = sb("stats", [P, 3, TB, 6])
        mean_var = sb("mean_var", [P, 3, TB, 2])
        log_var = sb("log_var", [P, 4, TB])
        rstd = sb("rstd", [P, 4, TB])
        normed = sb("normed", [P, TB, D])
        normed_t = sb("normed_t", [P, SEQ])
        qk = sb("qk", [P, 2 * SEQ])
        qk_hi = sb("qk_hi", [P, 2 * SEQ], F32R)
        qk_lo = sb("qk_lo", [P, 2 * SEQ], F32R)
        query_pack = [sb(f"query_pack{p}", [P, GROUPS, SEQ], F32R) for p in range(2)]
        key_pack = [sb(f"key_pack{p}", [P, HEADS, SEQ], F32R) for p in range(2)]
        v_ext = [sb(f"v_ext{p}", [P, TB, HEADS, VW]) for p in range(2)]
        row_max = sb("row_max", [P, TB, GH])
        max_parts = sb("max_parts", [P, TB, P])
        probs = sb("probs", [P, 2 * GH, TB, SEQ])
        mixed_v = sb("mixed_v", [P, SEQ])
        inv_sum = sb("inv_sum", [P, TB, GH])
        context = sb("context", [P, TB, D])
        context_t = sb("context_t", [P, SEQ])
        x1_bo = sb("x1_bo", [P, TB, D])
        hidden = sb("hidden", [P, TB, D])
        rows = sb("rows", [P, TB, TOPK, ROW])
        tok_t = sb("tok_t", [P, SEQ])
        logits = sb("logits", [P, TB, EXPERTS])
        top8 = sb("top8", [P, TB, 8])
        top8_at = sb("top8_at", [P, TB, 8], U32)
        top_at = sb("top_at", [P, TB, TOPK])
        chosen = sb("chosen", [P, TB, TOPK, EXPERTS])
        used = sb("used", [P, TB, EXPERTS], BF16)
        below_top = sb("below_top", [P, TB, TOPK])
        gate_exp = sb("gate_exp", [P, TB, TOPK])
        gate_sum = sb("gate_sum", [P, TB])
        gate_inv = sb("gate_inv", [P, TB])
        slot = sb("slot", [P, TB, EXPERTS])
        slot_of = sb("slot_of", [P, TB, TOPK, EXPERTS])
        place = sb("place", [P, TB * TOPK])
        place_i = sb("place_i", [P, TB * TOPK], I32)
        next_row = sb("next_row", [P, EXPERTS])

        tiles_i = sb("tiles_i", [P, EXPERTS], I32)
        counts_f = sb("counts_f", [P, EXPERTS])
        counts_i = sb("counts_i", [P, EXPERTS], I32)
        tiles_f = sb("tiles_f", [P, EXPERTS])
        tiles_upto = sb("tiles_upto", [P, EXPERTS, EXPERTS])
        tile_end = sb("tile_end", [P, EXPERTS])
        gap = sb("gap", [P, EXPERTS])
        past = sb("past", [P, MOE_TILES, EXPERTS])
        past_gap = sb("past_gap", [P, MOE_TILES, EXPERTS])
        tile_expert = sb("tile_expert", [P, MOE_TILES])
        tile_shift = sb("tile_shift", [P, MOE_TILES])
        tile_row = sb("tile_row", [P, MOE_TILES])
        expert_i = sb("expert_i", [P, MOE_TILES], I32)
        row_i = sb("row_i", [P, MOE_TILES], I32)
        pad_at = sb("pad_at", [P, EXPERTS])
        pad_at_i = sb("pad_at_i", [P, EXPERTS], I32)
        got = [sb(f"got{p}", [P, ROW]) for p in range(4)]
        got_t = [sb(f"got_t{p}", [P, P]) for p in range(2)]
        up = [sb(f"up{p}", [P, HID]) for p in range(2)]
        act = [sb(f"act{p}", [P, HID]) for p in range(2)]
        act_t = [v_ext[p][:].rearrange("p t h e -> p (t h e)")[:, 0:HID] for p in range(2)]
        down = [sb(f"down{p}", [P, D]) for p in range(2)]
        gated = [sb(f"gated{p}", [P, D]) for p in range(2)]
        goes_to = [sb(f"goes_to{p}", [P, 1], I32) for p in range(2)]
        first = [probs[:, 4 * p, :, 0:D] for p in range(2)]
        second = [probs[:, 4 * p + 1, :, 0:D] for p in range(2)]
        total = [probs[:, 4 * p + 2, :, 0:D] for p in range(2)]
        final = [probs[:, 4 * p + 3, :, 0:D] for p in range(2)]

        sorted_dram = nc.dram_tensor("sorted_dram", [EXPERTS * REGION + SPARE * P, ROW], F32, kind="Internal").ap()
        result_dram = nc.dram_tensor("result_dram", [TOPK * TOKENS + (EXPERTS + SPARE) * P, D], F32, kind="Internal").ap()

        spill = [nc.dram_tensor(f"spill{p}", [2, HEADS, PARTS, DH, SEQ], F32, kind="Internal").ap() for p in range(2)]

        banks = [ctx.enter_context(nc.psum_tensor(f"bank{i}", [P, 512], F32)) for i in range(8)]
        score_bank, exp_bank = banks[0:2], banks[2:4]
        pv_bank, turn_bank, front_a, front_b = banks[4:8]
        up_bank, act_t_bank, down_bank = banks[0:2], banks[2:4], banks[4:6]
        got_bank = banks[6]

        loaded_small = sem("loaded_small")
        loaded_x0 = sem("loaded_x0")
        loaded_x = sem("loaded_x")
        loaded_moe = sem("loaded_moe")
        pool_zeroed = sem("pool_zeroed")
        pool_consts = sem("pool_consts")
        setup_vec = sem("setup_vec")
        setup_scaled = sem("setup_scaled")
        setup_transposed = sem("setup_transposed")
        setup_evacuated = sem("setup_evacuated")
        setup_sq = sem("setup_sq")
        setup_arg = sem("setup_arg")
        setup_feat = sem("setup_feat")
        keys_zeroed = sem("keys_zeroed")
        stored_pads = sem("stored_pads")
        squared = sem("squared")
        b_filled, b_drained = sem("b_filled"), sem("b_drained")
        a_filled, a_drained = sem("a_filled"), sem("a_drained")
        stats_done = [sem(f"stats_done{n}") for n in range(3)]
        aggregated = [sem(f"aggregated{n}") for n in range(3)]
        logged = [sem(f"logged{n}") for n in range(3)]
        rstd_done = [sem(f"rstd_done{n}") for n in range(3)]
        x1_done = sem("x1_done")
        normed_done = sem("normed_done")
        hi_done, split_done = sem("hi_done"), sem("split_done")
        spilled = [sem(f"spilled{p}") for p in range(2)]
        packed = [sem(f"packed{p}") for p in range(2)]
        scores_filled, scores_drained = sem("scores_filled"), sem("scores_drained")
        max_hi, max_lo = sem("max_hi"), sem("max_lo")
        turn_filled, turn_drained = sem("turn_filled"), sem("turn_drained")
        keyed_filled = sem("keyed_filled")
        exp_done = sem("exp_done")
        pv_filled, pv_evacuated = sem("pv_filled"), sem("pv_evacuated")
        inverted = sem("inverted")
        x1_bo_done = sem("x1_bo_done")
        base_done = sem("base_done")
        token_row = sem("token_row")
        copied_row = sem("copied_row")
        counted_row = sem("counted_row")
        logits_done = sem("logits_done")
        top_done, top_at_done, top_at_f = sem("top_done"), sem("top_at_done"), sem("top_at_f")
        chosen_done, used_done = sem("chosen_done"), sem("used_done")
        below_done, gate_exp_done, gate_sum_done = sem("below_done"), sem("gate_exp_done"), sem("gate_sum_done")
        gate_inv_done, gate_done = sem("gate_inv_done"), sem("gate_done")
        slot_done, slot_of_done, place_done, placed = sem("slot_done"), sem("slot_of_done"), sem("place_done"), sem("placed")
        scattered = sem("scattered")
        table = sem("table")
        table_ready = sem("table_ready")
        pads_placed = sem("pads_placed")
        got_loaded = [sem(f"got_loaded{p}") for p in range(4)]
        got_turned, got_t_done = sem("got_turned"), sem("got_t_done")
        up_filled, up_drained = sem("up_filled"), sem("up_drained")
        act_done = sem("act_done")
        act_turned, act_t_done = sem("act_turned"), sem("act_t_done")
        down_filled, down_drained = sem("down_filled"), sem("down_drained")
        gated_done = sem("gated_done")
        goes_done = sem("goes_done")
        result_stored = [sem(f"result_stored{p}") for p in range(2)]
        results_back = [sem(f"results_back{p}") for p in range(2)]
        add1, add2, last_stats, last_aggr = sem("add1"), sem("add2"), sem("last_stats"), sem("last_aggr")
        last_log, last_rstd, last_done = sem("last_log"), sem("last_rstd"), sem("last_done")
        out_stored = [sem(f"out_stored{p}") for p in range(2)]

        SMALL = 14
        x_v = x.rearrange("(t p) d -> p t d", p=P)
        out_v = out.rearrange("(t p) d -> p t d", p=P)
        FIRST_TILES = 4 * TB

        block = ctx.enter_context(nc.Block())

        @block.sync
        def _(sp):
            def column(v):
                return v.rearrange("(p o) -> p o", o=1)

            def broadcast(v):
                return v.rearrange("(o n) -> o n", o=1).broadcast_to([P, v.shape[0]])

            for dst, src in (
                (xis_col[:], column(xis)), (proj_rd[:], proj), (w_in_dt[:], w_in_t),
                (wqkv_sb[:], w_qkv), (wo_sb[:], w_o), (wgate_sb[:], w_gate),
                (ln_cols[:, 0:1], column(ln1_w)), (ln_cols[:, 1:2], column(ln1_b)),
                (ln_cols[:, 2:3], column(ln2_w)), (ln_cols[:, 3:4], column(ln2_b)),
                (bqk_col[:, 0:1], column(b_qkv[0:D])), (bqk_col[:, 1:2], column(b_qkv[D:2 * D])),
                (bv_row[:], broadcast(b_qkv[2 * D:3 * D])), (bo_row[:], broadcast(b_o)),
            ):
                sp.dma_start(dst, src).then_inc(loaded_small, 16)
            sp.dma_start(xt_all[:, 0:FIRST_TILES * P], x_t[:, 0:FIRST_TILES * P]).then_inc(loaded_x0, 16)
            sp.dma_start(x1_all[:, 0:FIRST_TILES, :], x_v[:, 0:FIRST_TILES, :]).then_inc(loaded_x0, 16)
            sp.dma_start(xt_all[:, FIRST_TILES * P:], x_t[:, FIRST_TILES * P:]).then_inc(loaded_x, 16)
            sp.dma_start(x1_all[:, FIRST_TILES:, :], x_v[:, FIRST_TILES:, :]).then_inc(loaded_x, 16)

            def pack(b, p, half):
                keyed_before, spills, reads = (b - 1) * HEADS, (half + 1) * 16 * 2 * PARTS, half * 16 * PACKS
                if not isinstance(b, int):
                    keyed_before, spills, reads = sp.to_reg(keyed_before), sp.to_reg(spills), sp.to_reg(reads)
                sp.wait_ge(split_done, b + 1)
                at_least(sp, packed[p], reads)
                for n, orders in enumerate(PART_ORDER):
                    for c, lo in enumerate(orders):
                        part = qk_lo if lo else qk_hi
                        sp.dma_start(spill[p][n, :, c],
                                     part[:, n * SEQ:(n + 1) * SEQ].bitcast(F32)).then_inc(spilled[p], 16)
                sp.wait_ge(spilled[p], spills)
                at_least(sp, keyed_filled, keyed_before)
                sp.dma_start(query_pack[p][0:GH * PR, :, :].bitcast(F32),
                             spill[p][0].rearrange("(g j) c e t -> (j c e) g t", g=GROUPS)).then_inc(packed[p], 16)
                for j in range(GH):
                    sp.dma_start(key_pack[p][PR * j:PR * j + PR, :, :].bitcast(F32).rearrange("r (g j) t -> r g j t", j=GH)[:, :, j, :],
                                 spill[p][1].rearrange("(g j) c e t -> j (c e) g t", j=GH)[j]).then_inc(packed[p], 16)

            sp.wait_ge(keys_zeroed, 4)
            pack(0, 0, 0)

            def emit(body):
                if body.project:
                    pack(body.i + 1, 1 - body.p, body.half(1))

            run_bodies(sp, emit)

            sp.wait_ge(scattered, 16 * TB * TOPK * BATCHES)
            sp.wait_ge(pads_placed, 16 * EXPERTS)
            sp.wait_ge(stored_pads, 16 * SPARE)
            sp.wait_ge(table_ready, 1)

            def load_tile(n, q, r):
                row = sp.value_load(row_i[0:1, bass.ds(n, 1)], min_val=0, max_val=EXPERTS * REGION + (SPARE - 1) * P)
                at_least(sp, gated_done, n - 3)
                at_least(sp, goes_done, n - 3)
                sp.dma_start(got[q][:], sorted_dram[bass.ds(row, P), :]).then_inc(got_loaded[q], 16)

            for n in range(4):
                load_tile(n, n, 0)
            whole = MOE_TILES // 4
            with sp.Fori(1, whole) as r:
                for q in range(4):
                    load_tile(r * 4 + q, q, r)
            for n in range(4 * whole, MOE_TILES):
                load_tile(n, n % 4, n // 4)

            for p in range(2):
                sp.wait_ge(result_stored[p], 16 * ((MOE_TILES + 1 - p) // 2))

            def results(b, p, half):
                at_least(sp, add2, b - 1)
                r_v = result_dram[0:TOPK * TOKENS, :].rearrange("(s t p) d -> s p t d", s=TOPK, p=P)
                sp.dma_start(first[p], r_v[0][:, bass.ds(b * TB, TB), :]).then_inc(results_back[p], 16)
                sp.dma_start(second[p], r_v[1][:, bass.ds(b * TB, TB), :]).then_inc(results_back[p], 16)

            def store(b, p):
                sp.wait_ge(last_done, b + 1)
                sp.dma_start(out_v[:, bass.ds(b * TB, TB), :], final[p]).then_inc(out_stored[p], 16)

            results(0, 0, 0)
            results(1, 1, 0)
            with sp.Fori(0, BATCHES // 2 - 1) as pair:
                for p in range(2):
                    store(pair * 2 + p, p)
                    results(pair * 2 + 2 + p, p, pair + 1)
            for p in range(2):
                store(BATCHES - 2 + p, p)
            for p in range(2):
                sp.wait_ge(out_stored[p], 16 * BATCHES // 2)

        @block.gpsimd
        def _(pool):
            for buf, value in ((ident, 0.0), (before, 1.0), (head_rows, 1.0), (upto, 1.0), (pad_rows, 0.0)):
                pool.memset(buf[:], value).then_inc(pool_zeroed, 1)
            pool.wait_ge(pool_zeroed, 5)
            pool.affine_select(out=ident[:], in_=ident[:], compare_op=ALU.not_equal, fill=1.0, base=0,
                               pattern=[[-1, P]], channel_multiplier=1).then_inc(pool_consts, 1)
            pool.affine_select(out=before[:], in_=before[:], compare_op=ALU.is_gt, fill=0.0, base=0,
                               pattern=[[1, P]], channel_multiplier=-1).then_inc(pool_consts, 1)
            pool.affine_select(out=upto[:], in_=upto[:], compare_op=ALU.is_ge, fill=0.0, base=0,
                               pattern=[[1, EXPERTS], [-1, EXPERTS]], channel_multiplier=0).then_inc(pool_consts, 1)
            pool.affine_select(out=head_rows[:], in_=head_rows[:], compare_op=ALU.is_ge, fill=0.0, base=-96,
                               pattern=[[-2, GH]], channel_multiplier=1).then_inc(pool_consts, 1)
            pool.wait_ge(pool_consts, 4)
            pool.affine_select(out=head_rows[:], in_=head_rows[:], compare_op=ALU.is_ge, fill=0.0, base=97,
                               pattern=[[2, GH]], channel_multiplier=-1).then_inc(pool_consts, 1)
            iota = dict(allow_small_or_imprecise_dtypes=True)
            pool.iota(expert_no[:], pattern=[[1, EXPERTS]], base=0, channel_multiplier=0, **iota).then_inc(pool_consts, 1)
            pool.iota(tile_no[:], pattern=[[1, MOE_TILES]], base=0, channel_multiplier=0, **iota).then_inc(pool_consts, 1)
            pool.iota(next_row[:], pattern=[[REGION, EXPERTS]], base=0, channel_multiplier=0, **iota).then_inc(pool_consts, 1)
            pool.iota(result_row[:], pattern=[[P, TB], [TOKENS, TOPK]], base=0, channel_multiplier=1, **iota).then_inc(pool_consts, 1)
            pool.iota(pad_no[:], pattern=[[P, EXPERTS + SPARE]], base=TOPK * TOKENS, channel_multiplier=1, **iota).then_inc(pool_consts, 1)
            pool.iota(pad_at[:], pattern=[[0, EXPERTS]], base=0, channel_multiplier=1, **iota).then_inc(pool_consts, 1)
            pool.wait_ge(pool_consts, 11)
            pool.tensor_copy(pad_rows[:, :, ROW - 1], pad_no[:]).then_inc(pool_consts, 1)
            pool.wait_ge(pool_consts, 12)
            for k in range(SPARE):
                at = EXPERTS * REGION + k * P
                pool.dma_start(sorted_dram[at:at + P, :], pad_rows[:, EXPERTS + k, :]).then_inc(stored_pads, 16)
            pool.wait_ge(setup_evacuated, 1)
            pool.tensor_tensor(w_in_sq[:], w_in_dt[:], w_in_dt[:], ALU.mult).then_inc(setup_sq, 1)

            def square(b):
                at_least(pool, b_filled, 2 * (b - 1) + 1)
                pool.tensor_tensor(xsq[:], xt_all[:, bass.ds(b * SEQ, SEQ)], xt_all[:, bass.ds(b * SEQ, SEQ)],
                                   ALU.mult).then_inc(squared, 1)

            pool.wait_ge(loaded_x0, 32)
            square(0)
            square(1)
            pool.wait_ge(loaded_x, 32)

            def tail(body):
                b = body.i - 1
                tiles = bass.ds(b * TB, TB)
                if not (isinstance(body.i, int) and body.i == 1):
                    at_least(pool, base_done, b)
                pool.wait_ge(x1_done, b + 1)
                pool.tensor_tensor(x1_bo[:], x1_all[:, tiles, :], bo_row[:].unsqueeze(1).broadcast_to([P, TB, D]),
                                   ALU.add).then_inc(x1_bo_done, 1)
                pool.wait_ge(turn_drained, body.turn("proj") + 1)
                pool.tensor_tensor(base_all[:, tiles, :], hidden[:], x1_all[:, tiles, :], ALU.add).then_inc(base_done, 1)
                apart(pool, pool_consts, (token_row, b + 1))
                pool.tensor_copy(rows[:, :, 1, 0:D], rows[:, :, 0, 0:D]).then_inc(copied_row, 1)
                apart(pool, pool_consts, (counted_row, b))
                pool.tensor_copy(rows[:, :, :, ROW - 1], result_row[:]).then_inc(copied_row, 1)
                apart(pool, pool_consts, (copied_row, 2 * b + 2))
                pool.tensor_scalar(result_row[:], result_row[:], float(SEQ), None, ALU.add).then_inc(counted_row, 1)
                apart(pool, pool_consts, (gate_done, b + 1), (placed, b + 1))
                for t in range(TB):
                    for s in range(TOPK):
                        n = t * TOPK + s
                        pool.indirect_dma_start(
                            out=sorted_dram, out_offset=bass.IndirectOffsetOnAxis(ap=place_i[:, n:n + 1], axis=0),
                            in_=rows[:, t, s, :], in_offset=None).then_inc(scattered, 16)

            def emit(body):
                if body.front:
                    square(body.i + 2)
                if body.prev:
                    tail(body)

            run_bodies(pool, emit)

            pool.wait_ge(table_ready, 1)
            for e in range(EXPERTS):
                pool.indirect_dma_start(
                    out=sorted_dram, out_offset=bass.IndirectOffsetOnAxis(ap=pad_at_i[:, e:e + 1], axis=0),
                    in_=pad_rows[:, e, :], in_offset=None).then_inc(pads_placed, 16)

            def put(n, p, q, half, quarter):
                apart(pool, pool_consts, (got_loaded[q], (quarter + 1) * 16), (result_stored[p], half * 16))
                pool.tensor_copy(goes_to[p][:], got[q][:, ROW - 1:ROW]).then_inc(goes_done, 1)
                apart(pool, pool_consts, (goes_done, n + 1), (gated_done, n + 1))
                pool.indirect_dma_start(
                    out=result_dram, out_offset=bass.IndirectOffsetOnAxis(ap=goes_to[p][:, 0:1], axis=0),
                    in_=gated[p][:], in_offset=None).then_inc(result_stored[p], 16)

            whole = MOE_TILES // 4
            for n in range(4):
                put(n, n % 2, n, n // 2, 0)
            with pool.Fori(1, whole) as r:
                for q in range(4):
                    put(r * 4 + q, q % 2, q, r * 2 + q // 2, r)
            for n in range(4 * whole, MOE_TILES):
                put(n, n % 2, n % 4, n // 2, n // 4)

        @block.tensor
        def _(pe):
            pe.wait_ge(pool_consts, 1)
            pe.wait_ge(setup_scaled, 2)
            for n in range(2):
                last = pe.transpose(score_bank[0][:, n * D:(n + 1) * D], scaled_rd[:, n, :], ident[:])
            last.then_inc(setup_transposed, 1)
            pe.wait_ge(setup_evacuated, 1)
            pe.wait_ge(setup_sq, 1)
            pe.matmul(score_bank[1][:, 0:D], scaled_dr[:, 0, :], w_in_dt[:], start=True, stop=False)
            pe.matmul(score_bank[1][:, 0:D], scaled_dr[:, 1, :], w_in_sq[:], start=False, stop=True).then_inc(setup_arg, 1)

            def features(b):
                pe.wait_ge(squared, b + 1)
                at_least(pe, b_drained, 2 * b)
                pe.matmul(front_b[:, 0:SEQ], scaled_dr[:, 0, :], xt_all[:, bass.ds(b * SEQ, SEQ)], start=True, stop=False)
                pe.matmul(front_b[:, 0:SEQ], scaled_dr[:, 1, :], xsq[:], start=False, stop=True).then_inc(b_filled, 1)

            def mix(b):
                pe.wait_ge(b_drained, 2 * b + 1)
                at_least(pe, a_drained, 3 * b)
                for t in range(TB):
                    last = pe.matmul(front_a[:, t * D:(t + 1) * D], feat[:, t * P:(t + 1) * P], w_feat[:], start=True, stop=True)
                last.then_inc(a_filled, 1)

            def turn_normed(b):
                pe.wait_ge(normed_done, b + 1)
                pe.wait_ge(a_drained, 3 * b + 1)
                for t in range(TB):
                    last = pe.transpose(front_a[:, t * P:(t + 1) * P], normed[:, t, :], ident[:])
                last.then_inc(a_filled, 1)

            def project_qk(b):
                pe.wait_ge(a_drained, 3 * b + 2)
                pe.wait_ge(b_drained, 2 * b + 1)
                for n in range(2):
                    last = pe.matmul(front_b[:, n * SEQ:(n + 1) * SEQ], wqkv_sb[:, n * D:(n + 1) * D], normed_t[:],
                                     start=True, stop=True)
                last.then_inc(b_filled, 1)

            def project_v(b):
                pe.wait_ge(a_drained, 3 * b + 2)
                for t in range(TB):
                    last = pe.matmul(front_a[:, t * D:(t + 1) * D], normed_t[:, t * P:(t + 1) * P],
                                     wqkv_sb[:, 2 * D:3 * D], start=True, stop=True)
                last.then_inc(a_filled, 1)

            pe.wait_ge(setup_feat, 1)
            pe.wait_ge(loaded_small, 16 * SMALL)
            features(0)
            mix(0)
            turn_normed(0)
            project_qk(0)
            project_v(0)
            features(1)
            mix(1)
            turn_normed(1)

            def scores(body, g, u):
                group = body.i * GROUPS + g
                qt, pair = u // 2, u % 2
                if g == 0 and u == 0:
                    pe.wait_ge(packed[body.p], (body.half(0) + 1) * 16 * PACKS)
                at_least(pe, scores_drained, group * 4 + u - 1)
                h = GH * g + 2 * pair
                pe.matmul(score_bank[u % 2][:, :], query_pack[body.p][0:96, g, qt * P:(qt + 1) * P],
                          key_pack[body.p][0:96, h:h + 2, :], start=True, stop=True).then_inc(scores_filled, 1)

            def turn_max(body, name, group):
                pe.wait_ge(max_lo, group + 1)
                at_least(pe, turn_drained, body.turn(name))
                for t in range(TB):
                    last = pe.transpose(turn_bank[:, t * P:(t + 1) * P], max_parts[:, t, :], ident[:])
                last.then_inc(turn_filled, 1)

            def keyed(body, g, j, m_name):
                group = body.i * GROUPS + g - 1
                p, gg = (body.p, g - 1) if g else (1 - body.p, GROUPS - 1)
                if j == 0:
                    pe.wait_ge(turn_drained, body.turn(m_name) + 1)
                at_least(pe, exp_done, group * GH + j - 1)
                for kt in range(TB):
                    last = pe.matmul(exp_bank[j % 2][:, kt * SEQ:(kt + 1) * SEQ],
                                     key_pack[p][:, GH * gg + j, kt * P:(kt + 1) * P], query_pack[p][:, gg, :],
                                     start=True, stop=True)
                last.then_inc(keyed_filled, 1)

            def values(body, g):
                group = body.i * GROUPS + g - 2
                p, gg, b = (body.p, g - 2, body.i) if g >= 2 else (1 - body.p, g + 2, body.i - 1)
                pe.wait_ge(exp_done, group * GH + GH)
                at_least(pe, pv_evacuated, group)
                pe.wait_ge(a_drained, 3 * b + 3)
                for kt in range(TB):
                    for j in range(GH):
                        last = pe.matmul(pv_bank[VW * j:VW * j + VW, 0:SEQ], v_ext[p][:, kt, GH * gg + j, :],
                                         probs[:, GH * (gg % 2) + j, kt, :], start=kt == 0, stop=kt == TB - 1,
                                         tile_position=(0, VW * j))
                last.then_inc(pv_filled, 1)

            def turn_values(body, name, g):
                group = body.i * GROUPS + g - 2
                pe.wait_ge(pv_evacuated, group + 1)
                at_least(pe, turn_drained, body.turn(name))
                for t in range(TB):
                    last = pe.transpose(turn_bank[:, t * P:(t + 1) * P], mixed_v[:, t * P:(t + 1) * P], ident[:])
                last.then_inc(turn_filled, 1)

            def turn_context(body):
                pe.wait_ge(turn_drained, body.turn("ctx"))
                for t in range(TB):
                    last = pe.transpose(turn_bank[:, t * P:(t + 1) * P], context[:, t, :], ident[:])
                last.then_inc(turn_filled, 1)

            def project_out(body):
                pe.wait_ge(turn_drained, body.turn("proj"))
                for t in range(TB):
                    last = pe.matmul(turn_bank[:, t * D:(t + 1) * D], context_t[:, t * P:(t + 1) * P], wo_sb[:],
                                     start=True, stop=True)
                last.then_inc(turn_filled, 1)

            def turn_tokens(body):
                pe.wait_ge(token_row, body.i)
                pe.wait_ge(turn_drained, body.turn("ln2"))
                for t in range(TB):
                    last = pe.transpose(turn_bank[:, t * P:(t + 1) * P], rows[:, t, 0, 0:D], ident[:])
                last.then_inc(turn_filled, 1)

            def gate_logits(body):
                pe.wait_ge(turn_drained, body.turn("gate"))
                for t in range(TB):
                    last = pe.matmul(turn_bank[:, t * EXPERTS:(t + 1) * EXPERTS], tok_t[:, t * P:(t + 1) * P], wgate_sb[:],
                                     start=True, stop=True)
                last.then_inc(turn_filled, 1)

            def ranks(body):
                pe.wait_ge(used_done, body.i)
                pe.wait_ge(turn_drained, body.turn("rank"))
                e = EXPERTS
                pe.matmul(turn_bank[:, 0:e], before[:], used[:, 0, :], start=True, stop=True)
                pe.matmul(turn_bank[:, e:2 * e], before[:], used[:, 1, :], start=True, stop=False)
                pe.matmul(turn_bank[:, e:2 * e], ones_bf[:], used[:, 0, :], start=False, stop=True)
                pe.matmul(turn_bank[:, 2 * e:3 * e], ones_bf[:], used[:, 0, :], start=True, stop=False)
                pe.matmul(turn_bank[:, 2 * e:3 * e], ones_bf[:], used[:, 1, :], start=False, stop=True).then_inc(turn_filled, 1)

            def emit(body):
                first = not body.prev
                for g in range(GROUPS):
                    m_name = ("m3", "m0", "m1", "m2")[g]
                    u_name = ("u2", "u3", "u0", "u1")[g]
                    has_m = (g > 0 and body.core) or (g == 0 and body.prev)
                    has_u = (g >= 2 and body.core) or (g < 2 and body.prev)
                    if has_m:
                        turn_max(body, m_name, body.i * GROUPS + g - 1)
                    if body.core:
                        scores(body, g, 0)
                        scores(body, g, 1)
                    if has_u:
                        values(body, g)
                    if body.prev and g == 2:
                        project_out(body)
                    if g == 0 and body.project:
                        project_qk(body.i + 1)
                    if g == 1 and body.project:
                        project_v(body.i + 1)
                    if g == 3:
                        if body.front:
                            turn_normed(body.i + 2)
                        if body.prev:
                            gate_logits(body)
                    for j in range(GH):
                        if has_m and j == GH - 1 and has_u:
                            turn_values(body, u_name, g)
                        if has_m:
                            keyed(body, g, j, m_name)
                        if body.core and j < 2:
                            scores(body, g, 2 + j)
                    if has_u and not has_m:
                        turn_values(body, u_name, g)
                    if g == 0 and body.front:
                        features(body.i + 2)
                    if g == 1:
                        if body.front:
                            mix(body.i + 2)
                        if body.prev:
                            turn_context(body)
                    if g == 2 and body.prev:
                        turn_tokens(body)
                    if g == 3 and body.prev:
                        ranks(body)

            run_bodies(pe, emit)

            pe.wait_ge(table_ready, 1)
            pe.wait_ge(loaded_moe, 16 * 4)

            def expert_of(n):
                return pe.value_load(expert_i[0:1, bass.ds(n, 1)], min_val=0, max_val=EXPERTS - 1)

            def turn_got(n, p, q, quarter):
                pe.wait_ge(got_loaded[q], (quarter + 1) * 16)
                at_least(pe, got_t_done, n)
                pe.transpose(got_bank[:, 0:P], got[q][:, 0:D], ident[:]).then_inc(got_turned, 1)

            def go_up(n, p):
                e = expert_of(n)
                pe.wait_ge(got_t_done, n + 1)
                at_least(pe, up_drained, n - 1)
                pe.matmul(up_bank[p][:, :], got_t[p][:], w1_sb[:, bass.ds(e, 1), :], start=True, stop=True).then_inc(up_filled, 1)

            def turn_act(n, p):
                pe.wait_ge(act_done, n + 1)
                at_least(pe, act_t_done, n - 1)
                for c in range(HC):
                    last = pe.transpose(act_t_bank[p][:, c * P:(c + 1) * P], act[p][:, c * P:(c + 1) * P], ident[:])
                last.then_inc(act_turned, 1)

            def go_down(n, p):
                e = expert_of(n)
                pe.wait_ge(act_t_done, n + 1)
                at_least(pe, down_drained, n - 1)
                for c in range(HC):
                    last = pe.matmul(down_bank[p][:, 0:D], act_t[p][:, c * P:(c + 1) * P], w2_sb[:, bass.ds(e, 1), c, :],
                                     start=c == 0, stop=c == HC - 1)
                last.then_inc(down_filled, 1)

            def slot_of_pe(n, q, quarter, next_quarter):
                fixed = isinstance(n, int)
                if not fixed or n < MOE_TILES:
                    go_up(n, q % 2)
                if not fixed or n >= 2:
                    go_down(n - 2, q % 2)
                if not fixed or n + 1 < MOE_TILES:
                    turn_got(n + 1, (q + 1) % 2, (q + 1) % 4, next_quarter)
                if (not fixed or n >= 1) and (not fixed or n <= MOE_TILES):
                    turn_act(n - 1, (q + 1) % 2)

            turn_got(0, 0, 0, 0)
            whole = MOE_TILES // 4
            for n in range(4):
                slot_of_pe(n, n, 0, (n + 1) // 4)
            with pe.Fori(1, whole) as r:
                for q in range(4):
                    slot_of_pe(r * 4 + q, q, r, r + (q + 1) // 4)
            for n in range(4 * whole, MOE_TILES + 2):
                slot_of_pe(n, n % 4, n // 4, (n + 1) // 4)

        @block.scalar
        def _(a):
            a.preload_act_table_set("natural_log_exp_and_others")
            a.dma_start(w1_sb[:], w1.rearrange("e d h -> d e h")).then_inc(loaded_moe, 16)
            a.dma_start(w2_sb[:], w2.rearrange("e (c p) d -> p e c d", p=P)).then_inc(loaded_moe, 16)
            a.dma_start(b2_sb[:], b2.rearrange("(o e) d -> o e d", o=1).broadcast_to([P, EXPERTS, D])).then_inc(loaded_moe, 16)
            a.wait_ge(setup_arg, 1)
            a.activation(w_feat[:], score_bank[1][:, 0:D], ACT.Exp, bias=feat_bias[:, 0:1]).then_inc(setup_feat, 1)

            def feature_exp(b):
                a.wait_ge(b_filled, 2 * b + 1)
                at_least(a, a_filled, 3 * (b - 1) + 1)
                a.activation(feat[:], front_b[:, 0:SEQ], ACT.Exp, bias=feat_bias[:, 0:1]).then_inc(b_drained, 1)

            def inverse_std(n, b):
                a.wait_ge(aggregated[n], b + 1)
                a.activation(log_var[:, n, :], mean_var[:, n, :, 1], ACT.Ln, bias=eps_col[:, 0:1]).then_inc(logged[n], 1)
                a.wait_ge(logged[n], b + 1)
                a.activation(rstd[:, n, :], log_var[:, n, :], ACT.Exp, scale=-0.5).then_inc(rstd_done[n], 1)

            def bias_qk(b):
                a.wait_ge(b_filled, 2 * b + 2)
                at_least(a, split_done, b)
                for n in range(2):
                    last = a.activation(qk[:, n * SEQ:(n + 1) * SEQ], front_b[:, n * SEQ:(n + 1) * SEQ], ACT.Identity,
                                        bias=bqk_col[:, n:n + 1])
                last.then_inc(b_drained, 1)

            a.wait_ge(setup_vec, 4)
            a.wait_ge(loaded_small, 16 * SMALL)
            feature_exp(0)
            inverse_std(0, 0)
            inverse_std(1, 0)
            bias_qk(0)
            feature_exp(1)
            inverse_std(0, 1)
            inverse_std(1, 1)

            def place_max(body, g, name):
                p, gg = (body.p, g - 1) if g else (1 - body.p, GROUPS - 1)
                a.wait_ge(turn_filled, body.turn(name) + 1)
                a.activation(query_pack[p][96:P, gg, :], turn_bank[96:P, 0:SEQ], ACT.Copy).then_inc(turn_drained, 1)

            def evacuate_values(body, g, before_name):
                group = body.i * GROUPS + g - 2
                a.wait_ge(pv_filled, group + 1)
                if before_name:
                    a.wait_ge(turn_filled, body.turn(before_name) + 1)
                a.activation(mixed_v[:], pv_bank[:, 0:SEQ], ACT.Copy).then_inc(pv_evacuated, 1)

            def exponential(body, g, j):
                group = body.i * GROUPS + g - 1
                a.wait_ge(keyed_filled, group * GH + j + 1)
                if j == 0:
                    at_least(a, pv_filled, group - 1)
                a.activation(probs[:, GH * ((g + 1) % 2) + j, :, :], exp_bank[j % 2][:, :], ACT.Exp,
                             scale=SCALE).then_inc(exp_done, 1)

            def emit(body):
                if isinstance(body.i, int) and body.i == BATCHES - 2:
                    a.wait_ge(b_filled, 2 * BATCHES - 1)
                    a.dma_start(b1_sb, b1.rearrange("(o e) h -> o e h", o=1).broadcast_to([P, EXPERTS, HID])).then_inc(loaded_moe, 16)
                for g in range(GROUPS):
                    has_m = (g > 0 and body.core) or (g == 0 and body.prev)
                    has_u = (g >= 2 and body.core) or (g < 2 and body.prev)
                    if g == 2 and body.prev:
                        a.wait_ge(turn_filled, body.turn("ctx") + 1)
                        a.activation(context_t[:], turn_bank[:, 0:SEQ], ACT.Copy).then_inc(turn_drained, 1)
                    if has_m:
                        place_max(body, g, ("m3", "m0", "m1", "m2")[g])
                    if has_u:
                        before_name = ("m3", "u2", "u3" if body.prev else None, "u0")[g]
                        evacuate_values(body, g, before_name)
                    if g == 0 and body.project:
                        bias_qk(body.i + 1)
                    if g == 2 and body.front:
                        inverse_std(0, body.i + 2)
                    for j in range(GH):
                        if has_m:
                            exponential(body, g, j)
                        if g == 2 and j == 1:
                            if body.front:
                                inverse_std(1, body.i + 2)
                            if body.prev:
                                inverse_std(2, body.i - 1)
                    if g == 0 and body.front:
                        feature_exp(body.i + 2)
                    if g == 3 and body.prev:
                        a.wait_ge(below_done, body.i)
                        a.activation(gate_exp[:], below_top[:], ACT.Exp).then_inc(gate_exp_done, 1)

            run_bodies(a, emit)

            def tile_act(n, p):
                a.wait_ge(up_drained, n + 1)
                at_least(a, act_turned, n - 1)
                a.activation(act[p][:], up[p][:], ACT.Gelu_apprx_tanh).then_inc(act_done, 1)

            def tile_act_t(n, p):
                a.wait_ge(act_turned, n + 1)
                at_least(a, down_filled, n - 1)
                a.activation(act_t[p], act_t_bank[p][:, :], ACT.Copy).then_inc(act_t_done, 1)

            tile_act(0, 0)
            tile_act(1, 1)
            tile_act_t(0, 0)
            tile_act(2, 0)
            tile_act_t(1, 1)
            with a.Fori(1, (MOE_TILES - 1) // 2) as pair:
                tile_act(pair * 2 + 1, 1)
                tile_act_t(pair * 2, 0)
                tile_act(pair * 2 + 2, 0)
                tile_act_t(pair * 2 + 1, 1)
            tile_act_t(MOE_TILES - 1, 0)

            a.preload_act_table_set("natural_log_exp_and_others")

            def last_inverse(b, p):
                a.wait_ge(last_aggr, b + 1)
                a.activation(log_var[:, p, :], mean_var[:, p, :, 1], ACT.Ln, bias=eps_col[:, 0:1]).then_inc(last_log, 1)
                a.wait_ge(last_log, b + 1)
                a.activation(rstd[:, p, :], log_var[:, p, :], ACT.Exp, scale=-0.5).then_inc(last_rstd, 1)

            with a.Fori(0, BATCHES // 2) as pair:
                last_inverse(pair * 2, 0)
                last_inverse(pair * 2 + 1, 1)

        @block.vector
        def _(v):
            v.memset(zeros[:], 0.0).then_inc(setup_vec, 1)
            v.memset(eps_col[:], EPS).then_inc(setup_vec, 1)
            v.memset(ones_bf[:], 1.0).then_inc(setup_vec, 1)
            for p in range(2):
                v.memset(v_ext[p][:], 0.0)
            v.memset(max_parts[:], 0.0)
            v.wait_ge(loaded_small, 16 * SMALL)
            v.tensor_scalar(feat_bias[:], xis_col[:], -0.5 * math.log(D), None, ALU.add).then_inc(setup_vec, 1)
            v.tensor_tensor(neg_half_sq[:], xis_col[:], xis_col[:], ALU.mult).then_inc(setup_vec, 1)
            v.wait_ge(setup_vec, 5)
            for p in range(2):
                v.memset(v_ext[p][:, :, :, DH:DH + 1], 1.0)
            v.tensor_scalar(scaled_rd[:, 0, :], proj_rd[:], xis_col[:, 0:1], None, ALU.mult).then_inc(setup_scaled, 1)
            v.tensor_scalar(scaled_rd[:, 1, :], zeros[:, 0:D], neg_half_sq[:, 0:1], -0.5, ALU.add, ALU.mult).then_inc(setup_scaled, 1)
            v.wait_ge(setup_transposed, 1)
            v.tensor_copy(scaled_dr[:], score_bank[0][:, 0:2 * D].rearrange("p (n d) -> p n d", n=2)).then_inc(setup_evacuated, 1)
            v.wait_ge(pool_consts, 5)
            for p in range(2):
                v.memset(key_pack[p][0:96, :, :].bitcast(F32), 0.0).then_inc(keys_zeroed, 1)
                for h in range(HEADS):
                    last = v.tensor_scalar(key_pack[p][96:P, h, :], zeros[96:P, :], head_rows[96:P, h % GH:h % GH + 1], None, ALU.add)
                last.then_inc(keys_zeroed, 1)

            def statistics(n, b, source):
                for t in range(TB):
                    last = v.bn_stats(stats[:, n, t, :], source[:, t, :])
                last.then_inc(stats_done[n], 1)
                apart(v, setup_vec, (stats_done[n], b + 1))
                for t in range(TB):
                    last = v.bn_aggr(mean_var[:, n, t, :], stats[:, n, t, :])
                last.then_inc(aggregated[n], 1)

            def normalise(n, t, dst, src):
                return v.tensor_scalar(dst, src, mean_var[:, n, t, 0:1], rstd[:, n, t:t + 1], ALU.subtract, ALU.mult)

            def add_mixed(b):
                v.wait_ge(a_filled, 3 * b + 1)
                v.tensor_tensor(mixed[:], front_a[:, 0:SEQ].rearrange("p (t d) -> p t d", t=TB),
                                x1_all[:, bass.ds(b * TB, TB), :], ALU.add).then_inc(a_drained, 1)
                apart(v, setup_vec, (a_drained, 3 * b + 1))
                statistics(0, b, mixed)

            def first_norm(b):
                v.wait_ge(rstd_done[0], b + 1)
                for t in range(TB):
                    last = normalise(0, t, x1_all[:, bass.ds(b * TB + t, 1), :], mixed[:, t:t + 1, :])
                last.then_inc(x1_done, 1)
                apart(v, setup_vec, (x1_done, b + 1))
                for t in range(TB):
                    last = v.bn_stats(stats[:, 1, t, :], x1_all[:, bass.ds(b * TB + t, 1), :])
                last.then_inc(stats_done[1], 1)
                apart(v, setup_vec, (stats_done[1], b + 1))
                for t in range(TB):
                    last = v.bn_aggr(mean_var[:, 1, t, :], stats[:, 1, t, :])
                last.then_inc(aggregated[1], 1)

            def second_norm(b):
                v.wait_ge(rstd_done[1], b + 1)
                at_least(v, a_filled, 3 * (b - 1) + 2)
                for t in range(TB):
                    last = normalise(1, t, normed[:, t:t + 1, :], x1_all[:, bass.ds(b * TB + t, 1), :])
                last.then_inc(normed_done, 1)

            def evacuate_normed(b):
                v.wait_ge(a_filled, 3 * b + 2)
                v.tensor_scalar(normed_t[:], front_a[:, 0:SEQ], ln_cols[:, 0:1], ln_cols[:, 1:2], ALU.mult, ALU.add).then_inc(a_drained, 1)

            def split_qk(b, p_before, half_before):
                v.wait_ge(b_drained, 2 * b + 2)
                at_least(v, packed[p_before], half_before * 16 * PACKS)
                v.tensor_copy(qk_hi[:], qk[:]).then_inc(hi_done, 1)
                v.wait_ge(hi_done, b + 1)
                v.tensor_tensor(qk_lo[:], qk[:], qk_hi[:].bitcast(F32), ALU.subtract).then_inc(split_done, 1)

            def evacuate_v(b, p):
                v.wait_ge(a_filled, 3 * b + 3)
                at_least(v, pv_filled, (b - 1) * GROUPS)
                v.tensor_tensor(v_ext[p][:, :, :, 0:DH], front_a[:, 0:SEQ].rearrange("p (t h e) -> p t h e", t=TB, h=HEADS),
                                bv_row[:].rearrange("p (o h e) -> p o h e", o=1, h=HEADS).broadcast_to([P, TB, HEADS, DH]),
                                ALU.add).then_inc(a_drained, 1)

            v.wait_ge(loaded_x0, 32)
            add_mixed(0)
            first_norm(0)
            second_norm(0)
            evacuate_normed(0)
            split_qk(0, 1, 0)
            evacuate_v(0, 0)
            add_mixed(1)
            first_norm(1)
            second_norm(1)
            evacuate_normed(1)
            v.wait_ge(loaded_x, 32)

            def reduce_scores(body, g, u):
                group = body.i * GROUPS + g
                qt, pair = u // 2, u % 2
                v.wait_ge(scores_filled, group * 4 + u + 1)
                v.reduce_max(row_max[:, qt, 2 * pair:2 * pair + 2], score_bank[u % 2][:, :].rearrange("p (h k) -> p h k", h=2),
                             AX.X).then_inc(scores_drained, 1)

            def split_max(body, g, before_name):
                group = body.i * GROUPS + g
                v.wait_ge(scores_drained, group * 4 + 4)
                if before_name:
                    v.wait_ge(turn_filled, body.turn(before_name) + 1)
                parts = max_parts[:, :, 96:96 + 2 * GH].rearrange("p t (j s) -> p t j s", s=2)
                v.tensor_scalar(parts[:, :, :, 0].bitcast(F32R), row_max[:], -1.0, None, ALU.mult).then_inc(max_hi, 1)
                v.wait_ge(max_hi, group + 1)
                v.scalar_tensor_tensor(parts[:, :, :, 1].bitcast(F32R), row_max[:], -1.0, parts[:, :, :, 0],
                                       ALU.mult, ALU.subtract).then_inc(max_lo, 1)

            def normalise_values(body, g, name):
                group = body.i * GROUPS + g - 2
                gg = (g + 2) % GROUPS
                heads = turn_bank[:, 0:SEQ].rearrange("p (t j e) -> p t j e", t=TB, j=GH)
                v.wait_ge(turn_filled, body.turn(name) + 1)
                v.reciprocal(inv_sum[:], heads[:, :, :, DH]).then_inc(inverted, 1)
                v.wait_ge(inverted, group + 1)
                ctx_v = context[:, :, gg * GH * DH:(gg + 1) * GH * DH].rearrange("p t (j e) -> p t j e", j=GH)
                v.tensor_tensor(ctx_v, heads[:, :, :, 0:DH], inv_sum[:].unsqueeze(3).broadcast_to([P, TB, GH, DH]),
                                ALU.mult).then_inc(turn_drained, 1)

            def add_attention(body):
                b = body.i - 1
                v.wait_ge(turn_filled, body.turn("proj") + 1)
                v.wait_ge(x1_bo_done, b + 1)
                at_least(v, base_done, b)
                v.tensor_tensor(hidden[:], turn_bank[:, 0:SEQ].rearrange("p (t d) -> p t d", t=TB), x1_bo[:], ALU.add).then_inc(turn_drained, 1)
                apart(v, setup_vec, (turn_drained, body.turn("proj") + 1))
                statistics(2, b, hidden)

            def third_norm(body):
                b = body.i - 1
                v.wait_ge(rstd_done[2], b + 1)
                at_least(v, scattered, b * (16 * TB * TOPK))
                for t in range(TB):
                    last = normalise(2, t, rows[:, t, 0, 0:D], hidden[:, t, :])
                last.then_inc(token_row, 1)

            def evacuate_tokens(body):
                v.wait_ge(turn_filled, body.turn("ln2") + 1)
                v.tensor_scalar(tok_t[:], turn_bank[:, 0:SEQ], ln_cols[:, 2:3], ln_cols[:, 3:4], ALU.mult, ALU.add).then_inc(turn_drained, 1)

            def copy_logits(body):
                v.wait_ge(turn_filled, body.turn("gate") + 1)
                v.tensor_copy(logits[:], turn_bank[:, 0:TB * EXPERTS].rearrange("p (t e) -> p t e", t=TB)).then_inc(turn_drained, 1)

            def choose(body):
                b = body.i - 1
                apart(v, setup_vec, (turn_drained, body.turn("gate") + 1))
                for t in range(TB):
                    last = v.max(top8[:, t, :], logits[:, t, :])
                last.then_inc(top_done, 1)
                apart(v, setup_vec, (top_done, b + 1))
                for t in range(TB):
                    last = v.max_index(top8_at[:, t, :], top8[:, t, :], logits[:, t, :])
                last.then_inc(top_at_done, 1)
                v.tensor_tensor(below_top[:], top8[:, :, 0:TOPK], top8[:, :, 0:1].broadcast_to([P, TB, TOPK]), ALU.subtract).then_inc(below_done, 1)
                v.wait_ge(top_at_done, b + 1)
                v.tensor_copy(top_at[:], top8_at[:, :, 0:TOPK]).then_inc(top_at_f, 1)
                v.wait_ge(top_at_f, b + 1)
                v.tensor_tensor(chosen[:], expert_no[:].rearrange("p (a c e) -> p a c e", a=1, c=1).broadcast_to([P, TB, TOPK, EXPERTS]),
                                top_at[:].unsqueeze(3).broadcast_to([P, TB, TOPK, EXPERTS]), ALU.is_equal).then_inc(chosen_done, 1)
                v.wait_ge(chosen_done, b + 1)
                v.tensor_tensor(used[:], chosen[:, :, 0, :], chosen[:, :, 1, :], ALU.add).then_inc(used_done, 1)

            def gates(body):
                b = body.i - 1
                v.wait_ge(gate_exp_done, b + 1)
                v.reduce_sum(gate_sum[:], gate_exp[:], AX.X).then_inc(gate_sum_done, 1)
                v.wait_ge(gate_sum_done, b + 1)
                v.reciprocal(gate_inv[:], gate_sum[:]).then_inc(gate_inv_done, 1)
                v.wait_ge(gate_inv_done, b + 1)
                v.tensor_tensor(rows[:, :, :, D], gate_exp[:], gate_inv[:].unsqueeze(2).broadcast_to([P, TB, TOPK]), ALU.mult).then_inc(gate_done, 1)

            def places(body):
                b = body.i - 1
                ranks = turn_bank[:, 0:TB * EXPERTS].rearrange("p (t e) -> p t e", t=TB)
                v.wait_ge(turn_filled, body.turn("rank") + 1)
                v.tensor_tensor(slot[:], ranks, next_row[:].unsqueeze(1).broadcast_to([P, TB, EXPERTS]), ALU.add).then_inc(slot_done, 1)
                v.wait_ge(slot_done, b + 1)
                v.tensor_tensor(next_row[:], turn_bank[:, TB * EXPERTS:(TB + 1) * EXPERTS], next_row[:], ALU.add).then_inc(turn_drained, 1)
                v.tensor_tensor(slot_of[:], chosen[:], slot[:].unsqueeze(2).broadcast_to([P, TB, TOPK, EXPERTS]), ALU.mult).then_inc(slot_of_done, 1)
                v.wait_ge(slot_of_done, b + 1)
                v.reduce_sum(place[:], slot_of[:].rearrange("p t s e -> p (t s) e"), AX.X).then_inc(place_done, 1)
                v.wait_ge(place_done, b + 1)
                at_least(v, scattered, b * (16 * TB * TOPK))
                v.tensor_copy(place_i[:], place[:]).then_inc(placed, 1)

            def emit(body):
                for g in range(GROUPS):
                    has_u = (g >= 2 and body.core) or (g < 2 and body.prev)
                    before_name = ("m3" if body.prev else None, "m0", "m1", "m2")[g]
                    u_name = ("u2", "u3", "u0", "u1")[g]
                    if g == 3 and body.prev:
                        evacuate_tokens(body)
                    if body.core:
                        reduce_scores(body, g, 0)
                        reduce_scores(body, g, 1)
                    if g == 0 and body.project:
                        split_qk(body.i + 1, body.p, body.half(0) + 1)
                    if g == 1 and body.project:
                        evacuate_v(body.i + 1, 1 - body.p)
                    if g == 2:
                        if body.prev:
                            add_attention(body)
                        if body.front:
                            first_norm(body.i + 2)
                    if g == 3:
                        if body.front:
                            evacuate_normed(body.i + 2)
                        if body.prev:
                            copy_logits(body)
                    if body.core:
                        reduce_scores(body, g, 2)
                        reduce_scores(body, g, 3)
                        split_max(body, g, before_name)
                    if g == 3 and body.prev:
                        choose(body)
                    if has_u:
                        normalise_values(body, g, u_name)
                    if g == 1 and body.front:
                        add_mixed(body.i + 2)
                    if g == 2:
                        if body.front:
                            second_norm(body.i + 2)
                        if body.prev:
                            third_norm(body)
                    if g == 3 and body.prev:
                        gates(body)
                        places(body)

            run_bodies(v, emit)

            steps = [0]

            def link(instruction):
                steps[0] += 1
                instruction.then_inc(table, 1)
                v.wait_ge(table, steps[0])

            v.wait_ge(turn_drained, Body(BATCHES, False).turn("rank") + 1)
            v.tensor_tensor(pad_at[:], pad_at[:], next_row[:], ALU.add).then_inc(table, 1)
            steps[0] += 1
            link(v.scalar_tensor_tensor(counts_f[:], expert_no[:], -float(REGION), next_row[:], ALU.mult, ALU.add))
            link(v.tensor_scalar(counts_i[:], counts_f[:], float(P - 1), None, ALU.add))
            link(v.tensor_scalar(tiles_i[:], counts_i[:], int(math.log2(P)), None, ALU.arith_shift_right))
            link(v.tensor_copy(tiles_f[:], tiles_i[:]))
            link(v.tensor_tensor(tiles_upto[:], upto[:], tiles_f[:].unsqueeze(1).broadcast_to([P, EXPERTS, EXPERTS]), ALU.mult))
            link(v.reduce_sum(tile_end[:], tiles_upto[:], AX.X))
            link(v.tensor_scalar(gap[:], tiles_f[:], -float(P), float(REGION), ALU.mult, ALU.add))
            link(v.tensor_tensor(past[:], tile_no[:].unsqueeze(2).broadcast_to([P, MOE_TILES, EXPERTS]),
                                 tile_end[:].unsqueeze(1).broadcast_to([P, MOE_TILES, EXPERTS]), ALU.is_ge))
            link(v.reduce_sum(tile_expert[:], past[:], AX.X))
            link(v.tensor_tensor(past_gap[:], past[:], gap[:].unsqueeze(1).broadcast_to([P, MOE_TILES, EXPERTS]), ALU.mult))
            link(v.reduce_sum(tile_shift[:], past_gap[:], AX.X))
            link(v.scalar_tensor_tensor(tile_row[:], tile_no[:], float(P), tile_shift[:], ALU.mult, ALU.add))
            link(v.tensor_scalar(expert_i[:], tile_expert[:], float(EXPERTS - 1), None, ALU.min))
            link(v.tensor_copy(pad_at_i[:], pad_at[:]))
            v.tensor_copy(row_i[:], tile_row[:]).then_inc(table_ready, 1)
            v.wait_ge(table_ready, 1)
            v.wait_ge(loaded_moe, 16 * 4)

            def evacuate_got(n, p):
                v.wait_ge(got_turned, n + 1)
                at_least(v, up_filled, n - 1)
                v.tensor_scalar(got_t[p][:], got_bank[:, 0:P], ln_cols[:, 2:3], ln_cols[:, 3:4], ALU.mult, ALU.add).then_inc(got_t_done, 1)

            def bias_up(n, p):
                e = v.value_load(expert_i[0:1, bass.ds(n, 1)], min_val=0, max_val=EXPERTS - 1)
                v.wait_ge(up_filled, n + 1)
                at_least(v, act_done, n - 1)
                v.tensor_tensor(up[p][:].unsqueeze(1), up_bank[p][:, :].unsqueeze(1), b1_sb[:, bass.ds(e, 1), :], ALU.add).then_inc(up_drained, 1)

            def gate_down(n, p, q, half):
                e = v.value_load(expert_i[0:1, bass.ds(n, 1)], min_val=0, max_val=EXPERTS - 1)
                v.wait_ge(down_filled, n + 1)
                v.tensor_tensor(down[p][:].unsqueeze(1), down_bank[p][:, 0:D].unsqueeze(1), b2_sb[:, bass.ds(e, 1), :], ALU.add).then_inc(down_drained, 1)
                v.wait_ge(down_drained, n + 1)
                at_least(v, result_stored[p], 16 * half)
                v.tensor_scalar(gated[p][:], down[p][:], got[q][:, D:D + 1], None, ALU.mult).then_inc(gated_done, 1)

            def slot_of_v(n, q, halves):
                fixed = isinstance(n, int)
                if not fixed or n + 1 < MOE_TILES:
                    evacuate_got(n + 1, (q + 1) % 2)
                if not fixed or n < MOE_TILES:
                    bias_up(n, q % 2)
                if not fixed or n >= 2:
                    gate_down(n - 2, q % 2, (q + 2) % 4, halves)

            evacuate_got(0, 0)
            whole = MOE_TILES // 4
            for n in range(4):
                slot_of_v(n, n, (n - 2) // 2)
            with v.Fori(1, whole) as r:
                for q in range(4):
                    slot_of_v(r * 4 + q, q, r * 2 + (q - 2) // 2)
            for n in range(4 * whole, MOE_TILES + 2):
                slot_of_v(n, n % 4, (n - 2) // 2)

            def last_sum(b, p, half):
                v.wait_ge(results_back[p], 32 * half + 32)
                v.tensor_tensor(total[p], first[p], base_all[:, bass.ds(b * TB, TB), :], ALU.add).then_inc(add1, 1)
                v.wait_ge(add1, b + 1)
                v.tensor_tensor(total[p], total[p], second[p], ALU.add).then_inc(add2, 1)
                apart(v, setup_vec, (add2, b + 1))
                for t in range(TB):
                    last = v.bn_stats(stats[:, p, t, :], total[p][:, t, :])
                last.then_inc(last_stats, 1)
                apart(v, setup_vec, (last_stats, b + 1))
                for t in range(TB):
                    last = v.bn_aggr(mean_var[:, p, t, :], stats[:, p, t, :])
                last.then_inc(last_aggr, 1)

            def last_norm(b, p, half):
                v.wait_ge(last_rstd, b + 1)
                at_least(v, out_stored[p], 16 * half)
                for t in range(TB):
                    last = normalise(p, t, final[p][:, t, :], total[p][:, t, :])
                last.then_inc(last_done, 1)

            last_sum(0, 0, 0)
            last_sum(1, 1, 0)
            last_norm(0, 0, 0)
            last_sum(2, 0, 1)
            last_norm(1, 1, 0)
            with v.Fori(1, BATCHES // 2 - 1) as pair:
                last_sum(pair * 2 + 1, 1, pair)
                last_norm(pair * 2, 0, pair)
                last_sum(pair * 2 + 2, 0, pair + 1)
                last_norm(pair * 2 + 1, 1, pair)
            half = BATCHES // 2 - 1
            last_sum(BATCHES - 1, 1, half)
            last_norm(BATCHES - 2, 0, half)
            last_norm(BATCHES - 1, 1, half)




def kernel(L0_attn_x, L0_attn_input_weights, L0_attn_xis, L0_attn_proj_matrix, L0_ffn_ln1_w, L0_ffn_ln1_b,
           L0_ffn_ln2_w, L0_ffn_ln2_b, L0_ffn_w_qkv, L0_ffn_b_qkv, L0_ffn_w_o, L0_ffn_b_o, L0_ffn_w_gate,
           L0_ffn_w1, L0_ffn_b1, L0_ffn_w2, L0_ffn_b2):
    import numpy as np
    import concourse.bacc as bacc
    from concourse.bass_utils import run_bass_kernel_spmd

    x = np.asarray(L0_attn_x).reshape(TOKENS, D)
    given = {
        "x": x, "x_t": x.T, "w_in_t": np.asarray(L0_attn_input_weights).T, "xis": L0_attn_xis,
        "proj": L0_attn_proj_matrix, "ln1_w": L0_ffn_ln1_w, "ln1_b": L0_ffn_ln1_b, "ln2_w": L0_ffn_ln2_w,
        "ln2_b": L0_ffn_ln2_b, "w_qkv": L0_ffn_w_qkv, "b_qkv": L0_ffn_b_qkv, "w_o": L0_ffn_w_o,
        "b_o": L0_ffn_b_o, "w_gate": L0_ffn_w_gate, "w1": L0_ffn_w1, "b1": L0_ffn_b1, "w2": L0_ffn_w2,
        "b2": L0_ffn_b2,
    }
    nc = bacc.Bacc("TRN2", target_bir_lowering=False, num_devices=1)
    arrays, args = {}, {}
    for name, a in given.items():
        a = np.ascontiguousarray(a)
        arrays[f"{name}_dram"] = a
        args[name] = nc.dram_tensor(f"{name}_dram", a.shape, mybir.dt.from_np(a.dtype), kind="ExternalInput").ap()
    out = nc.dram_tensor("out_dram", (TOKENS, D), F32, kind="ExternalOutput").ap()
    build(nc, **args, out=out)
    r = run_bass_kernel_spmd(nc, [arrays], core_ids=[0])
    return r.results[0]["out_dram"].reshape(BATCHES, SEQ, D)
```

```python
import math
from contextlib import ExitStack

import concourse.bass as bass
from concourse import mybir

F32 = mybir.dt.float32
F32R = mybir.dt.float32r
BF16 = mybir.dt.bfloat16
I32 = mybir.dt.int32
U32 = mybir.dt.uint32
ACT = mybir.ActivationFunctionType
ALU = mybir.AluOpType
AX = mybir.AxisListType

P = 128
BATCHES, SEQ, D = 16, 256, 128
TILES = BATCHES * SEQ // P
TB = SEQ // P
HEADS, DH = 16, 8
GROUPS, GH = 4, 4
VW = 32
PARTS = 3
PART_ORDER = ((0, 0, 1), (0, 1, 0))
PR = PARTS * DH
PACKS = 1 + GH
EXPERTS, TOPK, HID = 8, 2, 512
HC = HID // P
TOKENS = BATCHES * SEQ
REGION = TOKENS + P
ROW = D + 2
MOE_TILES = (TOKENS * TOPK + EXPERTS * (P - 1)) // P
SPARE = MOE_TILES - TOKENS * TOPK // P
GOT = 8
PUT = 4
EPS = 1e-5
SCALE = 1.0 / math.sqrt(DH)


def at_least(eng, sem, value):
    if isinstance(value, int) and value <= 0:
        return
    eng.wait_ge(sem, value)


def apart(eng, held, *waits):
    if all(isinstance(value, int) for _, value in waits):
        for sem, value in waits:
            at_least(eng, sem, value)
        return
    waits = [(sem, eng.to_reg(value)) for sem, value in waits]
    eng.wait_ge(held, 1)
    for sem, value in waits:
        eng.wait_ge(sem, value)


class Body:

    def __init__(self, i, odd, pair=None):
        self.i, self.odd, self.pair = i, odd, pair
        self.p = 1 if odd else 0
        fixed = isinstance(i, int)
        self.core = not fixed or i < BATCHES
        self.prev = not fixed or 1 <= i <= BATCHES
        self.gate = not fixed or i >= 2
        self.project = not fixed or i + 1 < BATCHES
        self.front = not fixed or i + 2 < BATCHES

    def half(self, k):
        if isinstance(self.i, int):
            return (self.i + k) // 2
        return self.pair + (k + (3 if self.odd else 2)) // 2

    TURNS = ["m3", "ln2", "u2", "gate", "m0", "u3", "rank", "m1", "ctx", "u0", "proj", "m2", "u1"]
    CORE, GATE = ("m0", "m1", "m2", "u0", "u1"), ("ln2", "gate", "rank")

    def turns(self):
        return [n for n in self.TURNS
                if (self.core if n in self.CORE else self.gate if n in self.GATE else self.prev)]

    def turn(self, name):
        if isinstance(self.i, int):
            before = sum(len(Body(i, False).turns()) for i in range(self.i))
        else:
            before = len(Body(0, False).turns()) + len(Body(1, True).turns()) + (self.i - 2) * len(self.TURNS)
        return before + self.turns().index(name)


def run_bodies(eng, emit):
    for i in range(4):
        emit(Body(i, i % 2 == 1))
    with eng.Fori(1, BATCHES // 2 - 2) as pair:
        emit(Body(pair * 2 + 2, False, pair))
        emit(Body(pair * 2 + 3, True, pair))
    for i in range(BATCHES - 2, BATCHES + 2):
        emit(Body(i, i % 2 == 1))


def run_tiles(eng, emit, turns):
    for n in range(GOT):
        emit(n, n, 0)
    with eng.Fori(1, MOE_TILES // GOT) as r:
        for q in range(GOT):
            emit(r * GOT + q, q, r)
    for n in range(MOE_TILES // GOT * GOT, turns):
        emit(n, n % GOT, n // GOT)


def uses(r, q, ring):
    return r * (GOT // ring) + q // ring


def build(nc, x, x_t, w_in_t, xis, proj, ln1_w, ln1_b, ln2_w, ln2_b, w_qkv, b_qkv, w_o, b_o, w_gate,
          w1, b1, w2, b2, out):
    ctx = ExitStack()
    with ctx:
        def sb(name, shape, dt=F32):
            return ctx.enter_context(nc.sbuf_tensor(name, shape, dt))

        def sem(name):
            return ctx.enter_context(nc.semaphore(name))

        ident = sb("ident", [P, P])
        before = sb("before", [P, P], BF16)
        ones_bf = sb("ones_bf", [P, P], BF16)
        zeros = sb("zeros", [P, SEQ])
        eps_col = sb("eps_col", [P, 1])
        xis_col = sb("xis_col", [P, 1])
        neg_half_sq = sb("neg_half_sq", [P, 1])
        feat_bias = sb("feat_bias", [P, 1])
        proj_rd = sb("proj_rd", [P, D])
        scaled_rd = sb("scaled_rd", [P, 2, D])
        scaled_dr = sb("scaled_dr", [P, 2, D])
        w_in_dt = sb("w_in_dt", [P, D])
        w_in_sq = sb("w_in_sq", [P, D])
        w_feat = sb("w_feat", [P, D])
        wqkv_sb = sb("wqkv_sb", [P, 3 * D])
        bqk_col = sb("bqk_col", [P, 2])
        bv_row = sb("bv_row", [P, D])
        wo_sb = sb("wo_sb", [P, D])
        bo_row = sb("bo_row", [P, D])
        wgate_sb = sb("wgate_sb", [P, EXPERTS])
        ln_cols = sb("ln_cols", [P, 4])
        w1_sb = sb("w1_sb", [P, EXPERTS, HID])
        w2_sb = sb("w2_sb", [P, EXPERTS, HC, D])
        b2_sb = sb("b2_sb", [P, EXPERTS, D])
        head_rows = sb("head_rows", [P, GH])
        expert_no = sb("expert_no", [P, EXPERTS])
        upto = sb("upto", [P, EXPERTS, EXPERTS])
        tile_no = sb("tile_no", [P, MOE_TILES])
        result_row = sb("result_row", [P, TB, TOPK])
        pad_rows = sb("pad_rows", [P, EXPERTS + SPARE, ROW])
        pad_no = sb("pad_no", [P, EXPERTS + SPARE])

        x1_all = sb("x1_all", [P, TILES, D])
        base_all = sb("base_all", [P, TILES, D])
        xt_all = sb("xt_all", [P, TOKENS])
        assert EXPERTS * HID == TOKENS
        b1_sb = xt_all[:].rearrange("p (e h) -> p e h", e=EXPERTS)
        xsq = sb("xsq", [P, SEQ])
        feat = sb("feat", [P, SEQ])
        mixed = sb("mixed", [P, TB, D])
        stats = sb("stats", [P, 3, TB, 6])
        mean_var = sb("mean_var", [P, 3, TB, 2])
        log_var = sb("log_var", [P, 4, TB])
        rstd = sb("rstd", [P, 4, TB])
        normed = sb("normed", [P, TB, D])
        normed_t = sb("normed_t", [P, SEQ])
        qk = sb("qk", [P, 2 * SEQ])
        qk_hi = sb("qk_hi", [P, 2 * SEQ], F32R)
        qk_lo = sb("qk_lo", [P, 2 * SEQ], F32R)
        query_pack = [sb(f"query_pack{p}", [P, GROUPS, SEQ], F32R) for p in range(2)]
        key_pack = [sb(f"key_pack{p}", [P, HEADS, SEQ], F32R) for p in range(2)]
        v_ext = [sb(f"v_ext{p}", [P, TB, HEADS, VW]) for p in range(2)]
        row_max = [sb(f"row_max{p}", [P, TB, GH]) for p in range(2)]
        max_parts = sb("max_parts", [P, TB, P])
        probs = sb("probs", [P, 2 * GH, TB, SEQ])
        mixed_v = sb("mixed_v", [P, SEQ])
        inv_sum = sb("inv_sum", [P, TB, GH])
        context = sb("context", [P, TB, D])
        context_t = sb("context_t", [P, SEQ])
        x1_bo = sb("x1_bo", [P, TB, D])
        hidden = sb("hidden", [P, TB, D])
        rows = [sb(f"rows{p}", [P, TB, TOPK, ROW]) for p in range(2)]
        tok_t = sb("tok_t", [P, SEQ])
        logits = sb("logits", [P, TB, EXPERTS])
        top8 = sb("top8", [P, TB, 8])
        top8_at = sb("top8_at", [P, TB, 8], U32)
        top_at = sb("top_at", [P, TB, TOPK])
        chosen = sb("chosen", [P, TB, TOPK, EXPERTS])
        used = sb("used", [P, TB, EXPERTS], BF16)
        below_top = sb("below_top", [P, TB, TOPK])
        gate_exp = sb("gate_exp", [P, TB, TOPK])
        gate_sum = sb("gate_sum", [P, TB])
        gate_inv = sb("gate_inv", [P, TB])
        slot = sb("slot", [P, TB, EXPERTS])
        slot_of = sb("slot_of", [P, TB, TOPK, EXPERTS])
        place = sb("place", [P, TB * TOPK])
        place_i = sb("place_i", [P, TB * TOPK], I32)
        next_row = sb("next_row", [P, EXPERTS])

        tiles_i = sb("tiles_i", [P, EXPERTS], I32)
        counts_f = sb("counts_f", [P, EXPERTS])
        counts_i = sb("counts_i", [P, EXPERTS], I32)
        tiles_f = sb("tiles_f", [P, EXPERTS])
        tiles_upto = sb("tiles_upto", [P, EXPERTS, EXPERTS])
        tile_end = sb("tile_end", [P, EXPERTS])
        gap = sb("gap", [P, EXPERTS])
        past = sb("past", [P, MOE_TILES, EXPERTS])
        past_gap = sb("past_gap", [P, MOE_TILES, EXPERTS])
        tile_expert = sb("tile_expert", [P, MOE_TILES])
        tile_shift = sb("tile_shift", [P, MOE_TILES])
        tile_row = sb("tile_row", [P, MOE_TILES])
        expert_i = sb("expert_i", [P, MOE_TILES], I32)
        row_i = sb("row_i", [P, MOE_TILES], I32)
        pad_at = sb("pad_at", [P, EXPERTS])
        pad_at_i = sb("pad_at_i", [P, EXPERTS], I32)
        got_space = key_pack[0][:].bitcast(F32).rearrange("p h t -> p (h t)")
        got = [got_space[:, n * ROW:(n + 1) * ROW] for n in range(GOT)]
        got_t = [sb(f"got_t{p}", [P, P]) for p in range(2)]
        up = [sb(f"up{p}", [P, HID]) for p in range(2)]
        act = [sb(f"act{p}", [P, HID]) for p in range(2)]
        act_t = [v_ext[p][:].rearrange("p t h e -> p (t h e)")[:, 0:HID] for p in range(2)]
        down = [sb(f"down{p}", [P, D]) for p in range(2)]
        gated = [probs[:, n, 0, 0:D] for n in range(PUT)]
        goes_to = [sb(f"goes_to{p}", [P, 1], I32) for p in range(PUT)]
        first = [probs[:, 4 * p, :, 0:D] for p in range(2)]
        second = [probs[:, 4 * p + 1, :, 0:D] for p in range(2)]
        total = [probs[:, 4 * p + 2, :, 0:D] for p in range(2)]
        final = [probs[:, 4 * p + 3, :, 0:D] for p in range(2)]

        sorted_dram = nc.dram_tensor("sorted_dram", [EXPERTS * REGION + SPARE * P, ROW], F32, kind="Internal").ap()
        result_dram = nc.dram_tensor("result_dram", [TOPK * TOKENS + (EXPERTS + SPARE) * P, D], F32, kind="Internal").ap()

        spill = [nc.dram_tensor(f"spill{p}", [2, HEADS, PARTS, DH, SEQ], F32, kind="Internal").ap() for p in range(2)]

        banks = [ctx.enter_context(nc.psum_tensor(f"bank{i}", [P, 512], F32)) for i in range(8)]
        score_bank, exp_bank = banks[0:2], banks[2:4]
        pv_bank, turn_bank, front_a, front_b = banks[4:8]
        up_bank, act_t_bank, down_bank = banks[0:2], banks[2:4], banks[4:6]
        got_bank = banks[6]

        loaded_small = sem("loaded_small")
        loaded_x0 = sem("loaded_x0")
        loaded_x = sem("loaded_x")
        loaded_moe = sem("loaded_moe")
        pool_zeroed = sem("pool_zeroed")
        pool_consts = sem("pool_consts")
        setup_vec = sem("setup_vec")
        setup_scaled = sem("setup_scaled")
        setup_transposed = sem("setup_transposed")
        setup_evacuated = sem("setup_evacuated")
        setup_sq = sem("setup_sq")
        setup_arg = sem("setup_arg")
        setup_feat = sem("setup_feat")
        keys_zeroed = sem("keys_zeroed")
        stored_pads = sem("stored_pads")
        squared = sem("squared")
        arg_filled, arg_drained = sem("arg_filled"), sem("arg_drained")
        qk_filled, qk_drained = sem("qk_filled"), sem("qk_drained")
        a_filled, a_drained = sem("a_filled"), sem("a_drained")
        stats_done = [sem(f"stats_done{n}") for n in range(3)]
        aggregated = [sem(f"aggregated{n}") for n in range(3)]
        logged = [sem(f"logged{n}") for n in range(3)]
        rstd_done = [sem(f"rstd_done{n}") for n in range(3)]
        x1_done = sem("x1_done")
        normed_done = sem("normed_done")
        split_done = sem("split_done")
        spilled = [sem(f"spilled{p}") for p in range(2)]
        packed = [sem(f"packed{p}") for p in range(2)]
        scores_filled, scores_drained = sem("scores_filled"), sem("scores_drained")
        max_hi, max_lo = sem("max_hi"), sem("max_lo")
        turn_filled, turn_drained = sem("turn_filled"), sem("turn_drained")
        keyed_filled = sem("keyed_filled")
        exp_done = sem("exp_done")
        pv_filled, pv_evacuated = sem("pv_filled"), sem("pv_evacuated")
        inverted = sem("inverted")
        x1_bo_done = sem("x1_bo_done")
        base_done = sem("base_done")
        token_row = sem("token_row")
        copied_row = sem("copied_row")
        counted_row = sem("counted_row")
        logits_done = sem("logits_done")
        top_done, top_at_done, top_at_f = sem("top_done"), sem("top_at_done"), sem("top_at_f")
        chosen_done, used_done = sem("chosen_done"), sem("used_done")
        below_done, gate_exp_done, gate_sum_done = sem("below_done"), sem("gate_exp_done"), sem("gate_sum_done")
        gate_inv_done, gate_done = sem("gate_inv_done"), sem("gate_done")
        slot_done, slot_of_done, place_done, placed = sem("slot_done"), sem("slot_of_done"), sem("place_done"), sem("placed")
        scattered = sem("scattered")
        table = sem("table")
        table_ready = sem("table_ready")
        pads_placed = sem("pads_placed")
        got_loaded = [sem(f"got_loaded{p}") for p in range(GOT)]
        got_turned, got_t_done = sem("got_turned"), sem("got_t_done")
        up_filled, up_drained = sem("up_filled"), sem("up_drained")
        act_done = sem("act_done")
        act_turned, act_t_done = sem("act_turned"), sem("act_t_done")
        down_filled, down_drained = sem("down_filled"), sem("down_drained")
        gated_done = sem("gated_done")
        goes_done = sem("goes_done")
        result_stored = [sem(f"result_stored{p}") for p in range(PUT)]
        results_back = [sem(f"results_back{p}") for p in range(2)]
        add1, add2, last_stats, last_aggr = sem("add1"), sem("add2"), sem("last_stats"), sem("last_aggr")
        last_log, last_rstd, last_done = sem("last_log"), sem("last_rstd"), sem("last_done")
        out_stored = [sem(f"out_stored{p}") for p in range(2)]

        SMALL = 14
        x_v = x.rearrange("(t p) d -> p t d", p=P)
        out_v = out.rearrange("(t p) d -> p t d", p=P)
        FIRST_TILES = 4 * TB

        block = ctx.enter_context(nc.Block())

        @block.sync
        def _(sp):
            def column(v):
                return v.rearrange("(p o) -> p o", o=1)

            def broadcast(v):
                return v.rearrange("(o n) -> o n", o=1).broadcast_to([P, v.shape[0]])

            for dst, src in (
                (xis_col[:], column(xis)), (proj_rd[:], proj), (w_in_dt[:], w_in_t),
                (wqkv_sb[:], w_qkv), (wo_sb[:], w_o), (wgate_sb[:], w_gate),
                (ln_cols[:, 0:1], column(ln1_w)), (ln_cols[:, 1:2], column(ln1_b)),
                (ln_cols[:, 2:3], column(ln2_w)), (ln_cols[:, 3:4], column(ln2_b)),
                (bqk_col[:, 0:1], column(b_qkv[0:D])), (bqk_col[:, 1:2], column(b_qkv[D:2 * D])),
                (bv_row[:], broadcast(b_qkv[2 * D:3 * D])), (bo_row[:], broadcast(b_o)),
            ):
                sp.dma_start(dst, src).then_inc(loaded_small, 16)
            sp.dma_start(xt_all[:, 0:FIRST_TILES * P], x_t[:, 0:FIRST_TILES * P]).then_inc(loaded_x0, 16)
            sp.dma_start(x1_all[:, 0:FIRST_TILES, :], x_v[:, 0:FIRST_TILES, :]).then_inc(loaded_x0, 16)
            sp.dma_start(xt_all[:, FIRST_TILES * P:], x_t[:, FIRST_TILES * P:]).then_inc(loaded_x, 16)
            sp.dma_start(x1_all[:, FIRST_TILES:, :], x_v[:, FIRST_TILES:, :]).then_inc(loaded_x, 16)

            def pack(b, p, half):
                keyed_before, spills, reads, batches = (b - 1) * HEADS, (half + 1) * 16 * 2 * PARTS, half * 16 * PACKS, b + 1
                if not isinstance(b, int):
                    keyed_before, spills, reads, batches = [sp.to_reg(n) for n in (keyed_before, spills, reads, batches)]
                at_least(sp, packed[p], reads)
                for low, part, ready in ((0, qk_hi, qk_drained), (1, qk_lo, split_done)):
                    sp.wait_ge(ready, batches)
                    for n, orders in enumerate(PART_ORDER):
                        for c, lo in enumerate(orders):
                            if lo == low:
                                sp.dma_start(spill[p][n, :, c],
                                             part[:, n * SEQ:(n + 1) * SEQ].bitcast(F32)).then_inc(spilled[p], 16)
                sp.wait_ge(spilled[p], spills)
                at_least(sp, keyed_filled, keyed_before)
                sp.dma_start(query_pack[p][0:GH * PR, :, :].bitcast(F32),
                             spill[p][0].rearrange("(g j) c e t -> (j c e) g t", g=GROUPS)).then_inc(packed[p], 16)
                for j in range(GH):
                    sp.dma_start(key_pack[p][PR * j:PR * j + PR, :, :].bitcast(F32).rearrange("r (g j) t -> r g j t", j=GH)[:, :, j, :],
                                 spill[p][1].rearrange("(g j) c e t -> j (c e) g t", j=GH)[j]).then_inc(packed[p], 16)

            sp.wait_ge(keys_zeroed, 4)
            pack(0, 0, 0)

            def emit(body):
                if body.project:
                    pack(body.i + 1, 1 - body.p, body.half(1))

            run_bodies(sp, emit)

            sp.wait_ge(scattered, 16 * TB * TOPK * BATCHES)
            sp.wait_ge(pads_placed, 16 * EXPERTS)
            sp.wait_ge(stored_pads, 16 * SPARE)
            sp.wait_ge(table_ready, 1)

            def load_tile(n, q, r):
                row = sp.value_load(row_i[0:1, bass.ds(n, 1)], min_val=0, max_val=EXPERTS * REGION + (SPARE - 1) * P)
                at_least(sp, gated_done, n - GOT + 1)
                at_least(sp, goes_done, n - GOT + 1)
                sp.dma_start(got[q], sorted_dram[bass.ds(row, P), :]).then_inc(got_loaded[q], 16)

            run_tiles(sp, load_tile, MOE_TILES)

            for p in range(PUT):
                sp.wait_ge(result_stored[p], 16 * ((MOE_TILES + PUT - 1 - p) // PUT))

            def results(b, p, half):
                at_least(sp, add2, b - 1)
                r_v = result_dram[0:TOPK * TOKENS, :].rearrange("(s t p) d -> s p t d", s=TOPK, p=P)
                sp.dma_start(first[p], r_v[0][:, bass.ds(b * TB, TB), :]).then_inc(results_back[p], 16)
                sp.dma_start(second[p], r_v[1][:, bass.ds(b * TB, TB), :]).then_inc(results_back[p], 16)

            def store(b, p):
                sp.wait_ge(last_done, b + 1)
                sp.dma_start(out_v[:, bass.ds(b * TB, TB), :], final[p]).then_inc(out_stored[p], 16)

            results(0, 0, 0)
            results(1, 1, 0)
            with sp.Fori(0, BATCHES // 2 - 1) as pair:
                for p in range(2):
                    store(pair * 2 + p, p)
                    results(pair * 2 + 2 + p, p, pair + 1)
            for p in range(2):
                store(BATCHES - 2 + p, p)
            for p in range(2):
                sp.wait_ge(out_stored[p], 16 * BATCHES // 2)

        @block.gpsimd
        def _(pool):
            for buf, value in ((ident, 0.0), (before, 1.0), (head_rows, 1.0), (upto, 1.0), (pad_rows, 0.0)):
                pool.memset(buf[:], value).then_inc(pool_zeroed, 1)
            pool.wait_ge(pool_zeroed, 5)
            pool.affine_select(out=ident[:], in_=ident[:], compare_op=ALU.not_equal, fill=1.0, base=0,
                               pattern=[[-1, P]], channel_multiplier=1).then_inc(pool_consts, 1)
            pool.affine_select(out=before[:], in_=before[:], compare_op=ALU.is_gt, fill=0.0, base=0,
                               pattern=[[1, P]], channel_multiplier=-1).then_inc(pool_consts, 1)
            pool.affine_select(out=upto[:], in_=upto[:], compare_op=ALU.is_ge, fill=0.0, base=0,
                               pattern=[[1, EXPERTS], [-1, EXPERTS]], channel_multiplier=0).then_inc(pool_consts, 1)
            pool.affine_select(out=head_rows[:], in_=head_rows[:], compare_op=ALU.is_ge, fill=0.0, base=-96,
                               pattern=[[-2, GH]], channel_multiplier=1).then_inc(pool_consts, 1)
            pool.wait_ge(pool_consts, 4)
            pool.affine_select(out=head_rows[:], in_=head_rows[:], compare_op=ALU.is_ge, fill=0.0, base=97,
                               pattern=[[2, GH]], channel_multiplier=-1).then_inc(pool_consts, 1)
            iota = dict(allow_small_or_imprecise_dtypes=True)
            pool.iota(expert_no[:], pattern=[[1, EXPERTS]], base=0, channel_multiplier=0, **iota).then_inc(pool_consts, 1)
            pool.iota(tile_no[:], pattern=[[1, MOE_TILES]], base=0, channel_multiplier=0, **iota).then_inc(pool_consts, 1)
            pool.iota(next_row[:], pattern=[[REGION, EXPERTS]], base=0, channel_multiplier=0, **iota).then_inc(pool_consts, 1)
            pool.iota(result_row[:], pattern=[[P, TB], [TOKENS, TOPK]], base=0, channel_multiplier=1, **iota).then_inc(pool_consts, 1)
            pool.iota(pad_no[:], pattern=[[P, EXPERTS + SPARE]], base=TOPK * TOKENS, channel_multiplier=1, **iota).then_inc(pool_consts, 1)
            pool.iota(pad_at[:], pattern=[[0, EXPERTS]], base=0, channel_multiplier=1, **iota).then_inc(pool_consts, 1)
            pool.wait_ge(pool_consts, 11)
            pool.tensor_copy(pad_rows[:, :, ROW - 1], pad_no[:]).then_inc(pool_consts, 1)
            pool.wait_ge(pool_consts, 12)
            for k in range(SPARE):
                at = EXPERTS * REGION + k * P
                pool.dma_start(sorted_dram[at:at + P, :], pad_rows[:, EXPERTS + k, :]).then_inc(stored_pads, 16)
            pool.wait_ge(setup_evacuated, 1)
            pool.tensor_tensor(w_in_sq[:], w_in_dt[:], w_in_dt[:], ALU.mult).then_inc(setup_sq, 1)

            def square(b):
                at_least(pool, arg_filled, b)
                pool.tensor_tensor(xsq[:], xt_all[:, bass.ds(b * SEQ, SEQ)], xt_all[:, bass.ds(b * SEQ, SEQ)],
                                   ALU.mult).then_inc(squared, 1)

            pool.wait_ge(loaded_x0, 32)
            square(0)
            square(1)
            pool.wait_ge(loaded_x, 32)

            def residuals(body):
                b = body.i - 1
                at_least(pool, base_done, b)
                pool.wait_ge(x1_done, b + 1)
                pool.tensor_tensor(x1_bo[:], x1_all[:, bass.ds(b * TB, TB), :],
                                   bo_row[:].unsqueeze(1).broadcast_to([P, TB, D]), ALU.add).then_inc(x1_bo_done, 1)

            def base(body):
                tiles = bass.ds((body.i - 1) * TB, TB)
                pool.wait_ge(turn_drained, body.turn("proj") + 1)
                pool.tensor_tensor(base_all[:, tiles, :], hidden[:], x1_all[:, tiles, :], ALU.add).then_inc(base_done, 1)

            def third_norm(body):
                b = body.i - 1
                apart(pool, pool_consts, (rstd_done[2], b + 1),
                      (scattered, (b - 1) * (16 * TB * TOPK)))
                for t in range(TB):
                    last = pool.tensor_scalar(rows[1 - body.p][:, t, 0, 0:D], hidden[:, t, :],
                                              mean_var[:, 2, t, 0:1], rstd[:, 2, t:t + 1], ALU.subtract, ALU.mult)
                last.then_inc(token_row, 1)

            def low_parts(b):
                pool.wait_ge(qk_drained, b + 1)
                pool.tensor_tensor(qk_lo[:], qk[:], qk_hi[:].bitcast(F32), ALU.subtract).then_inc(split_done, 1)

            def copy_rows(body):
                b, mine = body.i - 2, rows[body.p]
                apart(pool, pool_consts, (token_row, b + 1))
                pool.tensor_copy(mine[:, :, 1, 0:D], mine[:, :, 0, 0:D]).then_inc(copied_row, 1)
                apart(pool, pool_consts, (counted_row, b))
                pool.tensor_copy(mine[:, :, :, ROW - 1], result_row[:]).then_inc(copied_row, 1)
                apart(pool, pool_consts, (copied_row, 2 * b + 2))
                pool.tensor_scalar(result_row[:], result_row[:], float(SEQ), None, ALU.add).then_inc(counted_row, 1)

            def scatter(body):
                b = body.i - 2
                apart(pool, pool_consts, (gate_done, b + 1), (placed, b + 1))
                for t in range(TB):
                    for s in range(TOPK):
                        n = t * TOPK + s
                        pool.indirect_dma_start(
                            out=sorted_dram, out_offset=bass.IndirectOffsetOnAxis(ap=place_i[:, n:n + 1], axis=0),
                            in_=rows[body.p][:, t, s, :], in_offset=None).then_inc(scattered, 16)

            def emit(body):
                if body.front:
                    square(body.i + 2)
                if body.gate:
                    copy_rows(body)
                if body.prev:
                    residuals(body)
                if body.project:
                    low_parts(body.i + 1)
                if body.gate:
                    scatter(body)
                if body.prev:
                    base(body)
                if body.prev:
                    third_norm(body)

            low_parts(0)
            run_bodies(pool, emit)

            pool.wait_ge(table_ready, 1)
            for e in range(EXPERTS):
                pool.indirect_dma_start(
                    out=sorted_dram, out_offset=bass.IndirectOffsetOnAxis(ap=pad_at_i[:, e:e + 1], axis=0),
                    in_=pad_rows[:, e, :], in_offset=None).then_inc(pads_placed, 16)

            def put(n, q, r):
                p = q % PUT
                apart(pool, pool_consts, (got_loaded[q], uses(r, q, GOT) * 16 + 16), (result_stored[p], uses(r, q, PUT) * 16))
                pool.tensor_copy(goes_to[p][:], got[q][:, ROW - 1:ROW]).then_inc(goes_done, 1)
                apart(pool, pool_consts, (goes_done, n + 1), (gated_done, n + 1))
                pool.indirect_dma_start(
                    out=result_dram, out_offset=bass.IndirectOffsetOnAxis(ap=goes_to[p][:, 0:1], axis=0),
                    in_=gated[p], in_offset=None).then_inc(result_stored[p], 16)

            run_tiles(pool, put, MOE_TILES)

        @block.tensor
        def _(pe):
            pe.wait_ge(pool_consts, 1)
            pe.wait_ge(setup_scaled, 2)
            for n in range(2):
                last = pe.transpose(score_bank[0][:, n * D:(n + 1) * D], scaled_rd[:, n, :], ident[:])
            last.then_inc(setup_transposed, 1)
            pe.wait_ge(setup_evacuated, 1)
            pe.wait_ge(setup_sq, 1)
            pe.matmul(score_bank[1][:, 0:D], scaled_dr[:, 0, :], w_in_dt[:], start=True, stop=False)
            pe.matmul(score_bank[1][:, 0:D], scaled_dr[:, 1, :], w_in_sq[:], start=False, stop=True).then_inc(setup_arg, 1)

            def features(b, qk_before):
                pe.wait_ge(squared, b + 1)
                at_least(pe, qk_drained, qk_before)
                pe.matmul(front_b[:, 0:SEQ], scaled_dr[:, 0, :], xt_all[:, bass.ds(b * SEQ, SEQ)], start=True, stop=False)
                pe.matmul(front_b[:, 0:SEQ], scaled_dr[:, 1, :], xsq[:], start=False, stop=True).then_inc(arg_filled, 1)

            def mix(b):
                pe.wait_ge(arg_drained, b + 1)
                at_least(pe, a_drained, 3 * b)
                for t in range(TB):
                    last = pe.matmul(front_a[:, t * D:(t + 1) * D], feat[:, t * P:(t + 1) * P], w_feat[:], start=True, stop=True)
                last.then_inc(a_filled, 1)

            def turn_normed(b):
                pe.wait_ge(normed_done, b + 1)
                pe.wait_ge(a_drained, 3 * b + 1)
                for t in range(TB):
                    last = pe.transpose(front_a[:, t * P:(t + 1) * P], normed[:, t, :], ident[:])
                last.then_inc(a_filled, 1)

            def project_qk(b, args_before):
                pe.wait_ge(a_drained, 3 * b + 2)
                pe.wait_ge(arg_drained, args_before)
                for n in range(2):
                    last = pe.matmul(front_b[:, n * SEQ:(n + 1) * SEQ], wqkv_sb[:, n * D:(n + 1) * D], normed_t[:],
                                     start=True, stop=True)
                last.then_inc(qk_filled, 1)

            def project_v(b):
                pe.wait_ge(a_drained, 3 * b + 2)
                for t in range(TB):
                    last = pe.matmul(front_a[:, t * D:(t + 1) * D], normed_t[:, t * P:(t + 1) * P],
                                     wqkv_sb[:, 2 * D:3 * D], start=True, stop=True)
                last.then_inc(a_filled, 1)

            pe.wait_ge(setup_feat, 1)
            pe.wait_ge(loaded_small, 16 * SMALL)
            features(0, 0)
            mix(0)
            turn_normed(0)
            project_qk(0, 1)
            project_v(0)
            features(1, 1)
            mix(1)

            def scores(body, g, u):
                group = body.i * GROUPS + g
                qt, pair = u // 2, u % 2
                if g == 0 and u == 0:
                    pe.wait_ge(packed[body.p], (body.half(0) + 1) * 16 * PACKS)
                at_least(pe, scores_drained, group * 4 + u - 1)
                h = GH * g + 2 * pair
                pe.matmul(score_bank[u % 2][:, :], query_pack[body.p][0:96, g, qt * P:(qt + 1) * P],
                          key_pack[body.p][0:96, h:h + 2, :], start=True, stop=True).then_inc(scores_filled, 1)

            def turn_max(body, name, group):
                pe.wait_ge(max_lo, group + 1)
                at_least(pe, turn_drained, body.turn(name))
                for t in range(TB):
                    last = pe.transpose(turn_bank[:, t * P:(t + 1) * P], max_parts[:, t, :], ident[:])
                last.then_inc(turn_filled, 1)

            def keyed(body, g, j, m_name):
                group = body.i * GROUPS + g - 1
                p, gg = (body.p, g - 1) if g else (1 - body.p, GROUPS - 1)
                if j == 0:
                    pe.wait_ge(turn_drained, body.turn(m_name) + 1)
                at_least(pe, exp_done, group * GH + j - 1)
                for kt in range(TB):
                    last = pe.matmul(exp_bank[j % 2][:, kt * SEQ:(kt + 1) * SEQ],
                                     key_pack[p][:, GH * gg + j, kt * P:(kt + 1) * P], query_pack[p][:, gg, :],
                                     start=True, stop=True)
                last.then_inc(keyed_filled, 1)

            def values(body, g):
                group = body.i * GROUPS + g - 2
                p, gg, b = (body.p, g - 2, body.i) if g >= 2 else (1 - body.p, g + 2, body.i - 1)
                pe.wait_ge(exp_done, group * GH + GH)
                at_least(pe, pv_evacuated, group)
                pe.wait_ge(a_drained, 3 * b + 3)
                for kt in range(TB):
                    for j in range(GH):
                        last = pe.matmul(pv_bank[VW * j:VW * j + VW, 0:SEQ], v_ext[p][:, kt, GH * gg + j, :],
                                         probs[:, GH * (gg % 2) + j, kt, :], start=kt == 0, stop=kt == TB - 1,
                                         tile_position=(0, VW * j))
                last.then_inc(pv_filled, 1)

            def turn_values(body, name, g):
                group = body.i * GROUPS + g - 2
                pe.wait_ge(pv_evacuated, group + 1)
                at_least(pe, turn_drained, body.turn(name))
                for t in range(TB):
                    last = pe.transpose(turn_bank[:, t * P:(t + 1) * P], mixed_v[:, t * P:(t + 1) * P], ident[:])
                last.then_inc(turn_filled, 1)

            def turn_context(body):
                pe.wait_ge(turn_drained, body.turn("ctx"))
                for t in range(TB):
                    last = pe.transpose(turn_bank[:, t * P:(t + 1) * P], context[:, t, :], ident[:])
                last.then_inc(turn_filled, 1)

            def project_out(body):
                pe.wait_ge(turn_drained, body.turn("proj"))
                for t in range(TB):
                    last = pe.matmul(turn_bank[:, t * D:(t + 1) * D], context_t[:, t * P:(t + 1) * P], wo_sb[:],
                                     start=True, stop=True)
                last.then_inc(turn_filled, 1)

            def turn_tokens(body):
                pe.wait_ge(token_row, body.i - 1)
                pe.wait_ge(turn_drained, body.turn("ln2"))
                for t in range(TB):
                    last = pe.transpose(turn_bank[:, t * P:(t + 1) * P], rows[body.p][:, t, 0, 0:D], ident[:])
                last.then_inc(turn_filled, 1)

            def gate_logits(body):
                pe.wait_ge(turn_drained, body.turn("gate"))
                for t in range(TB):
                    last = pe.matmul(turn_bank[:, t * EXPERTS:(t + 1) * EXPERTS], tok_t[:, t * P:(t + 1) * P], wgate_sb[:],
                                     start=True, stop=True)
                last.then_inc(turn_filled, 1)

            def ranks(body):
                pe.wait_ge(used_done, body.i - 1)
                pe.wait_ge(turn_drained, body.turn("rank"))
                e = EXPERTS
                pe.matmul(turn_bank[:, 0:e], before[:], used[:, 0, :], start=True, stop=True)
                pe.matmul(turn_bank[:, e:2 * e], before[:], used[:, 1, :], start=True, stop=False)
                pe.matmul(turn_bank[:, e:2 * e], ones_bf[:], used[:, 0, :], start=False, stop=True)
                pe.matmul(turn_bank[:, 2 * e:3 * e], ones_bf[:], used[:, 0, :], start=True, stop=False)
                pe.matmul(turn_bank[:, 2 * e:3 * e], ones_bf[:], used[:, 1, :], start=False, stop=True).then_inc(turn_filled, 1)

            def emit(body):
                for g in range(GROUPS):
                    m_name = ("m3", "m0", "m1", "m2")[g]
                    u_name = ("u2", "u3", "u0", "u1")[g]
                    has_m = (g > 0 and body.core) or (g == 0 and body.prev)
                    has_u = (g >= 2 and body.core) or (g < 2 and body.prev)
                    if body.core and g == 0:
                        scores(body, g, 0)
                        scores(body, g, 1)
                    if has_m:
                        turn_max(body, m_name, body.i * GROUPS + g - 1)
                    if has_u:
                        values(body, g)
                    if body.core:
                        scores(body, g, 2)
                    if has_m:
                        keyed(body, g, 0, m_name)
                    if body.core:
                        scores(body, g, 3)
                    if has_m:
                        keyed(body, g, 1, m_name)
                    if g == 0:
                        if body.project:
                            turn_normed(body.i + 1)
                        if body.gate:
                            turn_tokens(body)
                        if body.front:
                            features(body.i + 2, body.i + 1)
                    if g == 1 and body.project:
                        project_v(body.i + 1)
                    if g == 2 and body.prev:
                        turn_context(body)
                    if has_m:
                        keyed(body, g, 2, m_name)
                    if body.core and g + 1 < GROUPS:
                        scores(body, g + 1, 0)
                    if has_u:
                        turn_values(body, u_name, g)
                    if has_m:
                        keyed(body, g, 3, m_name)
                    if body.core and g + 1 < GROUPS:
                        scores(body, g + 1, 1)
                    if g == 0:
                        if body.project:
                            project_qk(body.i + 1, body.i + 3 if body.front else BATCHES)
                        if body.gate:
                            gate_logits(body)
                    if g == 1:
                        if body.front:
                            mix(body.i + 2)
                        if body.gate:
                            ranks(body)
                    if g == 2 and body.prev:
                        project_out(body)

            run_bodies(pe, emit)

            pe.wait_ge(table_ready, 1)
            pe.wait_ge(loaded_moe, 16 * 4)

            def expert_of(n):
                return pe.value_load(expert_i[0:1, bass.ds(n, 1)], min_val=0, max_val=EXPERTS - 1)

            def turn_got(n, q, r):
                pe.wait_ge(got_loaded[q % GOT], uses(r, q, GOT) * 16 + 16)
                at_least(pe, got_t_done, n)
                pe.transpose(got_bank[:, 0:P], got[q % GOT][:, 0:D], ident[:]).then_inc(got_turned, 1)

            def go_up(n, p):
                e = expert_of(n)
                pe.wait_ge(got_t_done, n + 1)
                at_least(pe, up_drained, n - 1)
                pe.matmul(up_bank[p][:, :], got_t[p][:], w1_sb[:, bass.ds(e, 1), :], start=True, stop=True).then_inc(up_filled, 1)

            def turn_act(n, p):
                pe.wait_ge(act_done, n + 1)
                at_least(pe, act_t_done, n - 1)
                for c in range(HC):
                    last = pe.transpose(act_t_bank[p][:, c * P:(c + 1) * P], act[p][:, c * P:(c + 1) * P], ident[:])
                last.then_inc(act_turned, 1)

            def go_down(n, p):
                e = expert_of(n)
                pe.wait_ge(act_t_done, n + 1)
                at_least(pe, down_drained, n - 1)
                for c in range(HC):
                    last = pe.matmul(down_bank[p][:, 0:D], act_t[p][:, c * P:(c + 1) * P], w2_sb[:, bass.ds(e, 1), c, :],
                                     start=c == 0, stop=c == HC - 1)
                last.then_inc(down_filled, 1)

            def slot_of_pe(n, q, r):
                fixed = isinstance(n, int)
                if not fixed or n < MOE_TILES:
                    go_up(n, q % 2)
                if not fixed or n + 1 < MOE_TILES:
                    turn_got(n + 1, q + 1, r)
                if not fixed or n >= 2:
                    go_down(n - 2, q % 2)
                if (not fixed or n >= 1) and (not fixed or n <= MOE_TILES):
                    turn_act(n - 1, (q + 1) % 2)

            turn_got(0, 0, 0)
            run_tiles(pe, slot_of_pe, MOE_TILES + 2)

        @block.scalar
        def _(a):
            a.preload_act_table_set("natural_log_exp_and_others")
            a.dma_start(w1_sb[:], w1.rearrange("e d h -> d e h")).then_inc(loaded_moe, 16)
            a.dma_start(w2_sb[:], w2.rearrange("e (c p) d -> p e c d", p=P)).then_inc(loaded_moe, 16)
            a.dma_start(b2_sb[:], b2.rearrange("(o e) d -> o e d", o=1).broadcast_to([P, EXPERTS, D])).then_inc(loaded_moe, 16)
            a.wait_ge(setup_arg, 1)
            a.activation(w_feat[:], score_bank[1][:, 0:D], ACT.Exp, bias=feat_bias[:, 0:1]).then_inc(setup_feat, 1)

            def feature_exp(b):
                a.wait_ge(arg_filled, b + 1)
                at_least(a, a_filled, 3 * (b - 1) + 1)
                a.activation(feat[:], front_b[:, 0:SEQ], ACT.Exp, bias=feat_bias[:, 0:1]).then_inc(arg_drained, 1)

            def inverse_std(n, b):
                a.wait_ge(aggregated[n], b + 1)
                a.activation(log_var[:, n, :], mean_var[:, n, :, 1], ACT.Ln, bias=eps_col[:, 0:1]).then_inc(logged[n], 1)
                a.wait_ge(logged[n], b + 1)
                a.activation(rstd[:, n, :], log_var[:, n, :], ACT.Exp, scale=-0.5).then_inc(rstd_done[n], 1)

            def bias_qk(b, k, p_before, half_before):
                n, rounded = k // 2, k % 2
                part = slice(n * SEQ, (n + 1) * SEQ)
                if k == 0:
                    a.wait_ge(qk_filled, b + 1)
                    at_least(a, split_done, b)
                    at_least(a, packed[p_before], half_before * 16 * PACKS)
                last = a.activation((qk_hi if rounded else qk)[:, part], front_b[:, part], ACT.Identity, bias=bqk_col[:, n:n + 1])
                if k == 3:
                    last.then_inc(qk_drained, 1)

            def evacuate_normed(b):
                a.wait_ge(a_filled, 3 * b + 2)
                a.activation(normed_t[:], front_a[:, 0:SEQ], ACT.Identity, bias=ln_cols[:, 1:2], scale=ln_cols[:, 0:1]).then_inc(a_drained, 1)

            def evacuate_tokens(body):
                a.wait_ge(turn_filled, body.turn("ln2") + 1)
                a.activation(tok_t[:], turn_bank[:, 0:SEQ], ACT.Identity, bias=ln_cols[:, 3:4], scale=ln_cols[:, 2:3]).then_inc(turn_drained, 1)

            a.wait_ge(setup_vec, 4)
            a.wait_ge(loaded_small, 16 * SMALL)
            feature_exp(0)
            inverse_std(0, 0)
            inverse_std(1, 0)
            evacuate_normed(0)
            for k in range(4):
                bias_qk(0, k, 0, 0)
            feature_exp(1)
            inverse_std(0, 1)
            inverse_std(1, 1)

            def place_max(body, g, name):
                p, gg = (body.p, g - 1) if g else (1 - body.p, GROUPS - 1)
                a.wait_ge(turn_filled, body.turn(name) + 1)
                a.activation(query_pack[p][96:P, gg, :], turn_bank[96:P, 0:SEQ], ACT.Copy).then_inc(turn_drained, 1)

            def evacuate_values(body, g, before_name):
                group = body.i * GROUPS + g - 2
                a.wait_ge(pv_filled, group + 1)
                if before_name:
                    a.wait_ge(turn_filled, body.turn(before_name) + 1)
                a.activation(mixed_v[:], pv_bank[:, 0:SEQ], ACT.Copy).then_inc(pv_evacuated, 1)

            def exponential(body, g, j):
                group = body.i * GROUPS + g - 1
                a.wait_ge(keyed_filled, group * GH + j + 1)
                if j == 0:
                    at_least(a, pv_filled, group - 1)
                a.activation(probs[:, GH * ((g + 1) % 2) + j, :, :], exp_bank[j % 2][:, :], ACT.Exp,
                             scale=SCALE).then_inc(exp_done, 1)

            def emit(body):
                if isinstance(body.i, int) and body.i == BATCHES - 2:
                    a.wait_ge(arg_filled, BATCHES)
                    a.dma_start(b1_sb, b1.rearrange("(o e) h -> o e h", o=1).broadcast_to([P, EXPERTS, HID])).then_inc(loaded_moe, 16)
                for g in range(GROUPS):
                    has_m = (g > 0 and body.core) or (g == 0 and body.prev)
                    has_u = (g >= 2 and body.core) or (g < 2 and body.prev)
                    if has_m:
                        place_max(body, g, ("m3", "m0", "m1", "m2")[g])
                    if g == 1 and body.project:
                        for k in range(2):
                            bias_qk(body.i + 1, k, body.p, body.half(0) + 1)
                    if has_u:
                        before_name = ("m3", "u2", "u3" if body.prev else None, "u0")[g]
                        evacuate_values(body, g, before_name)
                    if g == 1 and body.project:
                        bias_qk(body.i + 1, 2, body.p, body.half(0) + 1)
                    if body.front and g >= 2:
                        inverse_std(g - 2, body.i + 2)
                    if has_m:
                        exponential(body, g, 0)
                        exponential(body, g, 1)
                    if g == 0:
                        if body.project:
                            evacuate_normed(body.i + 1)
                        if body.gate:
                            evacuate_tokens(body)
                    if g == 1 and body.project:
                        bias_qk(body.i + 1, 3, body.p, body.half(0) + 1)
                    if g == 2 and body.prev:
                        a.wait_ge(turn_filled, body.turn("ctx") + 1)
                        a.activation(context_t[:], turn_bank[:, 0:SEQ], ACT.Copy).then_inc(turn_drained, 1)
                    if g == 3 and body.prev:
                        inverse_std(2, body.i - 1)
                    if has_m:
                        exponential(body, g, 2)
                    if g == 0 and body.front:
                        feature_exp(body.i + 2)
                    if has_m:
                        exponential(body, g, 3)
                    if g == 1 and body.gate:
                        a.wait_ge(below_done, body.i - 1)
                        a.activation(gate_exp[:], below_top[:], ACT.Exp).then_inc(gate_exp_done, 1)

            run_bodies(a, emit)

            def tile_act(n, p):
                a.wait_ge(up_drained, n + 1)
                at_least(a, act_turned, n - 1)
                a.activation(act[p][:], up[p][:], ACT.Gelu_apprx_tanh).then_inc(act_done, 1)

            def tile_act_t(n, p):
                a.wait_ge(act_turned, n + 1)
                at_least(a, down_filled, n - 1)
                a.activation(act_t[p], act_t_bank[p][:, :], ACT.Copy).then_inc(act_t_done, 1)

            tile_act(0, 0)
            tile_act(1, 1)
            tile_act_t(0, 0)
            tile_act(2, 0)
            tile_act_t(1, 1)
            with a.Fori(1, (MOE_TILES - 1) // 2) as pair:
                tile_act(pair * 2 + 1, 1)
                tile_act_t(pair * 2, 0)
                tile_act(pair * 2 + 2, 0)
                tile_act_t(pair * 2 + 1, 1)
            tile_act_t(MOE_TILES - 1, 0)

            a.preload_act_table_set("natural_log_exp_and_others")

            def last_inverse(b, p):
                a.wait_ge(last_aggr, b + 1)
                a.activation(log_var[:, p, :], mean_var[:, p, :, 1], ACT.Ln, bias=eps_col[:, 0:1]).then_inc(last_log, 1)
                a.wait_ge(last_log, b + 1)
                a.activation(rstd[:, p, :], log_var[:, p, :], ACT.Exp, scale=-0.5).then_inc(last_rstd, 1)

            with a.Fori(0, BATCHES // 2) as pair:
                last_inverse(pair * 2, 0)
                last_inverse(pair * 2 + 1, 1)

        @block.vector
        def _(v):
            v.memset(zeros[:], 0.0).then_inc(setup_vec, 1)
            v.memset(eps_col[:], EPS).then_inc(setup_vec, 1)
            v.memset(ones_bf[:], 1.0).then_inc(setup_vec, 1)
            for p in range(2):
                v.memset(v_ext[p][:], 0.0)
            v.memset(max_parts[:], 0.0)
            v.wait_ge(loaded_small, 16 * SMALL)
            v.tensor_scalar(feat_bias[:], xis_col[:], -0.5 * math.log(D), None, ALU.add).then_inc(setup_vec, 1)
            v.tensor_tensor(neg_half_sq[:], xis_col[:], xis_col[:], ALU.mult).then_inc(setup_vec, 1)
            v.wait_ge(setup_vec, 5)
            for p in range(2):
                v.memset(v_ext[p][:, :, :, DH:DH + 1], 1.0)
            v.tensor_scalar(scaled_rd[:, 0, :], proj_rd[:], xis_col[:, 0:1], None, ALU.mult).then_inc(setup_scaled, 1)
            v.tensor_scalar(scaled_rd[:, 1, :], zeros[:, 0:D], neg_half_sq[:, 0:1], -0.5, ALU.add, ALU.mult).then_inc(setup_scaled, 1)
            v.wait_ge(setup_transposed, 1)
            v.tensor_copy(scaled_dr[:], score_bank[0][:, 0:2 * D].rearrange("p (n d) -> p n d", n=2)).then_inc(setup_evacuated, 1)
            v.wait_ge(pool_consts, 5)
            for p in range(2):
                v.memset(key_pack[p][0:96, :, :].bitcast(F32), 0.0).then_inc(keys_zeroed, 1)
                for h in range(HEADS):
                    last = v.tensor_scalar(key_pack[p][96:P, h, :], zeros[96:P, :], head_rows[96:P, h % GH:h % GH + 1], None, ALU.add)
                last.then_inc(keys_zeroed, 1)

            def moments(n, b, source):
                for t in range(TB):
                    last = v.bn_stats(stats[:, n, t, :], source[t])
                last.then_inc(stats_done[n], 1)

            def aggregate(n, b):
                apart(v, setup_vec, (stats_done[n], b + 1))
                for t in range(TB):
                    last = v.bn_aggr(mean_var[:, n, t, :], stats[:, n, t, :])
                last.then_inc(aggregated[n], 1)

            def normalise(n, t, dst, src):
                return v.tensor_scalar(dst, src, mean_var[:, n, t, 0:1], rstd[:, n, t:t + 1], ALU.subtract, ALU.mult)

            def add_mixed(b):
                v.wait_ge(a_filled, 3 * b + 1)
                v.tensor_tensor(mixed[:], front_a[:, 0:SEQ].rearrange("p (t d) -> p t d", t=TB),
                                x1_all[:, bass.ds(b * TB, TB), :], ALU.add).then_inc(a_drained, 1)

            def moments_mixed(b):
                apart(v, setup_vec, (a_drained, 3 * b + 1))
                moments(0, b, [mixed[:, t, :] for t in range(TB)])

            def first_norm(b):
                v.wait_ge(rstd_done[0], b + 1)
                for t in range(TB):
                    last = normalise(0, t, x1_all[:, bass.ds(b * TB + t, 1), :], mixed[:, t:t + 1, :])
                last.then_inc(x1_done, 1)

            def moments_x1(b):
                apart(v, setup_vec, (x1_done, b + 1))
                moments(1, b, [x1_all[:, bass.ds(b * TB + t, 1), :] for t in range(TB)])

            def second_norm(b):
                v.wait_ge(rstd_done[1], b + 1)
                at_least(v, a_filled, 3 * (b - 1) + 2)
                for t in range(TB):
                    last = normalise(1, t, normed[:, t:t + 1, :], x1_all[:, bass.ds(b * TB + t, 1), :])
                last.then_inc(normed_done, 1)

            def evacuate_v(b, p):
                v.wait_ge(a_filled, 3 * b + 3)
                at_least(v, pv_filled, (b - 1) * GROUPS)
                v.tensor_tensor(v_ext[p][:, :, :, 0:DH], front_a[:, 0:SEQ].rearrange("p (t h e) -> p t h e", t=TB, h=HEADS),
                                bv_row[:].rearrange("p (o h e) -> p o h e", o=1, h=HEADS).broadcast_to([P, TB, HEADS, DH]),
                                ALU.add).then_inc(a_drained, 1)

            def front_start(b):
                add_mixed(b)
                moments_mixed(b)
                aggregate(0, b)
                first_norm(b)
                moments_x1(b)
                aggregate(1, b)
                second_norm(b)

            v.wait_ge(loaded_x0, 32)
            front_start(0)
            evacuate_v(0, 0)
            front_start(1)
            v.wait_ge(loaded_x, 32)

            def reduce_scores(body, g, u):
                group = body.i * GROUPS + g
                qt, pair = u // 2, u % 2
                v.wait_ge(scores_filled, group * 4 + u + 1)
                v.reduce_max(row_max[g % 2][:, qt, 2 * pair:2 * pair + 2], score_bank[u % 2][:, :].rearrange("p (h k) -> p h k", h=2),
                             AX.X).then_inc(scores_drained, 1)

            def max_and_values(body, g, before_name, u_name, has_u):
                group = body.i * GROUPS + g
                parts = max_parts[:, :, 96:96 + 2 * GH].rearrange("p t (j s) -> p t j s", s=2)
                heads = turn_bank[:, 0:SEQ].rearrange("p (t j e) -> p t j e", t=TB, j=GH)
                if body.core:
                    v.wait_ge(scores_drained, group * 4 + 4)
                    if before_name:
                        v.wait_ge(turn_filled, body.turn(before_name) + 1)
                    v.tensor_scalar(parts[:, :, :, 0].bitcast(F32R), row_max[g % 2][:], -1.0, None, ALU.mult).then_inc(max_hi, 1)
                    v.wait_ge(max_hi, group + 1)
                    v.scalar_tensor_tensor(parts[:, :, :, 1].bitcast(F32R), row_max[g % 2][:], -1.0, parts[:, :, :, 0],
                                           ALU.mult, ALU.subtract).then_inc(max_lo, 1)
                if has_u:
                    gg = (g + 2) % GROUPS
                    ctx_v = context[:, :, gg * GH * DH:(gg + 1) * GH * DH].rearrange("p t (j e) -> p t j e", j=GH)
                    v.wait_ge(turn_filled, body.turn(u_name) + 1)
                    v.reciprocal(inv_sum[:], heads[:, :, :, DH]).then_inc(inverted, 1)
                    v.wait_ge(inverted, group - 1)
                    v.tensor_tensor(ctx_v, heads[:, :, :, 0:DH], inv_sum[:].unsqueeze(3).broadcast_to([P, TB, GH, DH]),
                                    ALU.mult).then_inc(turn_drained, 1)

            def add_attention(body):
                b = body.i - 1
                v.wait_ge(turn_filled, body.turn("proj") + 1)
                v.wait_ge(x1_bo_done, b + 1)
                at_least(v, base_done, b)
                v.tensor_tensor(hidden[:], turn_bank[:, 0:SEQ].rearrange("p (t d) -> p t d", t=TB), x1_bo[:], ALU.add).then_inc(turn_drained, 1)

            def moments_hidden(body):
                apart(v, setup_vec, (turn_drained, body.turn("proj") + 1))
                moments(2, body.i - 1, [hidden[:, t, :] for t in range(TB)])

            def copy_logits(body):
                v.wait_ge(turn_filled, body.turn("gate") + 1)
                v.tensor_copy(logits[:], turn_bank[:, 0:TB * EXPERTS].rearrange("p (t e) -> p t e", t=TB)).then_inc(turn_drained, 1)

            def best(body):
                apart(v, setup_vec, (turn_drained, body.turn("gate") + 1))
                for t in range(TB):
                    last = v.max(top8[:, t, :], logits[:, t, :])
                last.then_inc(top_done, 1)

            def best_at(body):
                apart(v, setup_vec, (top_done, body.i - 1))
                for t in range(TB):
                    last = v.max_index(top8_at[:, t, :], top8[:, t, :], logits[:, t, :])
                last.then_inc(top_at_done, 1)
                v.tensor_tensor(below_top[:], top8[:, :, 0:TOPK], top8[:, :, 0:1].broadcast_to([P, TB, TOPK]), ALU.subtract).then_inc(below_done, 1)

            def best_numbers(body):
                v.wait_ge(top_at_done, body.i - 1)
                v.tensor_copy(top_at[:], top8_at[:, :, 0:TOPK]).then_inc(top_at_f, 1)

            def choose(body):
                v.wait_ge(top_at_f, body.i - 1)
                v.tensor_tensor(chosen[:], expert_no[:].rearrange("p (a c e) -> p a c e", a=1, c=1).broadcast_to([P, TB, TOPK, EXPERTS]),
                                top_at[:].unsqueeze(3).broadcast_to([P, TB, TOPK, EXPERTS]), ALU.is_equal).then_inc(chosen_done, 1)

            def mark_used(body):
                v.wait_ge(chosen_done, body.i - 1)
                v.tensor_tensor(used[:], chosen[:, :, 0, :], chosen[:, :, 1, :], ALU.add).then_inc(used_done, 1)

            def gate_total(body):
                v.wait_ge(gate_exp_done, body.i - 1)
                v.reduce_sum(gate_sum[:], gate_exp[:], AX.X).then_inc(gate_sum_done, 1)

            def gate_inverse(body):
                v.wait_ge(gate_sum_done, body.i - 1)
                v.reciprocal(gate_inv[:], gate_sum[:]).then_inc(gate_inv_done, 1)

            def gates(body):
                v.wait_ge(gate_inv_done, body.i - 1)
                v.tensor_tensor(rows[body.p][:, :, :, D], gate_exp[:], gate_inv[:].unsqueeze(2).broadcast_to([P, TB, TOPK]), ALU.mult).then_inc(gate_done, 1)

            def slots(body):
                ranks = turn_bank[:, 0:TB * EXPERTS].rearrange("p (t e) -> p t e", t=TB)
                v.wait_ge(turn_filled, body.turn("rank") + 1)
                v.tensor_tensor(slot[:], ranks, next_row[:].unsqueeze(1).broadcast_to([P, TB, EXPERTS]), ALU.add).then_inc(slot_done, 1)

            def advance(body):
                v.wait_ge(slot_done, body.i - 1)
                v.tensor_tensor(next_row[:], turn_bank[:, TB * EXPERTS:(TB + 1) * EXPERTS], next_row[:], ALU.add).then_inc(turn_drained, 1)
                v.tensor_tensor(slot_of[:], chosen[:], slot[:].unsqueeze(2).broadcast_to([P, TB, TOPK, EXPERTS]), ALU.mult).then_inc(slot_of_done, 1)

            def place_rows(body):
                v.wait_ge(slot_of_done, body.i - 1)
                v.reduce_sum(place[:], slot_of[:].rearrange("p t s e -> p (t s) e"), AX.X).then_inc(place_done, 1)

            def whole_places(body):
                v.wait_ge(place_done, body.i - 1)
                at_least(v, scattered, (body.i - 2) * (16 * TB * TOPK))
                v.tensor_copy(place_i[:], place[:]).then_inc(placed, 1)

            def emit(body):
                i = body.i
                for g in range(GROUPS):
                    has_u = (g >= 2 and body.core) or (g < 2 and body.prev)
                    before_name = ("m3" if body.prev else None, "m0", "m1", "m2")[g]
                    u_name = ("u2", "u3", "u0", "u1")[g]
                    if g == 1 and body.gate:
                        best(body)
                    if body.core:
                        reduce_scores(body, g, 0)
                    if g == 1 and body.gate:
                        best_at(body)
                    if g == 2 and body.front:
                        aggregate(0, i + 2)
                    if g == 3:
                        if body.front:
                            aggregate(1, i + 2)
                        if body.prev:
                            aggregate(2, i - 1)
                    if body.core:
                        reduce_scores(body, g, 1)
                    if g == 1:
                        if body.gate:
                            best_numbers(body)
                    if g == 2 and body.gate:
                        place_rows(body)
                        gate_total(body)
                    if body.core:
                        reduce_scores(body, g, 2)
                    if g == 1:
                        if body.gate:
                            choose(body)
                        if body.project:
                            evacuate_v(i + 1, 1 - body.p)
                    if g == 2 and body.gate:
                        whole_places(body)
                        gate_inverse(body)
                    if body.core:
                        reduce_scores(body, g, 3)
                    if g == 1 and body.gate:
                        mark_used(body)
                    if g == 2 and body.gate:
                        gates(body)
                    max_and_values(body, g, before_name, u_name, has_u)
                    if g == 0 and body.gate:
                        copy_logits(body)
                    if g == 1:
                        if body.gate:
                            slots(body)
                        if body.front:
                            add_mixed(i + 2)
                        if body.gate:
                            advance(body)
                        if body.front:
                            moments_mixed(i + 2)
                    if g == 2:
                        if body.front:
                            first_norm(i + 2)
                        if body.prev:
                            add_attention(body)
                        if body.front:
                            moments_x1(i + 2)
                        if body.prev:
                            moments_hidden(body)
                    if g == 3 and body.front:
                        second_norm(i + 2)

            run_bodies(v, emit)

            steps = [0]

            def link(instruction):
                steps[0] += 1
                instruction.then_inc(table, 1)
                v.wait_ge(table, steps[0])

            v.wait_ge(turn_drained, Body(BATCHES + 1, True).turn("rank") + 1)
            v.tensor_tensor(pad_at[:], pad_at[:], next_row[:], ALU.add).then_inc(table, 1)
            steps[0] += 1
            link(v.scalar_tensor_tensor(counts_f[:], expert_no[:], -float(REGION), next_row[:], ALU.mult, ALU.add))
            link(v.tensor_scalar(counts_i[:], counts_f[:], float(P - 1), None, ALU.add))
            link(v.tensor_scalar(tiles_i[:], counts_i[:], int(math.log2(P)), None, ALU.arith_shift_right))
            link(v.tensor_copy(tiles_f[:], tiles_i[:]))
            link(v.tensor_tensor(tiles_upto[:], upto[:], tiles_f[:].unsqueeze(1).broadcast_to([P, EXPERTS, EXPERTS]), ALU.mult))
            link(v.reduce_sum(tile_end[:], tiles_upto[:], AX.X))
            link(v.tensor_scalar(gap[:], tiles_f[:], -float(P), float(REGION), ALU.mult, ALU.add))
            link(v.tensor_tensor(past[:], tile_no[:].unsqueeze(2).broadcast_to([P, MOE_TILES, EXPERTS]),
                                 tile_end[:].unsqueeze(1).broadcast_to([P, MOE_TILES, EXPERTS]), ALU.is_ge))
            link(v.reduce_sum(tile_expert[:], past[:], AX.X))
            link(v.tensor_tensor(past_gap[:], past[:], gap[:].unsqueeze(1).broadcast_to([P, MOE_TILES, EXPERTS]), ALU.mult))
            link(v.reduce_sum(tile_shift[:], past_gap[:], AX.X))
            link(v.scalar_tensor_tensor(tile_row[:], tile_no[:], float(P), tile_shift[:], ALU.mult, ALU.add))
            link(v.tensor_scalar(expert_i[:], tile_expert[:], float(EXPERTS - 1), None, ALU.min))
            link(v.tensor_copy(pad_at_i[:], pad_at[:]))
            v.tensor_copy(row_i[:], tile_row[:]).then_inc(table_ready, 1)
            v.wait_ge(table_ready, 1)
            v.wait_ge(loaded_moe, 16 * 4)

            def evacuate_got(n, p):
                v.wait_ge(got_turned, n + 1)
                at_least(v, up_filled, n - 1)
                v.tensor_scalar(got_t[p][:], got_bank[:, 0:P], ln_cols[:, 2:3], ln_cols[:, 3:4], ALU.mult, ALU.add).then_inc(got_t_done, 1)

            def bias_up(n, p):
                e = v.value_load(expert_i[0:1, bass.ds(n, 1)], min_val=0, max_val=EXPERTS - 1)
                v.wait_ge(up_filled, n + 1)
                at_least(v, act_done, n - 1)
                v.tensor_tensor(up[p][:].unsqueeze(1), up_bank[p][:, :].unsqueeze(1), b1_sb[:, bass.ds(e, 1), :], ALU.add).then_inc(up_drained, 1)

            def gate_down(n, q, r):
                p = q % 2
                e = v.value_load(expert_i[0:1, bass.ds(n, 1)], min_val=0, max_val=EXPERTS - 1)
                v.wait_ge(down_filled, n + 1)
                v.tensor_tensor(down[p][:].unsqueeze(1), down_bank[p][:, 0:D].unsqueeze(1), b2_sb[:, bass.ds(e, 1), :], ALU.add).then_inc(down_drained, 1)
                v.wait_ge(down_drained, n + 1)
                at_least(v, result_stored[q % PUT], 16 * uses(r, q, PUT))
                v.tensor_scalar(gated[q % PUT], down[p][:], got[q % GOT][:, D:D + 1], None, ALU.mult).then_inc(gated_done, 1)

            def slot_of_v(n, q, r):
                fixed = isinstance(n, int)
                if not fixed or n < MOE_TILES:
                    bias_up(n, q % 2)
                if not fixed or n + 1 < MOE_TILES:
                    evacuate_got(n + 1, (q + 1) % 2)
                if not fixed or n >= 2:
                    gate_down(n - 2, q - 2, r)

            evacuate_got(0, 0)
            run_tiles(v, slot_of_v, MOE_TILES + 2)

            def last_sum(b, p, half):
                v.wait_ge(results_back[p], 32 * half + 32)
                v.tensor_tensor(total[p], first[p], base_all[:, bass.ds(b * TB, TB), :], ALU.add).then_inc(add1, 1)
                v.wait_ge(add1, b + 1)
                v.tensor_tensor(total[p], total[p], second[p], ALU.add).then_inc(add2, 1)
                apart(v, setup_vec, (add2, b + 1))
                for t in range(TB):
                    last = v.bn_stats(stats[:, p, t, :], total[p][:, t, :])
                last.then_inc(last_stats, 1)
                apart(v, setup_vec, (last_stats, b + 1))
                for t in range(TB):
                    last = v.bn_aggr(mean_var[:, p, t, :], stats[:, p, t, :])
                last.then_inc(last_aggr, 1)

            def last_norm(b, p, half):
                v.wait_ge(last_rstd, b + 1)
                at_least(v, out_stored[p], 16 * half)
                for t in range(TB):
                    last = normalise(p, t, final[p][:, t, :], total[p][:, t, :])
                last.then_inc(last_done, 1)

            last_sum(0, 0, 0)
            last_sum(1, 1, 0)
            last_norm(0, 0, 0)
            last_sum(2, 0, 1)
            last_norm(1, 1, 0)
            with v.Fori(1, BATCHES // 2 - 1) as pair:
                last_sum(pair * 2 + 1, 1, pair)
                last_norm(pair * 2, 0, pair)
                last_sum(pair * 2 + 2, 0, pair + 1)
                last_norm(pair * 2 + 1, 1, pair)
            half = BATCHES // 2 - 1
            last_sum(BATCHES - 1, 1, half)
            last_norm(BATCHES - 2, 0, half)
            last_norm(BATCHES - 1, 1, half)




def kernel(L0_attn_x, L0_attn_input_weights, L0_attn_xis, L0_attn_proj_matrix, L0_ffn_ln1_w, L0_ffn_ln1_b,
           L0_ffn_ln2_w, L0_ffn_ln2_b, L0_ffn_w_qkv, L0_ffn_b_qkv, L0_ffn_w_o, L0_ffn_b_o, L0_ffn_w_gate,
           L0_ffn_w1, L0_ffn_b1, L0_ffn_w2, L0_ffn_b2):
    import numpy as np
    import concourse.bacc as bacc
    from concourse.bass_utils import run_bass_kernel_spmd

    x = np.asarray(L0_attn_x).reshape(TOKENS, D)
    given = {
        "x": x, "x_t": x.T, "w_in_t": np.asarray(L0_attn_input_weights).T, "xis": L0_attn_xis,
        "proj": L0_attn_proj_matrix, "ln1_w": L0_ffn_ln1_w, "ln1_b": L0_ffn_ln1_b, "ln2_w": L0_ffn_ln2_w,
        "ln2_b": L0_ffn_ln2_b, "w_qkv": L0_ffn_w_qkv, "b_qkv": L0_ffn_b_qkv, "w_o": L0_ffn_w_o,
        "b_o": L0_ffn_b_o, "w_gate": L0_ffn_w_gate, "w1": L0_ffn_w1, "b1": L0_ffn_b1, "w2": L0_ffn_w2,
        "b2": L0_ffn_b2,
    }
    nc = bacc.Bacc("TRN2", target_bir_lowering=False, num_devices=1)
    arrays, args = {}, {}
    for name, a in given.items():
        a = np.ascontiguousarray(a)
        arrays[f"{name}_dram"] = a
        args[name] = nc.dram_tensor(f"{name}_dram", a.shape, mybir.dt.from_np(a.dtype), kind="ExternalInput").ap()
    out = nc.dram_tensor("out_dram", (TOKENS, D), F32, kind="ExternalOutput").ap()
    build(nc, **args, out=out)
    r = run_bass_kernel_spmd(nc, [arrays], core_ids=[0])
    return r.results[0]["out_dram"].reshape(BATCHES, SEQ, D)
```

```python
import math
from contextlib import ExitStack

import concourse.bass as bass
from concourse import mybir

F32 = mybir.dt.float32
F32R = mybir.dt.float32r
BF16 = mybir.dt.bfloat16
I32 = mybir.dt.int32
U32 = mybir.dt.uint32
ACT = mybir.ActivationFunctionType
ALU = mybir.AluOpType
AX = mybir.AxisListType

P = 128
BATCHES, SEQ, D = 16, 256, 128
TILES = BATCHES * SEQ // P
TB = SEQ // P
HEADS, DH = 16, 8
GROUPS, GH = 4, 4
VW = 32
PARTS = 3
PART_ORDER = ((0, 0, 1), (0, 1, 0))
PR = PARTS * DH
SPILLS = 4
PACKS = 1 + GH
EXPERTS, TOPK, HID = 8, 2, 512
HC = HID // P
TOKENS = BATCHES * SEQ
REGION = TOKENS + P
ROW = D + 2
MOE_TILES = (TOKENS * TOPK + EXPERTS * (P - 1)) // P
SPARE = MOE_TILES - TOKENS * TOPK // P
GOT = 8
PUT = 4
CT = 4
CHUNKS = TILES // CT
EPS = 1e-5
SCALE = 1.0 / math.sqrt(DH)


def at_least(eng, sem, value):
    if isinstance(value, int) and value <= 0:
        return
    eng.wait_ge(sem, value)


def apart(eng, held, *waits):
    if all(isinstance(value, int) for _, value in waits):
        for sem, value in waits:
            at_least(eng, sem, value)
        return
    waits = [(sem, eng.to_reg(value)) for sem, value in waits]
    eng.wait_ge(held, 1)
    for sem, value in waits:
        eng.wait_ge(sem, value)


class Body:

    def __init__(self, i, odd, pair=None):
        self.i, self.odd, self.pair = i, odd, pair
        self.p = 1 if odd else 0
        fixed = isinstance(i, int)
        self.core = not fixed or 0 <= i < BATCHES
        self.prev = not fixed or 0 <= i - 1 < BATCHES
        self.gate = not fixed or 0 <= i - 2 < BATCHES
        self.project = not fixed or 0 <= i + 1 < BATCHES
        self.front = not fixed or 0 <= i + 2 < BATCHES

    def half(self, k):
        if isinstance(self.i, int):
            return (self.i + k) // 2
        return self.pair + (k + (3 if self.odd else 2)) // 2

    USES = {
        "turn": (("m3", "prev"), ("tokens", "gate"), ("u2", "prev"), ("m0", "core"), ("u3", "prev"),
                 ("m1", "core"), ("u0", "core"), ("m2", "core"), ("u1", "core")),
        "a": (("normed", "project"), ("logits", "gate"), ("mixed", "front"), ("v", "project"), ("out", "prev")),
        "b": (("arg", "front"), ("qk", "project"), ("rank", "gate"), ("context", "prev")),
    }

    def has(self, bank):
        stages = {"core": self.core, "prev": self.prev, "gate": self.gate, "project": self.project, "front": self.front}
        return [name for name, stage in self.USES[bank] if stages[stage]]

    def before(self, name, ago=0):
        bank = next(bank for bank, names in self.USES.items() if name in [n for n, _ in names])
        if isinstance(self.i, int):
            done = sum(len(Body(i, False).has(bank)) for i in range(-2, self.i - ago))
            return done + Body(self.i - ago, False).has(bank).index(name)
        done = sum(len(Body(i, False).has(bank)) for i in range(-2, 2)) + self.has(bank).index(name)
        return (self.i - 2 - ago) * len(self.USES[bank]) + done

    def after(self, name, ago=0):
        if isinstance(self.i, int) and not any(name in Body(self.i - ago, False).has(bank) for bank in self.USES):
            return 0
        return self.before(name, ago) + 1


def pad_experts(eng, experts, ends_known, pads_placed, sorted_dram, end_row_i, pad_rows):
    eng.wait_ge(ends_known, 1)
    for e in experts:
        row = eng.value_load(end_row_i[0:1, e:e + 1], min_val=e * REGION, max_val=e * REGION + TOKENS)
        eng.dma_start(sorted_dram[bass.ds(row, P), :], pad_rows[:, e, :]).then_inc(pads_placed, 16)


def run_bodies(eng, emit):
    for i in range(4):
        emit(Body(i, i % 2 == 1))
    with eng.Fori(1, BATCHES // 2 - 2) as pair:
        emit(Body(pair * 2 + 2, False, pair))
        emit(Body(pair * 2 + 3, True, pair))
    for i in range(BATCHES - 2, BATCHES + 2):
        emit(Body(i, i % 2 == 1))


def run_tiles(eng, emit, turns):
    for n in range(GOT):
        emit(n, n, 0)
    with eng.Fori(1, MOE_TILES // GOT) as r:
        for q in range(GOT):
            emit(r * GOT + q, q, r)
    for n in range(MOE_TILES // GOT * GOT, turns):
        emit(n, n % GOT, n // GOT)


def uses(r, q, ring):
    return r * (GOT // ring) + q // ring


def build(nc, x, x_t, w_in_t, xis, proj, ln1_w, ln1_b, ln2_w, ln2_b, w_qkv, b_qkv, w_o, b_o, w_gate,
          w1, b1, w2, b2, out):
    ctx = ExitStack()
    with ctx:
        def sb(name, shape, dt=F32):
            return ctx.enter_context(nc.sbuf_tensor(name, shape, dt))

        def sem(name):
            return ctx.enter_context(nc.semaphore(name))

        ident = sb("ident", [P, P])
        before = sb("before", [P, P], BF16)
        ones_bf = sb("ones_bf", [P, P], BF16)
        zeros = sb("zeros", [P, SEQ])
        eps_col = sb("eps_col", [P, 1])
        xis_col = sb("xis_col", [P, 1])
        neg_half_sq = sb("neg_half_sq", [P, 1])
        feat_bias = sb("feat_bias", [P, 1])
        proj_rd = sb("proj_rd", [P, D])
        scaled_rd = sb("scaled_rd", [P, 2, D])
        scaled_dr = sb("scaled_dr", [P, 2, D])
        w_in_dt = sb("w_in_dt", [P, D])
        w_in_sq = sb("w_in_sq", [P, D])
        w_feat = sb("w_feat", [P, D])
        wqkv_sb = sb("wqkv_sb", [P, 3 * D])
        bqk_col = sb("bqk_col", [P, 2])
        bv_row = sb("bv_row", [P, D])
        wo_sb = sb("wo_sb", [P, D])
        bo_row = sb("bo_row", [P, D])
        wgate_sb = sb("wgate_sb", [P, EXPERTS])
        ln_cols = sb("ln_cols", [P, 4])
        w1_sb = sb("w1_sb", [P, EXPERTS, HID])
        w2_sb = sb("w2_sb", [P, EXPERTS, HC, D])
        b2_sb = sb("b2_sb", [P, EXPERTS, D])
        head_rows = sb("head_rows", [P, GH])
        expert_no = sb("expert_no", [P, EXPERTS])
        upto = sb("upto", [P, EXPERTS, EXPERTS])
        tile_no = sb("tile_no", [P, MOE_TILES])
        result_row = sb("result_row", [P, TB, TOPK])
        pad_rows = sb("pad_rows", [P, EXPERTS + SPARE, ROW])
        pad_no = sb("pad_no", [P, EXPERTS + SPARE])

        x1_all = sb("x1_all", [P, TILES, D])
        base_all = sb("base_all", [P, TILES, D])
        xt_all = sb("xt_all", [P, TOKENS])
        assert EXPERTS * HID == TOKENS
        b1_sb = xt_all[:].rearrange("p (e h) -> p e h", e=EXPERTS)
        xsq = sb("xsq", [P, SEQ])
        feat = sb("feat", [P, SEQ])
        mixed = sb("mixed", [P, TB, D])
        stats = sb("stats", [P, 3, TB, 6])
        mean_var = sb("mean_var", [P, 3, TB, 2])
        log_var = sb("log_var", [P, 4, TB])
        rstd = sb("rstd", [P, 4, TB])
        normed = sb("normed", [P, TB, D])
        normed_t = sb("normed_t", [P, SEQ])
        qk = sb("qk", [P, 2 * SEQ])
        qk_hi = sb("qk_hi", [P, 2 * SEQ], F32R)
        qk_lo = sb("qk_lo", [P, 2 * SEQ], F32R)
        query_pack = [sb(f"query_pack{p}", [P, GROUPS, SEQ], F32R) for p in range(2)]
        key_pack = [sb(f"key_pack{p}", [P, HEADS, SEQ], F32R) for p in range(2)]
        v_ext = [sb(f"v_ext{p}", [P, TB, HEADS, VW]) for p in range(2)]
        row_max = [sb(f"row_max{p}", [P, TB, GH]) for p in range(2)]
        max_parts = sb("max_parts", [P, TB, P])
        probs = sb("probs", [P, 2 * GH, TB, SEQ])
        mixed_v = sb("mixed_v", [P, SEQ])
        inv_sum = sb("inv_sum", [P, TB, GH])
        context = sb("context", [P, TB, D])
        context_t = sb("context_t", [P, SEQ])
        x1_bo = sb("x1_bo", [P, TB, D])
        hidden = sb("hidden", [P, TB, D])
        rows = [sb(f"rows{p}", [P, TB, TOPK, ROW]) for p in range(2)]
        tok_t = sb("tok_t", [P, SEQ])
        logits = sb("logits", [P, TB, EXPERTS])
        top8 = sb("top8", [P, TB, 8])
        top8_at = sb("top8_at", [P, TB, 8], U32)
        top_at = sb("top_at", [P, TB, TOPK])
        chosen = sb("chosen", [P, TB, TOPK, EXPERTS])
        used = sb("used", [P, TB, EXPERTS], BF16)
        below_top = sb("below_top", [P, TB, TOPK])
        gate_exp = sb("gate_exp", [P, TB, TOPK])
        gate_sum = sb("gate_sum", [P, TB])
        gate_inv = sb("gate_inv", [P, TB])
        slot = sb("slot", [P, TB, EXPERTS])
        slot_of = sb("slot_of", [P, TB, TOPK, EXPERTS])
        place = sb("place", [P, TB * TOPK])
        place_i = sb("place_i", [P, TB * TOPK], I32)
        next_row = sb("next_row", [P, EXPERTS])

        tiles_i = sb("tiles_i", [P, EXPERTS], I32)
        counts_f = sb("counts_f", [P, EXPERTS])
        counts_i = sb("counts_i", [P, EXPERTS], I32)
        tiles_f = sb("tiles_f", [P, EXPERTS])
        tiles_upto = sb("tiles_upto", [P, EXPERTS, EXPERTS])
        tile_end = sb("tile_end", [P, EXPERTS])
        gap = sb("gap", [P, EXPERTS])
        past = sb("past", [P, MOE_TILES, EXPERTS])
        past_gap = sb("past_gap", [P, MOE_TILES, EXPERTS])
        tile_expert = sb("tile_expert", [P, MOE_TILES])
        tile_shift = sb("tile_shift", [P, MOE_TILES])
        tile_row = sb("tile_row", [P, MOE_TILES])
        expert_i = sb("expert_i", [P, MOE_TILES], I32)
        expert_col = sb("expert_col", [P, MOE_TILES], I32)
        row_i = sb("row_i", [P, MOE_TILES], I32)
        end_row_i = sb("end_row_i", [P, EXPERTS], I32)
        got_space = key_pack[0][:].bitcast(F32).rearrange("p h t -> p (h t)")
        got = [got_space[:, n * ROW:(n + 1) * ROW] for n in range(GOT)]
        got_t = [sb(f"got_t{p}", [P, P]) for p in range(2)]
        up = [sb(f"up{p}", [P, HID]) for p in range(2)]
        act = [sb(f"act{p}", [P, HID]) for p in range(2)]
        act_t = [v_ext[p][:].rearrange("p t h e -> p (t h e)")[:, 0:HID] for p in range(2)]
        down = [sb(f"down{p}", [P, D]) for p in range(2)]
        gated = [probs[:, n, 0, 0:D] for n in range(PUT)]
        goes_to = [sb(f"goes_to{p}", [P, 1], I32) for p in range(PUT)]
        first_all = probs[:].rearrange("p a t (s d) -> p (a t s) d", d=D)
        second_all = x1_all
        chunk_stats = sb("chunk_stats", [P, 2, CT, 6])
        chunk_mean_var = sb("chunk_mean_var", [P, 2, CT, 2])
        chunk_log = sb("chunk_log", [P, 2, CT])
        chunk_rstd = sb("chunk_rstd", [P, 2, CT])
        chunk_shift = sb("chunk_shift", [P, 2, CT])

        sorted_dram = nc.dram_tensor("sorted_dram", [EXPERTS * REGION + SPARE * P, ROW], F32, kind="Internal").ap()
        result_dram = nc.dram_tensor("result_dram", [TOPK * TOKENS + (EXPERTS + SPARE) * P, D], F32, kind="Internal").ap()

        spill = [nc.dram_tensor(f"spill{p}", [2, D, PARTS, SEQ], F32, kind="Internal").ap() for p in range(2)]

        banks = [ctx.enter_context(nc.psum_tensor(f"bank{i}", [P, 512], F32)) for i in range(8)]
        score_bank, exp_bank = banks[0:2], banks[2:4]
        pv_bank, turn_bank, front_a, front_b = banks[4:8]
        up_bank, act_t_bank, down_bank = banks[0:2], banks[2:4], banks[4:6]
        got_bank = banks[6]

        loaded_features = sem("loaded_features")
        loaded_small = sem("loaded_small")
        loaded_x0 = sem("loaded_x0")
        loaded_x1 = sem("loaded_x1")
        loaded_x = sem("loaded_x")
        loaded_moe = sem("loaded_moe")
        pool_zeroed = sem("pool_zeroed")
        pool_consts = sem("pool_consts")
        setup_vec = sem("setup_vec")
        setup_scaled = sem("setup_scaled")
        setup_transposed = sem("setup_transposed")
        setup_evacuated = sem("setup_evacuated")
        setup_sq = sem("setup_sq")
        values_zeroed = sem("values_zeroed")
        setup_arg = sem("setup_arg")
        setup_feat = sem("setup_feat")
        keys_zeroed = [sem(f"keys_zeroed{p}") for p in range(2)]
        keys_ones = [sem(f"keys_ones{p}") for p in range(2)]
        stored_pads = sem("stored_pads")
        squared = sem("squared")
        b_filled, b_drained = sem("b_filled"), sem("b_drained")
        a_filled, a_drained = sem("a_filled"), sem("a_drained")
        stats_done = [sem(f"stats_done{n}") for n in range(3)]
        aggregated = [sem(f"aggregated{n}") for n in range(3)]
        logged = [sem(f"logged{n}") for n in range(3)]
        rstd_done = [sem(f"rstd_done{n}") for n in range(3)]
        x1_done = sem("x1_done")
        normed_done = sem("normed_done")
        split_done = sem("split_done")
        spilled = [sem(f"spilled{p}") for p in range(2)]
        packed = [sem(f"packed{p}") for p in range(2)]
        scores_filled, scores_drained = sem("scores_filled"), sem("scores_drained")
        max_hi, max_lo = sem("max_hi"), sem("max_lo")
        turn_filled, turn_drained = sem("turn_filled"), sem("turn_drained")
        keyed_filled = sem("keyed_filled")
        exp_done = sem("exp_done")
        pv_filled, pv_evacuated = sem("pv_filled"), sem("pv_evacuated")
        inverted = sem("inverted")
        x1_bo_done = sem("x1_bo_done")
        base_done = sem("base_done")
        token_row = sem("token_row")
        copied_row = sem("copied_row")
        counted_row = sem("counted_row")
        logits_done = sem("logits_done")
        top_done, top_at_done, top_at_f = sem("top_done"), sem("top_at_done"), sem("top_at_f")
        chosen_done, used_done = sem("chosen_done"), sem("used_done")
        below_done, gate_exp_done, gate_sum_done = sem("below_done"), sem("gate_exp_done"), sem("gate_sum_done")
        gate_inv_done, gate_done = sem("gate_inv_done"), sem("gate_done")
        slot_done, slot_of_done, place_done, placed = sem("slot_done"), sem("slot_of_done"), sem("place_done"), sem("placed")
        scattered = sem("scattered")
        table = sem("table")
        table_ready = sem("table_ready")
        pads_placed = sem("pads_placed")
        ends_known = sem("ends_known")
        got_loaded = [sem(f"got_loaded{p}") for p in range(GOT)]
        got_turned, got_t_done = sem("got_turned"), sem("got_t_done")
        up_filled, up_drained = sem("up_filled"), sem("up_drained")
        act_done = sem("act_done")
        act_turned, act_t_done = sem("act_turned"), sem("act_t_done")
        down_filled, down_drained = sem("down_filled"), sem("down_drained")
        gated_done = sem("gated_done")
        goes_done = sem("goes_done")
        result_stored = [sem(f"result_stored{p}") for p in range(PUT)]
        results_back = [sem(f"results_back{c}") for c in range(CHUNKS)]
        add1, add2, last_stats, last_aggr = sem("add1"), sem("add2"), sem("last_stats"), sem("last_aggr")
        last_log, last_rstd, last_done = sem("last_log"), sem("last_rstd"), sem("last_done")
        last_shift = sem("last_shift")
        out_stored = sem("out_stored")

        SMALL = 11
        x_v = x.rearrange("(t p) d -> p t d", p=P)
        out_v = out.rearrange("(t p) d -> p t d", p=P)
        FIRST_TILES = 2 * TB

        block = ctx.enter_context(nc.Block())

        @block.sync
        def _(sp):
            def column(v):
                return v.rearrange("(p o) -> p o", o=1)

            def broadcast(v):
                return v.rearrange("(o n) -> o n", o=1).broadcast_to([P, v.shape[0]])

            for dst, src in ((xis_col[:], column(xis)), (proj_rd[:], proj), (w_in_dt[:], w_in_t)):
                sp.dma_start(dst, src).then_inc(loaded_features, 16)

            def load_x(tiles, loaded):
                sp.dma_start(xt_all[:, tiles.start * P:tiles.stop * P], x_t[:, tiles.start * P:tiles.stop * P]).then_inc(loaded, 16)
                sp.dma_start(x1_all[:, tiles, :], x_v[:, tiles, :]).then_inc(loaded, 16)

            load_x(slice(0, FIRST_TILES), loaded_x0)
            small = (
                (ln_cols[:, 0:1], column(ln1_w)), (ln_cols[:, 1:2], column(ln1_b)),
                (wqkv_sb[:], w_qkv),
                (bqk_col[:, 0:1], column(b_qkv[0:D])), (bqk_col[:, 1:2], column(b_qkv[D:2 * D])),
                (bv_row[:], broadcast(b_qkv[2 * D:3 * D])), (bo_row[:], broadcast(b_o)),
                (ln_cols[:, 2:3], column(ln2_w)), (ln_cols[:, 3:4], column(ln2_b)),
                (wo_sb[:], w_o), (wgate_sb[:], w_gate),
            )
            assert len(small) == SMALL
            for dst, src in small:
                sp.dma_start(dst, src).then_inc(loaded_small, 16)
            load_x(slice(FIRST_TILES, 2 * FIRST_TILES), loaded_x1)

            def pack(body):
                b, p, half = body.i + 1, 1 - body.p, body.half(1)
                hi_ready = body.after("qk")
                keyed_before, spills, reads, batches = (b - 1) * HEADS, (half + 1) * 16 * SPILLS, half * 16 * PACKS, b + 1
                if not isinstance(b, int):
                    keyed_before, spills, reads, batches, hi_ready = [
                        sp.to_reg(n) for n in (keyed_before, spills, reads, batches, hi_ready)]
                at_least(sp, packed[p], reads)
                for low, part, ready, count in ((0, qk_hi, b_drained, hi_ready), (1, qk_lo, split_done, batches)):
                    sp.wait_ge(ready, count)
                    for n, orders in enumerate(PART_ORDER):
                        at = [c for c, lo in enumerate(orders) if lo == low]
                        dst = spill[p][n, :, at[0]:at[-1] + 1:at[-1] - at[0] or 1, :]
                        src = part[:, n * SEQ:(n + 1) * SEQ].bitcast(F32).unsqueeze(1)
                        sp.dma_start(dst, src.broadcast_to([P, len(at), SEQ])).then_inc(spilled[p], 16)
                sp.wait_ge(spilled[p], spills)
                at_least(sp, keyed_filled, keyed_before)
                sp.dma_start(query_pack[p][0:GH * PR, :, :].bitcast(F32),
                             spill[p][0].rearrange("(g j e) c t -> (j e c) g t", g=GROUPS, j=GH)).then_inc(packed[p], 16)
                for j in range(GH):
                    sp.dma_start(key_pack[p][PR * j:PR * j + PR, :, :].bitcast(F32).rearrange("r (g j) t -> r g j t", j=GH)[:, :, j, :],
                                 spill[p][1].rearrange("(g j e) c t -> j (e c) g t", j=GH, g=GROUPS)[j]).then_inc(packed[p], 16)

            sp.wait_ge(keys_zeroed[0], 1)
            sp.wait_ge(keys_ones[0], 2)
            pack(Body(-1, True))
            load_x(slice(2 * FIRST_TILES, TILES), loaded_x)
            sp.wait_ge(keys_zeroed[1], 1)
            sp.wait_ge(keys_ones[1], 1)

            def emit(body):
                if body.project:
                    pack(body)

            run_bodies(sp, emit)

            pad_experts(sp, range(0, EXPERTS, 2), ends_known, pads_placed, sorted_dram, end_row_i, pad_rows)

            sp.wait_ge(scattered, 16 * TB * TOPK * BATCHES)
            sp.wait_ge(pads_placed, 16 * EXPERTS)
            sp.wait_ge(stored_pads, 16 * SPARE)
            sp.wait_ge(table_ready, 1)

            def load_tile(n, q, r):
                row = sp.value_load(row_i[0:1, bass.ds(n, 1)], min_val=0, max_val=EXPERTS * REGION + (SPARE - 1) * P)
                at_least(sp, gated_done, n - GOT + 1)
                at_least(sp, goes_done, n - GOT + 1)
                sp.dma_start(got[q], sorted_dram[bass.ds(row, P), :]).then_inc(got_loaded[q], 16)

            run_tiles(sp, load_tile, MOE_TILES)

            for p in range(PUT):
                sp.wait_ge(result_stored[p], 16 * ((MOE_TILES + PUT - 1 - p) // PUT))

            r_v = result_dram[0:TOPK * TOKENS, :].rearrange("(s t p) d -> s p t d", s=TOPK, p=P)
            for c in range(CHUNKS):
                tiles = slice(c * CT, (c + 1) * CT)
                for which, dst in enumerate((first_all, second_all)):
                    sp.dma_start(dst[:, tiles, :], r_v[which][:, tiles, :]).then_inc(results_back[c], 16)
            for c in range(CHUNKS):
                tiles = slice(c * CT, (c + 1) * CT)
                sp.wait_ge(last_done, c + 1)
                sp.dma_start(out_v[:, tiles, :], first_all[:, tiles, :]).then_inc(out_stored, 16)
            sp.wait_ge(out_stored, 16 * CHUNKS)

        @block.gpsimd
        def _(pool):
            for buf, value in ((ident, 0.0), (before, 1.0), (head_rows, 1.0), (upto, 1.0), (pad_rows, 0.0)):
                pool.memset(buf[:], value).then_inc(pool_zeroed, 1)
            pool.wait_ge(pool_zeroed, 5)
            pool.affine_select(out=ident[:], in_=ident[:], compare_op=ALU.not_equal, fill=1.0, base=0,
                               pattern=[[-1, P]], channel_multiplier=1).then_inc(pool_consts, 1)
            pool.affine_select(out=before[:], in_=before[:], compare_op=ALU.is_gt, fill=0.0, base=0,
                               pattern=[[1, P]], channel_multiplier=-1).then_inc(pool_consts, 1)
            pool.affine_select(out=upto[:], in_=upto[:], compare_op=ALU.is_ge, fill=0.0, base=0,
                               pattern=[[1, EXPERTS], [-1, EXPERTS]], channel_multiplier=0).then_inc(pool_consts, 1)
            pool.affine_select(out=head_rows[:], in_=head_rows[:], compare_op=ALU.is_ge, fill=0.0, base=-96,
                               pattern=[[-2, GH]], channel_multiplier=1).then_inc(pool_consts, 1)
            pool.wait_ge(pool_consts, 4)
            pool.affine_select(out=head_rows[:], in_=head_rows[:], compare_op=ALU.is_ge, fill=0.0, base=97,
                               pattern=[[2, GH]], channel_multiplier=-1).then_inc(pool_consts, 1)
            iota = dict(allow_small_or_imprecise_dtypes=True)
            pool.iota(expert_no[:], pattern=[[1, EXPERTS]], base=0, channel_multiplier=0, **iota).then_inc(pool_consts, 1)
            pool.iota(tile_no[:], pattern=[[1, MOE_TILES]], base=0, channel_multiplier=0, **iota).then_inc(pool_consts, 1)
            pool.iota(next_row[:], pattern=[[REGION, EXPERTS]], base=0, channel_multiplier=0, **iota).then_inc(pool_consts, 1)
            pool.iota(result_row[:], pattern=[[P, TB], [TOKENS, TOPK]], base=0, channel_multiplier=1, **iota).then_inc(pool_consts, 1)
            pool.iota(pad_no[:], pattern=[[P, EXPERTS + SPARE]], base=TOPK * TOKENS, channel_multiplier=1, **iota).then_inc(pool_consts, 1)
            pool.wait_ge(pool_consts, 10)
            pool.tensor_copy(pad_rows[:, :, ROW - 1], pad_no[:]).then_inc(pool_consts, 1)
            pool.wait_ge(pool_consts, 11)
            pool.wait_ge(loaded_features, 48)
            pool.tensor_tensor(w_in_sq[:], w_in_dt[:], w_in_dt[:], ALU.mult).then_inc(setup_sq, 1)

            def square(body):
                b = body.i + 2
                at_least(pool, b_filled, body.after("arg", 1))
                pool.tensor_tensor(xsq[:], xt_all[:, bass.ds(b * SEQ, SEQ)], xt_all[:, bass.ds(b * SEQ, SEQ)],
                                   ALU.mult).then_inc(squared, 1)

            pool.wait_ge(loaded_x0, 32)
            square(Body(-2, False))
            pool.memset(key_pack[0][0:96, :, :].bitcast(F32), 0.0).then_inc(keys_zeroed[0], 1)
            pool.memset(key_pack[1][0:96, :, :].bitcast(F32), 0.0).then_inc(keys_zeroed[1], 1)
            square(Body(-1, True))
            for k in range(SPARE):
                at = EXPERTS * REGION + k * P
                pool.dma_start(sorted_dram[at:at + P, :], pad_rows[:, EXPERTS + k, :]).then_inc(stored_pads, 16)
            pool.wait_ge(loaded_small, 16 * SMALL)
            pool.wait_ge(loaded_x1, 32)

            def residuals(body):
                b = body.i - 1
                at_least(pool, base_done, b)
                pool.wait_ge(x1_done, b + 1)
                pool.tensor_tensor(x1_bo[:], x1_all[:, bass.ds(b * TB, TB), :],
                                   bo_row[:].unsqueeze(1).broadcast_to([P, TB, D]), ALU.add).then_inc(x1_bo_done, 1)

            def base(body):
                tiles = bass.ds((body.i - 1) * TB, TB)
                pool.wait_ge(a_drained, body.after("out"))
                pool.tensor_tensor(base_all[:, tiles, :], hidden[:], x1_all[:, tiles, :], ALU.add).then_inc(base_done, 1)

            def third_norm(body):
                b = body.i - 1
                apart(pool, pool_consts, (rstd_done[2], b + 1),
                      (scattered, (b - 1) * (16 * TB * TOPK)))
                for t in range(TB):
                    last = pool.tensor_scalar(rows[1 - body.p][:, t, 0, 0:D], hidden[:, t, :],
                                              mean_var[:, 2, t, 0:1], rstd[:, 2, t:t + 1], ALU.subtract, ALU.mult)
                last.then_inc(token_row, 1)

            def low_parts(body):
                pool.wait_ge(b_drained, body.after("qk"))
                pool.tensor_tensor(qk_lo[:], qk[:], qk_hi[:].bitcast(F32), ALU.subtract).then_inc(split_done, 1)

            def copy_rows(body):
                b, mine = body.i - 2, rows[body.p]
                apart(pool, pool_consts, (token_row, b + 1))
                pool.tensor_copy(mine[:, :, 1, 0:D], mine[:, :, 0, 0:D]).then_inc(copied_row, 1)
                apart(pool, pool_consts, (counted_row, b))
                pool.tensor_copy(mine[:, :, :, ROW - 1], result_row[:]).then_inc(copied_row, 1)
                apart(pool, pool_consts, (copied_row, 2 * b + 2))
                pool.tensor_scalar(result_row[:], result_row[:], float(SEQ), None, ALU.add).then_inc(counted_row, 1)

            def scatter(body):
                b = body.i - 2
                apart(pool, pool_consts, (gate_done, b + 1), (placed, b + 1))
                for t in range(TB):
                    for s in range(TOPK):
                        n = t * TOPK + s
                        pool.indirect_dma_start(
                            out=sorted_dram, out_offset=bass.IndirectOffsetOnAxis(ap=place_i[:, n:n + 1], axis=0),
                            in_=rows[body.p][:, t, s, :], in_offset=None).then_inc(scattered, 16)

            def emit(body):
                if isinstance(body.i, int) and body.i == 2:
                    pool.wait_ge(loaded_x, 32)
                if body.front:
                    square(body)
                if body.gate:
                    copy_rows(body)
                if body.prev:
                    residuals(body)
                if body.project:
                    low_parts(body)
                if body.gate:
                    scatter(body)
                if body.prev and body.core:
                    third_norm(body)
                if body.prev:
                    base(body)

            low_parts(Body(-1, True))
            run_bodies(pool, emit)

            def put(n, q, r):
                p = q % PUT
                apart(pool, pool_consts, (got_loaded[q], uses(r, q, GOT) * 16 + 16), (result_stored[p], uses(r, q, PUT) * 16))
                pool.tensor_copy(goes_to[p][:], got[q][:, ROW - 1:ROW]).then_inc(goes_done, 1)
                apart(pool, pool_consts, (goes_done, n + 1), (gated_done, n + 1))
                pool.indirect_dma_start(
                    out=result_dram, out_offset=bass.IndirectOffsetOnAxis(ap=goes_to[p][:, 0:1], axis=0),
                    in_=gated[p], in_offset=None).then_inc(result_stored[p], 16)

            run_tiles(pool, put, MOE_TILES)

            for c in range(CHUNKS):
                tiles = slice(c * CT, (c + 1) * CT)
                pool.wait_ge(results_back[c], 32)
                pool.tensor_tensor(base_all[:, tiles, :], first_all[:, tiles, :], base_all[:, tiles, :], ALU.add).then_inc(add1, 1)

        @block.tensor
        def _(pe):
            pe.wait_ge(pool_consts, 1)
            pe.wait_ge(setup_scaled, 2)
            for n in range(2):
                last = pe.transpose(score_bank[0][:, n * D:(n + 1) * D], scaled_rd[:, n, :], ident[:])
            last.then_inc(setup_transposed, 1)
            pe.wait_ge(setup_evacuated, 1)
            pe.wait_ge(setup_sq, 1)
            pe.matmul(score_bank[1][:, 0:D], scaled_dr[:, 0, :], w_in_dt[:], start=True, stop=False)
            pe.matmul(score_bank[1][:, 0:D], scaled_dr[:, 1, :], w_in_sq[:], start=False, stop=True).then_inc(setup_arg, 1)

            def features(body):
                b = body.i + 2
                pe.wait_ge(squared, b + 1)
                at_least(pe, b_drained, body.before("arg"))
                pe.matmul(front_b[:, 0:SEQ], scaled_dr[:, 0, :], xt_all[:, bass.ds(b * SEQ, SEQ)], start=True, stop=False)
                pe.matmul(front_b[:, 0:SEQ], scaled_dr[:, 1, :], xsq[:], start=False, stop=True).then_inc(b_filled, 1)

            def mix(body):
                pe.wait_ge(b_drained, body.after("arg"))
                at_least(pe, a_drained, body.before("mixed"))
                for t in range(TB):
                    last = pe.matmul(front_a[:, t * D:(t + 1) * D], feat[:, t * P:(t + 1) * P], w_feat[:], start=True, stop=True)
                last.then_inc(a_filled, 1)

            def turn_normed(body):
                pe.wait_ge(normed_done, body.i + 2)
                pe.wait_ge(a_drained, body.before("normed"))
                for t in range(TB):
                    last = pe.transpose(front_a[:, t * P:(t + 1) * P], normed[:, t, :], ident[:])
                last.then_inc(a_filled, 1)

            def project_qk(body):
                pe.wait_ge(a_drained, body.after("normed"))
                pe.wait_ge(b_drained, body.before("qk"))
                for n in range(2):
                    last = pe.matmul(front_b[:, n * SEQ:(n + 1) * SEQ], wqkv_sb[:, n * D:(n + 1) * D], normed_t[:],
                                     start=True, stop=True)
                last.then_inc(b_filled, 1)

            def project_v(body):
                pe.wait_ge(a_drained, body.before("v"))
                for t in range(TB):
                    last = pe.matmul(front_a[:, t * D:(t + 1) * D], normed_t[:, t * P:(t + 1) * P],
                                     wqkv_sb[:, 2 * D:3 * D], start=True, stop=True)
                last.then_inc(a_filled, 1)

            pe.wait_ge(setup_feat, 1)
            features(Body(-2, False))
            mix(Body(-2, False))
            features(Body(-1, True))
            turn_normed(Body(-1, True))
            mix(Body(-1, True))
            pe.wait_ge(loaded_small, 16 * SMALL)
            project_qk(Body(-1, True))
            project_v(Body(-1, True))

            def scores(body, g, u):
                group = body.i * GROUPS + g
                qt, pair = u // 2, u % 2
                if g == 0 and u == 0:
                    pe.wait_ge(packed[body.p], (body.half(0) + 1) * 16 * PACKS)
                at_least(pe, scores_drained, group * 4 + u - 1)
                h = GH * g + 2 * pair
                pe.matmul(score_bank[u % 2][:, :], query_pack[body.p][0:96, g, qt * P:(qt + 1) * P],
                          key_pack[body.p][0:96, h:h + 2, :], start=True, stop=True).then_inc(scores_filled, 1)

            def turn_max(body, name, group):
                pe.wait_ge(max_lo, group + 1)
                at_least(pe, turn_drained, body.before(name))
                for t in range(TB):
                    last = pe.transpose(turn_bank[:, t * P:(t + 1) * P], max_parts[:, t, :], ident[:])
                last.then_inc(turn_filled, 1)

            def keyed(body, g, j, m_name):
                group = body.i * GROUPS + g - 1
                p, gg = (body.p, g - 1) if g else (1 - body.p, GROUPS - 1)
                if j == 0:
                    pe.wait_ge(turn_drained, body.after(m_name))
                at_least(pe, exp_done, group * GH + j - 1)
                for kt in range(TB):
                    last = pe.matmul(exp_bank[j % 2][:, kt * SEQ:(kt + 1) * SEQ],
                                     key_pack[p][:, GH * gg + j, kt * P:(kt + 1) * P], query_pack[p][:, gg, :],
                                     start=True, stop=True)
                last.then_inc(keyed_filled, 1)

            def values(body, g):
                group = body.i * GROUPS + g - 2
                p, gg, ago = (body.p, g - 2, 1) if g >= 2 else (1 - body.p, g + 2, 2)
                pe.wait_ge(exp_done, group * GH + GH)
                at_least(pe, pv_evacuated, group)
                pe.wait_ge(a_drained, body.after("v", ago))
                for kt in range(TB):
                    for j in range(GH):
                        last = pe.matmul(pv_bank[VW * j:VW * j + VW, 0:SEQ], v_ext[p][:, kt, GH * gg + j, :],
                                         probs[:, GH * (gg % 2) + j, kt, :], start=kt == 0, stop=kt == TB - 1,
                                         tile_position=(0, VW * j))
                last.then_inc(pv_filled, 1)

            def turn_values(body, name, g):
                group = body.i * GROUPS + g - 2
                pe.wait_ge(pv_evacuated, group + 1)
                at_least(pe, turn_drained, body.before(name))
                for t in range(TB):
                    last = pe.transpose(turn_bank[:, t * P:(t + 1) * P], mixed_v[:, t * P:(t + 1) * P], ident[:])
                last.then_inc(turn_filled, 1)

            def turn_context(body):
                pe.wait_ge(turn_drained, body.after("u3"))
                pe.wait_ge(b_drained, body.before("context"))
                for t in range(TB):
                    last = pe.transpose(front_b[:, t * P:(t + 1) * P], context[:, t, :], ident[:])
                last.then_inc(b_filled, 1)

            def project_out(body):
                pe.wait_ge(b_drained, body.after("context"))
                pe.wait_ge(a_drained, body.before("out"))
                for t in range(TB):
                    last = pe.matmul(front_a[:, t * D:(t + 1) * D], context_t[:, t * P:(t + 1) * P], wo_sb[:],
                                     start=True, stop=True)
                last.then_inc(a_filled, 1)

            def turn_tokens(body):
                pe.wait_ge(token_row, body.i - 1)
                pe.wait_ge(turn_drained, body.before("tokens"))
                for t in range(TB):
                    last = pe.transpose(turn_bank[:, t * P:(t + 1) * P], rows[body.p][:, t, 0, 0:D], ident[:])
                last.then_inc(turn_filled, 1)

            def gate_logits(body):
                pe.wait_ge(turn_drained, body.after("tokens"))
                pe.wait_ge(a_drained, body.before("logits"))
                for t in range(TB):
                    last = pe.matmul(front_a[:, t * EXPERTS:(t + 1) * EXPERTS], tok_t[:, t * P:(t + 1) * P], wgate_sb[:],
                                     start=True, stop=True)
                last.then_inc(a_filled, 1)

            def ranks(body):
                pe.wait_ge(used_done, body.i - 1)
                pe.wait_ge(b_drained, body.before("rank"))
                e = EXPERTS
                pe.matmul(front_b[:, 0:e], before[:], used[:, 0, :], start=True, stop=True)
                pe.matmul(front_b[:, e:2 * e], before[:], used[:, 1, :], start=True, stop=False)
                pe.matmul(front_b[:, e:2 * e], ones_bf[:], used[:, 0, :], start=False, stop=True)
                pe.matmul(front_b[:, 2 * e:3 * e], ones_bf[:], used[:, 0, :], start=True, stop=False)
                pe.matmul(front_b[:, 2 * e:3 * e], ones_bf[:], used[:, 1, :], start=False, stop=True).then_inc(b_filled, 1)

            def emit(body):
                for g in range(GROUPS):
                    m_name = ("m3", "m0", "m1", "m2")[g]
                    u_name = ("u2", "u3", "u0", "u1")[g]
                    has_m = (g > 0 and body.core) or (g == 0 and body.prev)
                    has_u = (g >= 2 and body.core) or (g < 2 and body.prev)
                    if body.core and g == 0:
                        scores(body, g, 0)
                    if g == 1 and body.project:
                        project_qk(body)
                    if body.core and g == 0:
                        scores(body, g, 1)
                    if g == 3 and body.prev:
                        project_out(body)
                    if has_m:
                        turn_max(body, m_name, body.i * GROUPS + g - 1)
                    if g == 2 and body.project:
                        project_v(body)
                    if has_u:
                        values(body, g)
                    if body.core:
                        scores(body, g, 2)
                    if has_m:
                        keyed(body, g, 0, m_name)
                    if g == 0 and body.gate:
                        turn_tokens(body)
                    if body.core:
                        scores(body, g, 3)
                    if has_m:
                        keyed(body, g, 1, m_name)
                    if g == 0:
                        if body.project:
                            turn_normed(body)
                        if body.front:
                            features(body)
                    if g == 1 and body.front:
                        mix(body)
                    if g == 2 and body.prev:
                        turn_context(body)
                    if has_m:
                        keyed(body, g, 2, m_name)
                    if body.core and g + 1 < GROUPS:
                        scores(body, g + 1, 0)
                    if has_u:
                        turn_values(body, u_name, g)
                    if has_m:
                        keyed(body, g, 3, m_name)
                    if body.core and g + 1 < GROUPS:
                        scores(body, g + 1, 1)
                    if g == 0 and body.gate:
                        gate_logits(body)
                    if g == 1 and body.gate:
                        ranks(body)

            run_bodies(pe, emit)

            pe.wait_ge(table_ready, 1)
            pe.wait_ge(loaded_moe, 16 * 4)

            w1_cols = w1_sb[:].rearrange("p e h -> p (e h)")
            w2_cols = w2_sb[:].rearrange("p e c d -> p (e c d)")

            def columns_of(n):
                return pe.value_load(expert_col[0:1, bass.ds(n, 1)], min_val=0, max_val=(EXPERTS - 1) * HID)

            def turn_got(n, q, r):
                pe.wait_ge(got_loaded[q % GOT], uses(r, q, GOT) * 16 + 16)
                at_least(pe, got_t_done, n)
                pe.transpose(got_bank[:, 0:P], got[q % GOT][:, 0:D], ident[:]).then_inc(got_turned, 1)

            def go_up(n, p, col):
                pe.wait_ge(got_t_done, n + 1)
                at_least(pe, up_drained, n - 1)
                pe.matmul(up_bank[p][:, :], got_t[p][:], w1_cols[:, bass.ds(col, HID)], start=True, stop=True).then_inc(up_filled, 1)

            def turn_act(n, p):
                pe.wait_ge(act_done, n + 1)
                at_least(pe, act_t_done, n - 1)
                for c in range(HC):
                    last = pe.transpose(act_t_bank[p][:, c * P:(c + 1) * P], act[p][:, c * P:(c + 1) * P], ident[:])
                last.then_inc(act_turned, 1)

            def go_down(n, p, col):
                pe.wait_ge(act_t_done, n + 1)
                at_least(pe, down_drained, n - 1)
                for c in range(HC):
                    last = pe.matmul(down_bank[p][:, 0:D], act_t[p][:, c * P:(c + 1) * P], w2_cols[:, c * D:][:, bass.ds(col, D)],
                                     start=c == 0, stop=c == HC - 1)
                last.then_inc(down_filled, 1)

            round_cols = {}

            def slot_of_pe(n, q, r):
                fixed = isinstance(n, int)
                up, down = not fixed or n < MOE_TILES, not fixed or n >= 3
                down_col = (round_cols[q - 3] if q >= 3 else columns_of(n - 3)) if down else None
                if q >= 3:
                    up_col = round_cols[q] = columns_of(n) if up else None
                if not fixed or n + 1 < MOE_TILES:
                    turn_got(n + 1, q + 1, r)
                if not fixed or 0 <= n - 2 < MOE_TILES:
                    turn_act(n - 2, q % 2)
                if down:
                    go_down(n - 3, (q + 1) % 2, down_col)
                if q < 3:
                    up_col = round_cols[q] = columns_of(n) if up else None
                if up:
                    go_up(n, q % 2, up_col)

            turn_got(0, 0, 0)
            run_tiles(pe, slot_of_pe, MOE_TILES + 3)

        @block.scalar
        def _(a):
            a.preload_act_table_set("natural_log_exp_and_others")

            def key_ones(p, heads):
                for h in heads:
                    last = a.activation(key_pack[p][96:P, h, :], zeros[96:P, :], ACT.Identity, bias=head_rows[96:P, h % GH:h % GH + 1])
                last.then_inc(keys_ones[p], 1)

            a.wait_ge(pool_consts, 5)
            a.wait_ge(setup_vec, 1)
            key_ones(0, range(HEADS // 2))
            a.wait_ge(setup_arg, 1)
            a.activation(w_feat[:], score_bank[1][:, 0:D], ACT.Exp, bias=feat_bias[:, 0:1]).then_inc(setup_feat, 1)

            def feature_exp(body):
                a.wait_ge(b_filled, body.after("arg"))
                at_least(a, a_filled, body.after("mixed", 1))
                a.activation(feat[:], front_b[:, 0:SEQ], ACT.Exp, bias=feat_bias[:, 0:1]).then_inc(b_drained, 1)

            def inverse_std(n, b):
                a.wait_ge(aggregated[n], b + 1)
                a.activation(log_var[:, n, :], mean_var[:, n, :, 1], ACT.Ln, bias=eps_col[:, 0:1]).then_inc(logged[n], 1)
                a.wait_ge(logged[n], b + 1)
                a.activation(rstd[:, n, :], log_var[:, n, :], ACT.Exp, scale=-0.5).then_inc(rstd_done[n], 1)

            def bias_qk(body, k):
                n, rounded = k // 2, k % 2
                part = slice(n * SEQ, (n + 1) * SEQ)
                if k == 0:
                    a.wait_ge(b_filled, body.after("qk"))
                    at_least(a, split_done, body.i + 1)
                    at_least(a, packed[body.p], (body.half(0) + 1) * 16 * PACKS)
                last = a.activation((qk_hi if rounded else qk)[:, part], front_b[:, part], ACT.Identity, bias=bqk_col[:, n:n + 1])
                if k == 3:
                    last.then_inc(b_drained, 1)

            def evacuate_normed(body):
                a.wait_ge(a_filled, body.after("normed"))
                a.activation(normed_t[:], front_a[:, 0:SEQ], ACT.Identity, bias=ln_cols[:, 1:2], scale=ln_cols[:, 0:1]).then_inc(a_drained, 1)

            def evacuate_tokens(body):
                a.wait_ge(turn_filled, body.after("tokens"))
                a.activation(tok_t[:], turn_bank[:, 0:SEQ], ACT.Identity, bias=ln_cols[:, 3:4], scale=ln_cols[:, 2:3]).then_inc(turn_drained, 1)

            a.wait_ge(setup_vec, 4)
            feature_exp(Body(-2, False))
            inverse_std(0, 0)
            feature_exp(Body(-1, True))
            inverse_std(1, 0)
            a.wait_ge(loaded_small, 16 * SMALL)
            evacuate_normed(Body(-1, True))
            for k in range(4):
                bias_qk(Body(-1, True), k)
            inverse_std(0, 1)
            inverse_std(1, 1)
            key_ones(1, range(HEADS))

            def place_max(body, g, name):
                p, gg = (body.p, g - 1) if g else (1 - body.p, GROUPS - 1)
                a.wait_ge(turn_filled, body.after(name))
                a.activation(query_pack[p][96:P, gg, :], turn_bank[96:P, 0:SEQ], ACT.Copy).then_inc(turn_drained, 1)

            def evacuate_values(body, g, before_name):
                group = body.i * GROUPS + g - 2
                a.wait_ge(pv_filled, group + 1)
                if before_name:
                    a.wait_ge(turn_filled, body.after(before_name))
                a.activation(mixed_v[:], pv_bank[:, 0:SEQ], ACT.Copy).then_inc(pv_evacuated, 1)

            def exponential(body, g, j):
                group = body.i * GROUPS + g - 1
                a.wait_ge(keyed_filled, group * GH + j + 1)
                if j == 0:
                    at_least(a, pv_filled, group - 1)
                a.activation(probs[:, GH * ((g + 1) % 2) + j, :, :], exp_bank[j % 2][:, :], ACT.Exp,
                             scale=SCALE).then_inc(exp_done, 1)

            def evacuate_context(body):
                a.wait_ge(b_filled, body.after("context"))
                a.activation(context_t[:], front_b[:, 0:SEQ], ACT.Copy).then_inc(b_drained, 1)

            def exponents_of_gates(body):
                a.wait_ge(below_done, body.i - 1)
                a.activation(gate_exp[:], below_top[:], ACT.Exp).then_inc(gate_exp_done, 1)

            def emit(body):
                if isinstance(body.i, int) and body.i == 1:
                    a.dma_start(w1_sb[:], w1.rearrange("e d h -> d e h")).then_inc(loaded_moe, 16)
                    a.dma_start(w2_sb[:], w2.rearrange("e (c p) d -> p e c d", p=P)).then_inc(loaded_moe, 16)
                    a.dma_start(b2_sb[:], b2.rearrange("(o e) d -> o e d", o=1).broadcast_to([P, EXPERTS, D])).then_inc(loaded_moe, 16)
                if isinstance(body.i, int) and body.i == BATCHES - 2:
                    a.wait_ge(b_filled, Body(BATCHES - 3, True).after("arg"))
                    a.dma_start(b1_sb, b1.rearrange("(o e) h -> o e h", o=1).broadcast_to([P, EXPERTS, HID])).then_inc(loaded_moe, 16)
                for g in range(GROUPS):
                    has_m = (g > 0 and body.core) or (g == 0 and body.prev)
                    has_u = (g >= 2 and body.core) or (g < 2 and body.prev)
                    if g == 1 and body.project:
                        bias_qk(body, 0)
                    if g == 2 and body.gate:
                        exponents_of_gates(body)
                    if has_m:
                        place_max(body, g, ("m3", "m0", "m1", "m2")[g])
                    if g == 1 and body.project:
                        bias_qk(body, 1)
                    if has_u:
                        evacuate_values(body, g, ("m3", "u2", "u3" if body.prev else None, "u0")[g])
                    if g == 1 and body.project:
                        bias_qk(body, 2)
                    if g == 3 and body.front:
                        inverse_std(1, body.i + 2)
                    if has_m:
                        exponential(body, g, 0)
                    if g == 3 and body.prev:
                        inverse_std(2, body.i - 1)
                    if has_m:
                        exponential(body, g, 1)
                    if g == 0:
                        if body.gate:
                            evacuate_tokens(body)
                        if body.project:
                            evacuate_normed(body)
                    if g == 1 and body.project:
                        bias_qk(body, 3)
                    if g == 2 and body.prev:
                        evacuate_context(body)
                    if has_m:
                        exponential(body, g, 2)
                    if g == 0 and body.front:
                        feature_exp(body)
                    if g == 2 and body.front:
                        inverse_std(0, body.i + 2)
                    if has_m:
                        exponential(body, g, 3)

            run_bodies(a, emit)
            pad_experts(a, range(1, EXPERTS, 2), ends_known, pads_placed, sorted_dram, end_row_i, pad_rows)

            def tile_act(n, p):
                a.wait_ge(up_drained, n + 1)
                at_least(a, act_turned, n - 1)
                a.activation(act[p][:], up[p][:], ACT.Gelu_apprx_tanh).then_inc(act_done, 1)

            def tile_act_t(n, p):
                a.wait_ge(act_turned, n + 1)
                at_least(a, down_filled, n - 1)
                a.activation(act_t[p], act_t_bank[p][:, :], ACT.Copy).then_inc(act_t_done, 1)

            tile_act(0, 0)
            tile_act(1, 1)
            tile_act_t(0, 0)
            tile_act(2, 0)
            tile_act_t(1, 1)
            with a.Fori(1, (MOE_TILES - 1) // 2) as pair:
                tile_act(pair * 2 + 1, 1)
                tile_act_t(pair * 2, 0)
                tile_act(pair * 2 + 2, 0)
                tile_act_t(pair * 2 + 1, 1)
            tile_act_t(MOE_TILES - 1, 0)

            a.preload_act_table_set("natural_log_exp_and_others")

            def last_norm(c):
                a.wait_ge(last_shift, c + 1)
                for t in range(CT):
                    last = a.activation(first_all[:, c * CT + t, :], base_all[:, c * CT + t, :], ACT.Identity,
                                        bias=chunk_shift[:, c % 2, t:t + 1], scale=chunk_rstd[:, c % 2, t:t + 1])
                last.then_inc(last_done, 1)

            for c in range(CHUNKS):
                a.wait_ge(last_aggr, c + 1)
                a.activation(chunk_log[:, c % 2, :], chunk_mean_var[:, c % 2, :, 1], ACT.Ln, bias=eps_col[:, 0:1]).then_inc(last_log, 1)
                a.wait_ge(last_log, c + 1)
                a.activation(chunk_rstd[:, c % 2, :], chunk_log[:, c % 2, :], ACT.Exp, scale=-0.5).then_inc(last_rstd, 1)
                if c:
                    last_norm(c - 1)
            last_norm(CHUNKS - 1)

        @block.vector
        def _(v):
            v.memset(zeros[:], 0.0).then_inc(setup_vec, 1)
            v.memset(eps_col[:], EPS).then_inc(setup_vec, 1)
            v.memset(ones_bf[:], 1.0).then_inc(setup_vec, 1)
            v.memset(max_parts[:], 0.0)
            v.wait_ge(loaded_features, 48)
            v.tensor_scalar(feat_bias[:], xis_col[:], -0.5 * math.log(D), None, ALU.add).then_inc(setup_vec, 1)
            v.tensor_tensor(neg_half_sq[:], xis_col[:], xis_col[:], ALU.mult).then_inc(setup_vec, 1)
            v.wait_ge(setup_vec, 5)
            v.tensor_scalar(scaled_rd[:, 0, :], proj_rd[:], xis_col[:, 0:1], None, ALU.mult).then_inc(setup_scaled, 1)
            v.tensor_scalar(scaled_rd[:, 1, :], zeros[:, 0:D], neg_half_sq[:, 0:1], -0.5, ALU.add, ALU.mult).then_inc(setup_scaled, 1)
            v.wait_ge(setup_transposed, 1)
            v.tensor_copy(scaled_dr[:], score_bank[0][:, 0:2 * D].rearrange("p (n d) -> p n d", n=2)).then_inc(setup_evacuated, 1)
            for p in range(2):
                v.memset(v_ext[p][:], 0.0).then_inc(values_zeroed, 1)
            v.wait_ge(values_zeroed, 2)
            for p in range(2):
                v.memset(v_ext[p][:, :, :, DH:DH + 1], 1.0)
            v.wait_ge(pool_consts, 5)
            for h in range(HEADS // 2, HEADS):
                last = v.tensor_scalar(key_pack[0][96:P, h, :], zeros[96:P, :], head_rows[96:P, h % GH:h % GH + 1], None, ALU.add)
            last.then_inc(keys_ones[0], 1)
            def moments(n, b, source):
                for t in range(TB):
                    last = v.bn_stats(stats[:, n, t, :], source[t])
                last.then_inc(stats_done[n], 1)

            def aggregate(n, b):
                apart(v, setup_vec, (stats_done[n], b + 1))
                for t in range(TB):
                    last = v.bn_aggr(mean_var[:, n, t, :], stats[:, n, t, :])
                last.then_inc(aggregated[n], 1)

            def normalise(n, t, dst, src):
                return v.tensor_scalar(dst, src, mean_var[:, n, t, 0:1], rstd[:, n, t:t + 1], ALU.subtract, ALU.mult)

            def add_mixed(body):
                b = body.i + 2
                v.wait_ge(a_filled, body.after("mixed"))
                v.tensor_tensor(mixed[:], front_a[:, 0:SEQ].rearrange("p (t d) -> p t d", t=TB),
                                x1_all[:, bass.ds(b * TB, TB), :], ALU.add).then_inc(a_drained, 1)

            def moments_mixed(body):
                b = body.i + 2
                apart(v, setup_vec, (a_drained, body.after("mixed")))
                moments(0, b, [mixed[:, t, :] for t in range(TB)])

            def first_norm(b):
                v.wait_ge(rstd_done[0], b + 1)
                for t in range(TB):
                    last = normalise(0, t, x1_all[:, bass.ds(b * TB + t, 1), :], mixed[:, t:t + 1, :])
                last.then_inc(x1_done, 1)

            def moments_x1(b):
                apart(v, setup_vec, (x1_done, b + 1))
                moments(1, b, [x1_all[:, bass.ds(b * TB + t, 1), :] for t in range(TB)])

            def second_norm(body):
                b = body.i + 2
                v.wait_ge(rstd_done[1], b + 1)
                at_least(v, a_filled, body.after("normed"))
                for t in range(TB):
                    last = normalise(1, t, normed[:, t:t + 1, :], x1_all[:, bass.ds(b * TB + t, 1), :])
                last.then_inc(normed_done, 1)

            def evacuate_v(body):
                p = 1 - body.p
                v.wait_ge(a_filled, body.after("v"))
                at_least(v, pv_filled, body.i * GROUPS)
                v.tensor_tensor(v_ext[p][:, :, :, 0:DH], front_a[:, 0:SEQ].rearrange("p (t h e) -> p t h e", t=TB, h=HEADS),
                                bv_row[:].rearrange("p (o h e) -> p o h e", o=1, h=HEADS).broadcast_to([P, TB, HEADS, DH]),
                                ALU.add).then_inc(a_drained, 1)

            def front_start(body):
                b = body.i + 2
                add_mixed(body)
                moments_mixed(body)
                aggregate(0, b)
                first_norm(b)
                moments_x1(b)
                aggregate(1, b)
                second_norm(body)

            v.wait_ge(loaded_x0, 32)
            front_start(Body(-2, False))
            front_start(Body(-1, True))
            v.wait_ge(loaded_small, 16 * SMALL)
            evacuate_v(Body(-1, True))
            v.wait_ge(loaded_x1, 32)

            def reduce_scores(body, g, u):
                group = body.i * GROUPS + g
                qt, pair = u // 2, u % 2
                v.wait_ge(scores_filled, group * 4 + u + 1)
                v.reduce_max(row_max[g % 2][:, qt, 2 * pair:2 * pair + 2], score_bank[u % 2][:, :].rearrange("p (h k) -> p h k", h=2),
                             AX.X).then_inc(scores_drained, 1)

            def parts_of_max():
                return max_parts[:, :, 96:96 + 2 * GH].rearrange("p t (j s) -> p t j s", s=2)

            def high_of_max(body, g, before_name):
                v.wait_ge(scores_drained, (body.i * GROUPS + g) * 4 + 4)
                if before_name:
                    v.wait_ge(turn_filled, body.after(before_name))
                v.tensor_scalar(parts_of_max()[:, :, :, 0].bitcast(F32R), row_max[g % 2][:], -1.0, None, ALU.mult).then_inc(max_hi, 1)

            def low_of_max(body, g):
                parts = parts_of_max()
                v.wait_ge(max_hi, body.i * GROUPS + g + 1)
                v.scalar_tensor_tensor(parts[:, :, :, 1].bitcast(F32R), row_max[g % 2][:], -1.0, parts[:, :, :, 0],
                                       ALU.mult, ALU.subtract).then_inc(max_lo, 1)

            def normalise_values(body, g, u_name):
                heads = turn_bank[:, 0:SEQ].rearrange("p (t j e) -> p t j e", t=TB, j=GH)
                gg = (g + 2) % GROUPS
                ctx_v = context[:, :, gg * GH * DH:(gg + 1) * GH * DH].rearrange("p t (j e) -> p t j e", j=GH)
                v.wait_ge(turn_filled, body.after(u_name))
                v.reciprocal(inv_sum[:], heads[:, :, :, DH]).then_inc(inverted, 1)
                v.wait_ge(inverted, body.i * GROUPS + g - 1)
                v.tensor_tensor(ctx_v, heads[:, :, :, 0:DH], inv_sum[:].unsqueeze(3).broadcast_to([P, TB, GH, DH]),
                                ALU.mult).then_inc(turn_drained, 1)

            def add_attention(body):
                b = body.i - 1
                v.wait_ge(a_filled, body.after("out"))
                v.wait_ge(x1_bo_done, b + 1)
                at_least(v, base_done, b)
                v.tensor_tensor(hidden[:], front_a[:, 0:SEQ].rearrange("p (t d) -> p t d", t=TB), x1_bo[:], ALU.add).then_inc(a_drained, 1)

            def moments_hidden(body):
                apart(v, setup_vec, (a_drained, body.after("out")))
                moments(2, body.i - 1, [hidden[:, t, :] for t in range(TB)])

            def third_norm(body):
                b = body.i - 1
                apart(v, setup_vec, (rstd_done[2], b + 1),
                      (scattered, (b - 1) * (16 * TB * TOPK)))
                for t in range(TB):
                    last = v.tensor_scalar(rows[1 - body.p][:, t, 0, 0:D], hidden[:, t, :],
                                              mean_var[:, 2, t, 0:1], rstd[:, 2, t:t + 1], ALU.subtract, ALU.mult)
                last.then_inc(token_row, 1)

            def copy_logits(body):
                v.wait_ge(a_filled, body.after("logits"))
                v.tensor_copy(logits[:], front_a[:, 0:TB * EXPERTS].rearrange("p (t e) -> p t e", t=TB)).then_inc(a_drained, 1)

            def best(body):
                apart(v, setup_vec, (a_drained, body.after("logits")))
                for t in range(TB):
                    last = v.max(top8[:, t, :], logits[:, t, :])
                last.then_inc(top_done, 1)

            def best_at(body):
                apart(v, setup_vec, (top_done, body.i - 1))
                for t in range(TB):
                    last = v.max_index(top8_at[:, t, :], top8[:, t, :], logits[:, t, :])
                last.then_inc(top_at_done, 1)
                v.tensor_tensor(below_top[:], top8[:, :, 0:TOPK], top8[:, :, 0:1].broadcast_to([P, TB, TOPK]), ALU.subtract).then_inc(below_done, 1)

            def best_numbers(body):
                v.wait_ge(top_at_done, body.i - 1)
                v.tensor_copy(top_at[:], top8_at[:, :, 0:TOPK]).then_inc(top_at_f, 1)

            def choose(body):
                v.wait_ge(top_at_f, body.i - 1)
                v.tensor_tensor(chosen[:], expert_no[:].rearrange("p (a c e) -> p a c e", a=1, c=1).broadcast_to([P, TB, TOPK, EXPERTS]),
                                top_at[:].unsqueeze(3).broadcast_to([P, TB, TOPK, EXPERTS]), ALU.is_equal).then_inc(chosen_done, 1)

            def mark_used(body):
                v.wait_ge(chosen_done, body.i - 1)
                v.tensor_tensor(used[:], chosen[:, :, 0, :], chosen[:, :, 1, :], ALU.add).then_inc(used_done, 1)

            def gate_total(body):
                v.wait_ge(gate_exp_done, body.i - 1)
                v.reduce_sum(gate_sum[:], gate_exp[:], AX.X).then_inc(gate_sum_done, 1)

            def gate_inverse(body):
                v.wait_ge(gate_sum_done, body.i - 1)
                v.reciprocal(gate_inv[:], gate_sum[:]).then_inc(gate_inv_done, 1)

            def gates(body):
                v.wait_ge(gate_inv_done, body.i - 1)
                v.tensor_tensor(rows[body.p][:, :, :, D], gate_exp[:], gate_inv[:].unsqueeze(2).broadcast_to([P, TB, TOPK]), ALU.mult).then_inc(gate_done, 1)

            def slots(body):
                ranks = front_b[:, 0:TB * EXPERTS].rearrange("p (t e) -> p t e", t=TB)
                v.wait_ge(b_filled, body.after("rank"))
                v.tensor_tensor(slot[:], ranks, next_row[:].unsqueeze(1).broadcast_to([P, TB, EXPERTS]), ALU.add).then_inc(slot_done, 1)

            def advance(body):
                v.wait_ge(slot_done, body.i - 1)
                v.tensor_tensor(next_row[:], front_b[:, TB * EXPERTS:(TB + 1) * EXPERTS], next_row[:], ALU.add).then_inc(b_drained, 1)
                v.tensor_tensor(slot_of[:], chosen[:], slot[:].unsqueeze(2).broadcast_to([P, TB, TOPK, EXPERTS]), ALU.mult).then_inc(slot_of_done, 1)

            def place_rows(body):
                v.wait_ge(slot_of_done, body.i - 1)
                v.reduce_sum(place[:], slot_of[:].rearrange("p t s e -> p (t s) e"), AX.X).then_inc(place_done, 1)

            def whole_places(body):
                v.wait_ge(place_done, body.i - 1)
                at_least(v, scattered, (body.i - 2) * (16 * TB * TOPK))
                v.tensor_copy(place_i[:], place[:]).then_inc(placed, 1)

            def emit(body):
                i = body.i
                if isinstance(i, int) and i == 2:
                    v.wait_ge(loaded_x, 32)
                for g in range(GROUPS):
                    has_u = (g >= 2 and body.core) or (g < 2 and body.prev)
                    before_name = ("m3" if body.prev else None, "m0", "m1", "m2")[g]
                    u_name = ("u2", "u3", "u0", "u1")[g]
                    if body.core:
                        reduce_scores(body, g, 0)
                    if g == 1 and body.gate:
                        copy_logits(body)
                    if g == 2:
                        if body.front:
                            aggregate(0, i + 2)
                        if body.gate:
                            slots(body)
                    if g == 3:
                        if body.front:
                            aggregate(1, i + 2)
                        if body.prev:
                            aggregate(2, i - 1)
                    if body.core:
                        reduce_scores(body, g, 1)
                    if g == 1:
                        if body.gate:
                            best(body)
                            best_at(body)
                    if g == 2:
                        if body.gate:
                            advance(body)
                        if body.project:
                            evacuate_v(body)
                    if body.core:
                        reduce_scores(body, g, 2)
                    if g == 2:
                        if body.gate:
                            place_rows(body)
                            gate_total(body)
                    if body.core:
                        reduce_scores(body, g, 3)
                    if g == 1 and body.gate:
                        best_numbers(body)
                    if g == 2 and body.gate:
                        whole_places(body)
                    if body.core:
                        high_of_max(body, g, before_name)
                    if g == 1:
                        if body.gate:
                            choose(body)
                        if body.front:
                            add_mixed(body)
                    if g == 2 and body.gate:
                        gate_inverse(body)
                    if body.core:
                        low_of_max(body, g)
                    if g == 1 and body.gate:
                        mark_used(body)
                    if g == 2 and body.gate:
                        gates(body)
                    if has_u:
                        normalise_values(body, g, u_name)
                    if g == 1 and body.front:
                        moments_mixed(body)
                    if g == 2:
                        if body.front:
                            first_norm(i + 2)
                        if body.prev:
                            add_attention(body)
                        if body.front:
                            moments_x1(i + 2)
                        if body.prev:
                            moments_hidden(body)
                    if g == 3 and body.front:
                        second_norm(body)
                    if g == 3 and body.prev and not body.core:
                        third_norm(body)

            run_bodies(v, emit)

            steps = [0]

            def link(instruction):
                steps[0] += 1
                instruction.then_inc(table, 1)
                v.wait_ge(table, steps[0])

            v.wait_ge(b_drained, Body(BATCHES + 1, True).after("rank"))
            v.tensor_copy(end_row_i[:], next_row[:]).then_inc(ends_known, 1)
            link(v.scalar_tensor_tensor(counts_f[:], expert_no[:], -float(REGION), next_row[:], ALU.mult, ALU.add))
            link(v.tensor_scalar(counts_i[:], counts_f[:], float(P - 1), None, ALU.add))
            link(v.tensor_scalar(tiles_i[:], counts_i[:], int(math.log2(P)), None, ALU.arith_shift_right))
            link(v.tensor_copy(tiles_f[:], tiles_i[:]))
            link(v.tensor_tensor(tiles_upto[:], upto[:], tiles_f[:].unsqueeze(1).broadcast_to([P, EXPERTS, EXPERTS]), ALU.mult))
            link(v.reduce_sum(tile_end[:], tiles_upto[:], AX.X))
            link(v.tensor_scalar(gap[:], tiles_f[:], -float(P), float(REGION), ALU.mult, ALU.add))
            link(v.tensor_tensor(past[:], tile_no[:].unsqueeze(2).broadcast_to([P, MOE_TILES, EXPERTS]),
                                 tile_end[:].unsqueeze(1).broadcast_to([P, MOE_TILES, EXPERTS]), ALU.is_ge))
            link(v.reduce_sum(tile_expert[:], past[:], AX.X))
            link(v.tensor_tensor(past_gap[:], past[:], gap[:].unsqueeze(1).broadcast_to([P, MOE_TILES, EXPERTS]), ALU.mult))
            link(v.reduce_sum(tile_shift[:], past_gap[:], AX.X))
            link(v.scalar_tensor_tensor(tile_row[:], tile_no[:], float(P), tile_shift[:], ALU.mult, ALU.add))
            link(v.tensor_scalar(expert_i[:], tile_expert[:], float(EXPERTS - 1), None, ALU.min))
            link(v.tensor_scalar(expert_col[:], tile_expert[:], float(EXPERTS - 1), float(HID), ALU.min, ALU.mult))
            v.tensor_copy(row_i[:], tile_row[:]).then_inc(table_ready, 1)
            v.wait_ge(table_ready, 1)
            v.wait_ge(loaded_moe, 16 * 4)

            def evacuate_got(n, p):
                v.wait_ge(got_turned, n + 1)
                at_least(v, up_filled, n - 1)
                v.tensor_scalar(got_t[p][:], got_bank[:, 0:P], ln_cols[:, 2:3], ln_cols[:, 3:4], ALU.mult, ALU.add).then_inc(got_t_done, 1)

            def bias_up(n, p):
                e = v.value_load(expert_i[0:1, bass.ds(n, 1)], min_val=0, max_val=EXPERTS - 1)
                v.wait_ge(up_filled, n + 1)
                at_least(v, act_done, n - 1)
                v.tensor_tensor(up[p][:].unsqueeze(1), up_bank[p][:, :].unsqueeze(1), b1_sb[:, bass.ds(e, 1), :], ALU.add).then_inc(up_drained, 1)

            def gate_down(n, q, r):
                p = q % 2
                e = v.value_load(expert_i[0:1, bass.ds(n, 1)], min_val=0, max_val=EXPERTS - 1)
                v.wait_ge(down_filled, n + 1)
                v.tensor_tensor(down[p][:].unsqueeze(1), down_bank[p][:, 0:D].unsqueeze(1), b2_sb[:, bass.ds(e, 1), :], ALU.add).then_inc(down_drained, 1)
                v.wait_ge(down_drained, n + 1)
                at_least(v, result_stored[q % PUT], 16 * uses(r, q, PUT))
                v.tensor_scalar(gated[q % PUT], down[p][:], got[q % GOT][:, D:D + 1], None, ALU.mult).then_inc(gated_done, 1)

            def slot_of_v(n, q, r):
                fixed = isinstance(n, int)
                if not fixed or n + 1 < MOE_TILES:
                    evacuate_got(n + 1, (q + 1) % 2)
                if not fixed or n >= 3:
                    gate_down(n - 3, q - 3, r)
                if not fixed or n < MOE_TILES:
                    bias_up(n, q % 2)

            evacuate_got(0, 0)
            run_tiles(v, slot_of_v, MOE_TILES + 3)

            def last_sum(c):
                tiles = slice(c * CT, (c + 1) * CT)
                v.wait_ge(results_back[c], 32)
                v.wait_ge(add1, c + 1)
                v.tensor_tensor(base_all[:, tiles, :], base_all[:, tiles, :], second_all[:, tiles, :], ALU.add).then_inc(add2, 1)

            def last_moments(c):
                v.wait_ge(add2, c + 1)
                for t in range(CT):
                    last = v.bn_stats(chunk_stats[:, c % 2, t, :], base_all[:, c * CT + t, :])
                last.then_inc(last_stats, 1)
                v.wait_ge(last_stats, c + 1)
                for t in range(CT):
                    last = v.bn_aggr(chunk_mean_var[:, c % 2, t, :], chunk_stats[:, c % 2, t, :])
                last.then_inc(last_aggr, 1)

            def last_shifts(c):
                v.wait_ge(last_rstd, c + 1)
                v.scalar_tensor_tensor(chunk_shift[:, c % 2, :], chunk_mean_var[:, c % 2, :, 0], -1.0,
                                       chunk_rstd[:, c % 2, :], ALU.mult, ALU.mult).then_inc(last_shift, 1)

            last_sum(0)
            last_moments(0)
            for c in range(1, CHUNKS):
                last_sum(c)
                last_shifts(c - 1)
                last_moments(c)
            last_shifts(CHUNKS - 1)


def kernel(L0_attn_x, L0_attn_input_weights, L0_attn_xis, L0_attn_proj_matrix, L0_ffn_ln1_w, L0_ffn_ln1_b,
           L0_ffn_ln2_w, L0_ffn_ln2_b, L0_ffn_w_qkv, L0_ffn_b_qkv, L0_ffn_w_o, L0_ffn_b_o, L0_ffn_w_gate,
           L0_ffn_w1, L0_ffn_b1, L0_ffn_w2, L0_ffn_b2):
    import numpy as np
    import concourse.bacc as bacc
    from concourse.bass_utils import run_bass_kernel_spmd

    x = np.asarray(L0_attn_x).reshape(TOKENS, D)
    given = {
        "x": x, "x_t": x.T, "w_in_t": np.asarray(L0_attn_input_weights).T, "xis": L0_attn_xis,
        "proj": L0_attn_proj_matrix, "ln1_w": L0_ffn_ln1_w, "ln1_b": L0_ffn_ln1_b, "ln2_w": L0_ffn_ln2_w,
        "ln2_b": L0_ffn_ln2_b, "w_qkv": L0_ffn_w_qkv, "b_qkv": L0_ffn_b_qkv, "w_o": L0_ffn_w_o,
        "b_o": L0_ffn_b_o, "w_gate": L0_ffn_w_gate, "w1": L0_ffn_w1, "b1": L0_ffn_b1, "w2": L0_ffn_w2,
        "b2": L0_ffn_b2,
    }
    nc = bacc.Bacc("TRN2", target_bir_lowering=False, num_devices=1)
    arrays, args = {}, {}
    for name, a in given.items():
        a = np.ascontiguousarray(a)
        arrays[f"{name}_dram"] = a
        args[name] = nc.dram_tensor(f"{name}_dram", a.shape, mybir.dt.from_np(a.dtype), kind="ExternalInput").ap()
    out = nc.dram_tensor("out_dram", (TOKENS, D), F32, kind="ExternalOutput").ap()
    build(nc, **args, out=out)
    r = run_bass_kernel_spmd(nc, [arrays], core_ids=[0])
    return r.results[0]["out_dram"].reshape(BATCHES, SEQ, D)
```
